# Optimizing a Trainium2 kernel written in Bass

```python
import numpy as np
import jax
import jax.numpy as jnp

def _softmax(x, axis=-1):
    return jax.nn.softmax(x, axis=axis)

def _gelu(x):
    return jax.nn.gelu(x, approximate=True)

def _silu(x):
    return jax.nn.silu(x)

def _sigmoid(x):
    return jax.nn.sigmoid(x)

def _layernorm(x, axis=-1, eps=1e-05):
    m = jnp.mean(x, axis=axis, keepdims=True)
    v = jnp.var(x, axis=axis, keepdims=True)
    return (x - m) / jnp.sqrt(v + eps)

def _scatter_add(tgt, idx, src, axis=0):
    return tgt.at[idx].add(src)

def _segment_sum(src, seg, n):
    return jax.ops.segment_sum(src, seg, n)
kernel_name = 'mk_gnn_ffn_d1_gnn_r64_74f551'

def setup_inputs(seed: int=0):
    np.random.seed(seed)
    _w = jnp.asarray

    def _rec_inputs():
        import jax
        import jax.numpy as jnp
        _gk = jax.random.key(seed)
        x = -0.0001126 + 1 * jax.random.normal(jax.random.fold_in(_gk, 1), (50000, 256), jnp.float32)
        src = jax.random.randint(jax.random.fold_in(_gk, 2), (12500,), 0, 50000, jnp.int32)
        dst = jnp.minimum((50000 * jax.random.uniform(jax.random.fold_in(_gk, 3), (12500,)) ** 2.0).astype(jnp.int32), 49999)
        _o = jnp.argsort(dst, stable=True)
        src = src[_o]
        dst = dst[_o]
        return (x, src, dst)
    x, src, dst = _rec_inputs()

    def _L0_gnn_setup():
        import jax, jax.numpy as jnp
        import numpy as np
        H, C = (4, 64)
        NEG_SLOPE = 0.2

        def _gatv2_layer(x, src, dst, n, Wl, Wr, att, b):
            xl = (x @ Wl).reshape(n, H, C)
            xr = (x @ Wr).reshape(n, H, C)
            e = jax.nn.leaky_relu(xl[src] + xr[dst], NEG_SLOPE)
            logits = jnp.einsum('ehc,hc->eh', e, att)
            m = jax.ops.segment_max(logits, dst, num_segments=n)
            ex = jnp.exp(logits - m[dst])
            denom = jax.ops.segment_sum(ex, dst, num_segments=n)
            alpha = ex / (denom[dst] + 1e-16)
            msg = xl[src] * alpha[:, :, None]
            out = jax.ops.segment_sum(msg, dst, num_segments=n)
            return out.reshape(n, H * C) + b
        key = jax.random.key(seed)
        ks = jax.random.split(key, 10)
        N, E, F = (30000, 7500, 256)
        x = jax.random.normal(ks[0], (N, F), dtype=jnp.float32)
        edge_index = jax.random.randint(ks[1], (2, E), 0, N, dtype=jnp.int64)
        s = 1.0 / np.sqrt(F)

        def w(k, shape):
            return jax.random.uniform(k, shape, jnp.float32, -s, s)
        return {'x': x, 'edge_index': edge_index, 'Wl1': w(ks[2], (F, H * C)), 'Wr1': w(ks[3], (F, H * C)), 'att1': w(ks[4], (H, C)), 'b1': jnp.zeros((H * C,), jnp.float32), 'Wl2': w(ks[5], (F, H * C)), 'Wr2': w(ks[6], (F, H * C)), 'att2': w(ks[7], (H, C)), 'b2': jnp.zeros((H * C,), jnp.float32)}
    _L0_gnn_all = _L0_gnn_setup()
    _L0_gnn_in = {k: v for k, v in _L0_gnn_all.items() if k in ('Wl1', 'Wr1', 'att1', 'b1', 'Wl2', 'Wr2', 'att2', 'b2')}
    del _L0_gnn_all

    def _L0_ffn_setup():
        import jax, jax.numpy as jnp
        import numpy as np
        B, A = (64, 8)
        IN, OUT = (256, 256)
        SH1, SH2 = (256, 128)
        EH1, EH2 = (128, 64)
        E, TOPK = (4, 2)

        def _shared_mlp(x, W1, b1, W2, b2, W3, b3):
            h = jax.nn.relu(x @ W1 + b1)
            h = jax.nn.relu(h @ W2 + b2)
            return h @ W3 + b3

        def _experts_mlp(x, eW1, eb1, eW2, eb2, eW3, eb3):
            h = jax.nn.relu(jnp.einsum('baf,efh->ebah', x, eW1) + eb1[:, None, None, :])
            h = jax.nn.relu(jnp.einsum('ebah,ehg->ebag', h, eW2) + eb2[:, None, None, :])
            o = jnp.einsum('ebag,ego->ebao', h, eW3) + eb3[:, None, None, :]
            return jnp.moveaxis(o, 0, -1)
        key = jax.random.key(seed)
        ks = jax.random.split(key, 16)
        s = 0.05
        return {'x': jax.random.normal(ks[0], (B, A, IN), jnp.float32), 'sW1': jax.random.normal(ks[1], (IN, SH1), jnp.float32) * s, 'sb1': jnp.zeros((SH1,), jnp.float32), 'sW2': jax.random.normal(ks[2], (SH1, SH2), jnp.float32) * s, 'sb2': jnp.zeros((SH2,), jnp.float32), 'sW3': jax.random.normal(ks[3], (SH2, OUT), jnp.float32) * s, 'sb3': jnp.zeros((OUT,), jnp.float32), 'eW1': jax.random.normal(ks[4], (E, IN, EH1), jnp.float32) * s, 'eb1': jnp.zeros((E, EH1), jnp.float32), 'eW2': jax.random.normal(ks[5], (E, EH1, EH2), jnp.float32) * s, 'eb2': jnp.zeros((E, EH2), jnp.float32), 'eW3': jax.random.normal(ks[6], (E, EH2, OUT), jnp.float32) * s, 'eb3': jnp.zeros((E, OUT), jnp.float32), 'gW': jax.random.normal(ks[7], (IN, E), jnp.float32) * s, 'gb': jnp.zeros((E,), jnp.float32)}
    _L0_ffn_all = _L0_ffn_setup()
    _L0_ffn_in = {k: v for k, v in _L0_ffn_all.items() if k in ('sW1', 'sb1', 'sW2', 'sb2', 'sW3', 'sb3', 'eW1', 'eb1', 'eW2', 'eb2', 'eW3', 'eb3', 'gW', 'gb')}
    del _L0_ffn_all
    return {'x': x, 'src': src, 'dst': dst, 'L0_gnn_Wl1': _L0_gnn_in['Wl1'], 'L0_gnn_Wr1': _L0_gnn_in['Wr1'], 'L0_gnn_att1': _L0_gnn_in['att1'], 'L0_gnn_b1': _L0_gnn_in['b1'], 'L0_gnn_Wl2': _L0_gnn_in['Wl2'], 'L0_gnn_Wr2': _L0_gnn_in['Wr2'], 'L0_gnn_att2': _L0_gnn_in['att2'], 'L0_gnn_b2': _L0_gnn_in['b2'], 'L0_ffn_sW1': _L0_ffn_in['sW1'], 'L0_ffn_sb1': _L0_ffn_in['sb1'], 'L0_ffn_sW2': _L0_ffn_in['sW2'], 'L0_ffn_sb2': _L0_ffn_in['sb2'], 'L0_ffn_sW3': _L0_ffn_in['sW3'], 'L0_ffn_sb3': _L0_ffn_in['sb3'], 'L0_ffn_eW1': _L0_ffn_in['eW1'], 'L0_ffn_eb1': _L0_ffn_in['eb1'], 'L0_ffn_eW2': _L0_ffn_in['eW2'], 'L0_ffn_eb2': _L0_ffn_in['eb2'], 'L0_ffn_eW3': _L0_ffn_in['eW3'], 'L0_ffn_eb3': _L0_ffn_in['eb3'], 'L0_ffn_gW': _L0_ffn_in['gW'], 'L0_ffn_gb': _L0_ffn_in['gb']}

def reference(x, src, dst, L0_gnn_Wl1, L0_gnn_Wr1, L0_gnn_att1, L0_gnn_b1, L0_gnn_Wl2, L0_gnn_Wr2, L0_gnn_att2, L0_gnn_b2, L0_ffn_sW1, L0_ffn_sb1, L0_ffn_sW2, L0_ffn_sb2, L0_ffn_sW3, L0_ffn_sb3, L0_ffn_eW1, L0_ffn_eb1, L0_ffn_eW2, L0_ffn_eb2, L0_ffn_eW3, L0_ffn_eb3, L0_ffn_gW, L0_ffn_gb):
    import jax
    import jax.numpy as jnp

    def _L0_gnn_ref(x, edge_index, Wl1, Wr1, att1, b1, Wl2, Wr2, att2, b2):
        import jax, jax.numpy as jnp
        import numpy as np
        H, C = (4, 64)
        NEG_SLOPE = 0.2

        def _gatv2_layer(x, src, dst, n, Wl, Wr, att, b):
            xl = (x @ Wl).reshape(n, H, C)
            xr = (x @ Wr).reshape(n, H, C)
            e = jax.nn.leaky_relu(xl[src] + xr[dst], NEG_SLOPE)
            logits = jnp.einsum('ehc,hc->eh', e, att)
            m = jax.ops.segment_max(logits, dst, num_segments=n)
            ex = jnp.exp(logits - m[dst])
            denom = jax.ops.segment_sum(ex, dst, num_segments=n)
            alpha = ex / (denom[dst] + 1e-16)
            msg = xl[src] * alpha[:, :, None]
            out = jax.ops.segment_sum(msg, dst, num_segments=n)
            return out.reshape(n, H * C) + b
        n = x.shape[0]
        loops = jnp.arange(n, dtype=edge_index.dtype)
        src = jnp.concatenate([edge_index[0], loops])
        dst = jnp.concatenate([edge_index[1], loops])
        h = _gatv2_layer(x, src, dst, n, Wl1, Wr1, att1, b1)
        h = jax.nn.elu(h)
        h = _gatv2_layer(h, src, dst, n, Wl2, Wr2, att2, b2)
        return h

    def _L0_ffn_ref(x, sW1, sb1, sW2, sb2, sW3, sb3, eW1, eb1, eW2, eb2, eW3, eb3, gW, gb):
        import jax, jax.numpy as jnp
        import numpy as np
        B, A = (64, 8)
        IN, OUT = (256, 256)
        SH1, SH2 = (256, 128)
        EH1, EH2 = (128, 64)
        E, TOPK = (4, 2)

        def _shared_mlp(x, W1, b1, W2, b2, W3, b3):
            h = jax.nn.relu(x @ W1 + b1)
            h = jax.nn.relu(h @ W2 + b2)
            return h @ W3 + b3

        def _experts_mlp(x, eW1, eb1, eW2, eb2, eW3, eb3):
            h = jax.nn.relu(jnp.einsum('baf,efh->ebah', x, eW1) + eb1[:, None, None, :])
            h = jax.nn.relu(jnp.einsum('ebah,ehg->ebag', h, eW2) + eb2[:, None, None, :])
            o = jnp.einsum('ebag,ego->ebao', h, eW3) + eb3[:, None, None, :]
            return jnp.moveaxis(o, 0, -1)
        all_out = _experts_mlp(x, eW1, eb1, eW2, eb2, eW3, eb3)
        shared = _shared_mlp(x, sW1, sb1, sW2, sb2, sW3, sb3)
        gates = jax.nn.softmax(x @ gW + gb, axis=-1)
        topv, topi = jax.lax.top_k(gates, TOPK)
        topw = jax.nn.softmax(topv, axis=-1)
        sel = jnp.take_along_axis(all_out, topi[:, :, None, :], axis=-1)
        gated = jnp.sum(sel * topw[:, :, None, :], axis=-1)
        return shared + gated
    edge_index = jnp.stack([src, dst])
    x = x + _L0_gnn_ref(_layernorm(x, axis=-1), edge_index, L0_gnn_Wl1, L0_gnn_Wr1, L0_gnn_att1, L0_gnn_b1, L0_gnn_Wl2, L0_gnn_Wr2, L0_gnn_att2, L0_gnn_b2)
    x = x + _L0_ffn_ref(_layernorm(x, axis=-1)[None], L0_ffn_sW1, L0_ffn_sb1, L0_ffn_sW2, L0_ffn_sb2, L0_ffn_sW3, L0_ffn_sb3, L0_ffn_eW1, L0_ffn_eb1, L0_ffn_eW2, L0_ffn_eb2, L0_ffn_eW3, L0_ffn_eb3, L0_ffn_gW, L0_ffn_gb)[0]
    return x

_drawn_inputs = setup_inputs


def setup_inputs(seed=0):
    import zlib

    import numpy as np

    out = dict(_drawn_inputs(seed))
    spreads = {'L0_gnn_b1': (0.0, 0.1),
     'L0_gnn_b2': (0.0, 0.1),
     'L0_ffn_sb1': (0.0, 0.409),
     'L0_ffn_sb2': (0.0, 0.1),
     'L0_ffn_sb3': (0.0, 0.1),
     'L0_ffn_eb1': (0.0, 0.8),
     'L0_ffn_eb2': (0.0, 0.501),
     'L0_ffn_eb3': (0.0, 0.1),
     'L0_ffn_gb': (0.0, 0.366)}
    factors = {'L0_gnn_Wr1': 30.354, 'L0_gnn_att1': 8.0, 'L0_gnn_Wr2': 62.407, 'L0_gnn_att2': 34.666}
    for name, (base, spread) in spreads.items():
        noise = np.random.default_rng([zlib.crc32(name.encode()), seed]).standard_normal(out[name].shape)
        drawn = base * np.exp(spread * noise) if base else spread * noise
        out[name] = jnp.asarray(drawn.astype(out[name].dtype))
    for name, factor in factors.items():
        out[name] = (out[name] * factor).astype(out[name].dtype)
    return out
```

```python
from contextlib import ExitStack

import concourse.bass as bass
from concourse import mybir

F32 = mybir.dt.float32
I32 = mybir.dt.int32
ALU = mybir.AluOpType
ACT = mybir.ActivationFunctionType
AXX = mybir.AxisListType.X

P = 128
F = 256
KC = F // P
J = 4
G = P * J
H, C = 4, 64
SLOTS = 2
BIG = 1e30
LN_EPS = 1e-5
DEN_EPS = 1e-16
SLOPE = 0.2
NE = 4
TOPK = 2
EH1, EH2 = 128, 64
NC1 = 2 + NE


class Shared:

    def __init__(self, nodes, edges):
        self.nodes, self.edges = nodes, edges
        self.groups, self.tiles = -(-nodes // G), -(-edges // P)


def run(eng, pairs, steps):
    aheads = [ahead for _, ahead in steps]
    groups = 2 * pairs
    first = 1 - min(0, *aheads) // 2
    end = (groups - 1 - max(0, *aheads)) // 2

    def at(k, slot):
        for step, ahead in steps:
            step(k + (slot + ahead) // 2, (slot + ahead) % 2)

    def apart(g):
        for step, ahead in steps:
            if 0 <= g + ahead < groups:
                step((g + ahead) // 2, (g + ahead) % 2)

    for g in range(-max(aheads), 2 * first):
        apart(g)
    assert first < end
    with eng.Fori(first, end) as k:
        for slot in range(SLOTS):
            at(k, slot)
    for g in range(2 * end, groups - min(0, *aheads)):
        apart(g)


def done(g):
    return g + SLOTS


def start_counts(nc, semaphores, counts):
    with nc.Block() as block:
        @block.sync
        def _(sp):
            for semaphore in semaphores:
                sp.sem_clear(semaphore)
            for count in counts:
                sp.sem_inc(count, SLOTS - 1)


def wait_apart(eng, m, semaphore, value):
    eng.wait_ge(semaphore, value)
    eng.sem_inc(m.passed, 1)


def group_rows(n, g, groups):
    return n - G if isinstance(g, int) and g == groups - 1 else g * G


def nodes_of(dram, start):
    return dram[bass.ds(start, G), :].rearrange("(p j) f -> p j f", j=J)


def setup(nc, m, a, ctx):

    def sb(name, shape, dt=F32):
        return ctx.enter_context(nc.sbuf_tensor(name, shape, dt))

    nt = m.tiles
    m.ident = sb("ident", [P, P])
    m.minus_half = sb("minus_half", [P, 2 * J])
    m.ln_eps = sb("ln_eps", [P, 2 * J])
    m.last_row_ones = sb("last_row_ones", [P, P])
    m.w_gat = [sb(f"w_gat{i}", [P, KC, 2 * F]) for i in range(2)]
    m.att = [sb(f"att{i}", [P, F]) for i in range(2)]
    m.b_gat = [sb(f"b_gat{i}", [P, F]) for i in range(2)]
    m.w1 = sb("w1", [P, KC, NC1 * P])
    m.b1 = sb("b1", [P, NC1])
    m.sw2 = sb("sw2", [P, KC, P])
    m.ew2 = sb("ew2", [P, NE, EH2])
    m.b2 = sb("b2", [P, 3])
    m.sw3 = sb("sw3", [P, F])
    m.ew3 = sb("ew3", [P, 2, F])
    m.b3 = sb("b3", [NE + 1, F])
    m.gw = sb("gw", [P, KC, NE])
    m.gb = sb("gb", [P, NE])
    m.tie = sb("tie", [P, NE, NE])
    m.over_features = sb("over_features", [NE + 1, 2, P])
    m.dst_row = sb("dst_row", [P, 1 + nt * P], I32)
    m.src_col = sb("src_col", [P, nt], I32)
    m.dst_col = sb("dst_col", [P, nt], I32)
    m.put_col = sb("put_col", [P, nt], I32)
    m.dst_colf = sb("dst_colf", [P, nt])
    m.carry_pen = sb("carry_pen", [P, nt])
    m.scr_rows = sb("scr_rows", [nt, 3, P], I32)
    m.scr_rowsf = sb("scr_rowsf", [nt, 3, P])
    m.scr_cols = sb("scr_cols", [P, 3, nt])
    m.scr_a = sb("scr_a", [P, nt])

    loaded = nc.alloc_semaphore("setup_loaded")
    idx_loaded = nc.alloc_semaphore("setup_idx_loaded")
    cleared = nc.alloc_semaphore("setup_cleared")
    m.passed = nc.alloc_semaphore("passed")
    ident_ready = nc.alloc_semaphore("setup_ident_ready")
    rows_ready = nc.alloc_semaphore("setup_rows_ready")
    cols_ready = nc.alloc_semaphore("setup_cols_ready")
    step = nc.alloc_semaphore("setup_step")
    full, tail = m.edges // P, m.edges % P
    plain = [
        (m.w_gat[i][:, :, s * F:(s + 1) * F], w.rearrange("(c p) n -> p c n", p=P))
        for i in range(2) for s, w in enumerate((a[f"L0_gnn_Wl{i + 1}"], a[f"L0_gnn_Wr{i + 1}"]))
    ]
    for i in range(2):
        plain.append((m.att[i][:, :], a[f"L0_gnn_att{i + 1}"].rearrange("h c -> (h c)").partition_broadcast(P)))
        plain.append((m.b_gat[i][:, :], a[f"L0_gnn_b{i + 1}"].partition_broadcast(P)))
    plain += [
        (m.w1[:, :, 0:2 * P], a["L0_ffn_sW1"].rearrange("(c p) n -> p c n", p=P)),
        (m.sw2[:, :, :], a["L0_ffn_sW2"].rearrange("(c p) n -> p c n", p=P)),
        (m.ew2[:, :, :], a["L0_ffn_eW2"].rearrange("e p n -> p e n")),
        (m.sw3[:, :], a["L0_ffn_sW3"]),
        (m.b3[0:NE, :], a["L0_ffn_eb3"]),
        (m.b3[NE:NE + 1, :], a["L0_ffn_sb3"].partition_broadcast(1)),
        (m.gw[:, :, :], a["L0_ffn_gW"].rearrange("(c p) n -> p c n", p=P)),
        (m.gb[:, :], a["L0_ffn_gb"].partition_broadcast(P)),
        (m.b1[:, 0:2], a["L0_ffn_sb1"].rearrange("(c p) -> p c", p=P)),
        (m.b1[:, 2:NC1], a["L0_ffn_eb1"].rearrange("e p -> p e")),
        (m.b2[:, 0:1], a["L0_ffn_sb2"].rearrange("(c p) -> p c", p=P)),
    ]
    for e in range(NE):
        plain.append((m.w1[:, :, (2 + e) * P:(3 + e) * P], a["L0_ffn_eW1"][e].rearrange("(c p) n -> p c n", p=P)))
        half = slice((e % 2) * EH2, (e % 2 + 1) * EH2)
        plain.append((m.ew3[half, e // 2, :], a["L0_ffn_eW3"][e]))
        plain.append((m.b2[half, 1 + e // 2:2 + e // 2], a["L0_ffn_eb2"][e:e + 1, :].rearrange("e p -> p e")))
    src, dst = a["src"], a["dst"]
    indexes = [
        (m.scr_rows[0:full, 0, :], src[0:full * P].rearrange("(t p) -> t p", p=P)),
        (m.scr_rows[0:full, 1, :], dst[0:full * P].rearrange("(t p) -> t p", p=P)),
        (m.scr_rows[0:full, 2, :], dst[1:full * P + 1].rearrange("(t p) -> t p", p=P)),
        (m.scr_rows[full:full + 1, 0, 0:tail], src[full * P:m.edges].partition_broadcast(1)),
        (m.scr_rows[full:full + 1, 1, 0:tail], dst[full * P:m.edges].partition_broadcast(1)),
        (m.scr_rows[full:full + 1, 2, 0:tail - 1], dst[full * P + 1:m.edges].partition_broadcast(1)),
        (m.dst_row[:, 1:1 + m.edges], dst.partition_broadcast(P)),
    ]

    with nc.psum_tensor("ps_cols", [P, 3, nt], F32) as ps_cols, nc.Block() as block:
        @block.sync
        def _(sp):
            with nc.allow_non_contiguous_dma(reason="bias columns, once"):
                for out, in_ in plain:
                    sp.dma_start(out, in_).then_inc(loaded, 16)
            sp.wait_ge(cleared, 2)
            for out, in_ in indexes:
                sp.dma_start(out, in_).then_inc(idx_loaded, 16)
            sp.wait_ge(loaded, 16 * len(plain))

        @block.gpsimd
        def _(pool):
            pool.memset(m.ident[:, :], 0.0).then_inc(step, 1)
            pool.memset(m.last_row_ones[:, :], 0.0).then_inc(step, 1)
            pool.memset(m.tie[:, :, :], 1.0).then_inc(step, 1)
            pool.memset(m.over_features[:, :, :], 0.0).then_inc(step, 1)
            pool.wait_ge(step, 4)
            pool.affine_select(out=m.over_features[:, :, :].rearrange("e q (i f) -> e q i f", i=2),
                               in_=m.over_features[:, :, :].rearrange("e q (i f) -> e q i f", i=2),
                               compare_op=ALU.not_equal, fill=1.0, base=0, pattern=[[-2, 2], [-1, 2], [0, EH2]],
                               channel_multiplier=1).then_inc(step, 1)
            pool.affine_select(out=m.ident[:, :], in_=m.ident[:, :], compare_op=ALU.not_equal, fill=1.0, base=0,
                               pattern=[[-1, P]], channel_multiplier=1).then_inc(ident_ready, 1)
            pool.affine_select(out=m.last_row_ones[:, :], in_=m.last_row_ones[:, :], compare_op=ALU.not_equal,
                               fill=1.0, base=1 - P, pattern=[[0, P]], channel_multiplier=1).then_inc(step, 1)
            pool.affine_select(out=m.tie[:, :, :], in_=m.tie[:, :, :], compare_op=ALU.is_gt, fill=0.0, base=0,
                               pattern=[[1, NE], [-1, NE]], channel_multiplier=0).then_inc(step, 1)
            pool.wait_ge(step, 7)

        @block.vector
        def _(dve):
            dve.memset(m.scr_rows[:, :, :], -1).then_inc(cleared, 1)
            dve.memset(m.dst_row[:, :], -1).then_inc(cleared, 1)
            dve.memset(m.ln_eps[:, :], LN_EPS)
            dve.memset(m.minus_half[:, :], -0.5).then_inc(rows_ready, 1)
            dve.wait_ge(idx_loaded, 16 * len(indexes))
            dve.tensor_copy(m.scr_rowsf[:, :, :], m.scr_rows[:, :, :]).then_inc(rows_ready, 1)
            dve.wait_ge(cols_ready, 1)
            dve.tensor_copy(m.scr_cols[:, :, :], ps_cols[:, :, :]).then_inc(cols_ready, 1)
            dve.wait_ge(cols_ready, 2)
            dve.tensor_copy(m.src_col[:, :], m.scr_cols[:, 0, :]).then_inc(cols_ready, 1)
            dve.tensor_copy(m.dst_col[:, :], m.scr_cols[:, 1, :]).then_inc(cols_ready, 1)
            dve.tensor_copy(m.dst_colf[:, :], m.scr_cols[:, 1, :]).then_inc(cols_ready, 1)
            dve.tensor_tensor(m.scr_a[:, :], m.scr_cols[:, 1, :], m.scr_cols[:, 2, :], ALU.is_equal).then_inc(cols_ready, 1)
            before = m.dst_row[:, 0:nt * P].rearrange("p (t e) -> p t e", e=P)[:, :, 0]
            dve.tensor_tensor(m.carry_pen[:, :], m.scr_cols[:, 1, :], before, ALU.is_equal).then_inc(cols_ready, 1)
            dve.wait_ge(cols_ready, 7)
            dve.scalar_tensor_tensor(out=m.put_col[:, :], in0=m.scr_a[:, :], scalar=float(m.nodes), in1=m.scr_cols[:, 1, :],
                                     op0=ALU.mult, op1=ALU.add).then_inc(cols_ready, 1)
            dve.tensor_scalar(m.carry_pen[:, :], m.carry_pen[:, :], -1.0, BIG, ALU.add, ALU.mult).then_inc(cols_ready, 1)
            dve.wait_ge(cols_ready, 9)

        @block.tensor
        def _(pe):
            pe.wait_ge(ident_ready, 1)
            pe.wait_ge(rows_ready, 2)
            for i in range(3):
                last = pe.transpose(ps_cols[:, i, :], m.scr_rowsf[:, i, :], m.ident[0:nt, 0:nt])
            last.then_inc(cols_ready, 1)


def dense(nc, m, layer, feed, resid, out):
    pairs = m.groups // 2
    name = f"d{layer}_"
    norm = layer == 0
    with ExitStack() as ctx:
        def sb(n, shape, dt=F32):
            return ctx.enter_context(nc.sbuf_tensor(name + n, shape, dt))

        semaphores = []

        def sem(n):
            semaphores.append(ctx.enter_context(nc.semaphore(name + n)))
            return semaphores[-1]

        x = sb("x", [P, SLOTS, J, F])
        side = sb("side", [P, SLOTS, J, F])
        stats = sb("stats", [P, SLOTS, J, 6])
        moments = sb("moments", [P, SLOTS, J, 2])
        var = sb("var", [P, SLOTS, J])
        rstd = sb("rstd", [P, SLOTS, J])
        xt = sb("xt", [P, SLOTS, KC, G])
        z = sb("z", [P, SLOTS, J, F])
        low = sb("low", [P, SLOTS, J, F])
        res = sb("res", [P, SLOTS, J, F])
        ps_t = [ctx.enter_context(nc.psum_tensor(f"{name}ps_t{i}", [P, KC, G], F32)) for i in range(SLOTS)]
        ps_o = [ctx.enter_context(nc.psum_tensor(f"{name}ps_o{i}", [P, J, F], F32)) for i in range(SLOTS)]

        x_loaded = [sem(f"x_loaded{i}") for i in range(SLOTS)]
        r_loaded = [sem(f"r_loaded{i}") for i in range(SLOTS)]
        stored = [sem(f"stored{i}") for i in range(SLOTS)]
        counts = [sem(n) for n in ("stats_ready", "moments_ready", "var_ready", "rstd_ready", "rows_ready", "turned",
                                   "xt_ready", "product_ready", "z_ready", "low_ready", "exp_ready", "res_ready")]
        (stats_ready, moments_ready, var_ready, rstd_ready, rows_ready, turned,
         xt_ready, product_ready, z_ready, low_ready, exp_ready, res_ready) = counts
        rows_of = side if norm else x
        start_counts(nc, semaphores, counts)

        with nc.Block() as block:
            @block.sync
            def _(sp):
                def load(k, slot):
                    g = 2 * k + slot
                    start = group_rows(m.nodes, g, m.groups)
                    sp.wait_ge(rows_ready if norm else turned, done(g - SLOTS))
                    sp.dma_start(x[:, slot, :, :], nodes_of(feed, start)).then_inc(x_loaded[slot], 16)
                    if not norm:
                        sp.wait_ge(z_ready, done(g - SLOTS))
                        sp.dma_start(side[:, slot, :, :], nodes_of(resid, start)).then_inc(r_loaded[slot], 16)

                run(sp, pairs, [(load, 0)])

            @block.vector
            def _(dve):
                def statistics(k, slot):
                    g = 2 * k + slot
                    dve.wait_ge(x_loaded[slot], 16 * k + 16)
                    for j in range(J):
                        last = dve.bn_stats(stats[:, slot, j, :], x[:, slot, j, :])
                    last.then_inc(stats_ready, 1)
                    dve.wait_ge(rstd_ready, done(g - SLOTS))
                    wait_apart(dve, m, stats_ready, done(g))
                    for j in range(J):
                        last = dve.bn_aggr(moments[:, slot, j, :], stats[:, slot, j, :])
                    last.then_inc(moments_ready, 1)

                def normalise(k, slot):
                    g = 2 * k + slot
                    dve.wait_ge(rstd_ready, done(g))
                    dve.wait_ge(turned, done(g - SLOTS))
                    for j in range(J):
                        last = dve.tensor_scalar(side[:, slot, j, :], x[:, slot, j, :], moments[:, slot, j, 0:1],
                                                 rstd[:, slot, j:j + 1], ALU.subtract, ALU.mult)
                    last.then_inc(rows_ready, 1)

                def biased(k, slot):
                    g = 2 * k + slot
                    bias = m.b_gat[layer][:, :].unsqueeze(1).broadcast_to([P, J, F])
                    dve.wait_ge(res_ready, done(g - SLOTS))
                    dve.wait_ge(product_ready, done(g))
                    dve.tensor_tensor(z[:, slot, :, :], ps_o[slot][:, :, :], bias, ALU.add).then_inc(z_ready, 1)

                def elu(k, slot):
                    g = 2 * k + slot
                    dve.wait_ge(stored[slot], 16 * k)
                    dve.wait_ge(exp_ready, done(g))
                    dve.scalar_tensor_tensor(out=res[:, slot, :, :], in0=ps_o[slot][:, :, :], scalar=-1.0,
                                             in1=z[:, slot, :, :], op0=ALU.add, op1=ALU.max).then_inc(res_ready, 1)

                def sum_of_product(k, slot):
                    g = 2 * k + slot
                    dve.wait_ge(product_ready, done(g))
                    dve.wait_ge(z_ready, done(g))
                    dve.wait_ge(stored[slot], 16 * k)
                    dve.tensor_tensor(res[:, slot, :, :], ps_o[slot][:, :, :], z[:, slot, :, :], ALU.add).then_inc(res_ready, 1)

                if norm:
                    run(dve, pairs, [(biased, 0), (statistics, 3), (elu, 0), (normalise, 3)])
                else:
                    run(dve, pairs, [(sum_of_product, 0)])

            @block.gpsimd
            def _(pool):
                def scales(k, slot):
                    g = 2 * k + slot
                    pool.wait_ge(moments_ready, done(g))
                    pool.tensor_tensor(var[:, slot, :], moments[:, slot, :, 1], m.ln_eps[:, 0:J], ALU.add).then_inc(var_ready, 1)
                    pool.wait_ge(rows_ready, done(g - SLOTS))
                    pool.wait_ge(var_ready, done(g))
                    pool.tensor_tensor(rstd[:, slot, :], var[:, slot, :], m.minus_half[:, 0:J], ALU.pow).then_inc(rstd_ready, 1)

                def resid_bias(k, slot):
                    g = 2 * k + slot
                    pool.wait_ge(r_loaded[slot], 16 * k + 16)
                    pool.wait_ge(res_ready, done(g - SLOTS))
                    bias = m.b_gat[layer][:, :].unsqueeze(1).broadcast_to([P, J, F])
                    pool.tensor_tensor(z[:, slot, :, :], side[:, slot, :, :], bias, ALU.add).then_inc(z_ready, 1)

                run(pool, pairs, [(scales if norm else resid_bias, 0)])

            @block.tensor
            def _(pe):
                def turn(k, slot):
                    g = 2 * k + slot
                    if norm:
                        pe.wait_ge(rows_ready, done(g))
                    else:
                        pe.wait_ge(x_loaded[slot], 16 * k + 16)
                    pe.wait_ge(xt_ready, done(g - SLOTS))
                    for c in range(KC):
                        for j in range(J):
                            last = pe.transpose(ps_t[slot][:, c, j * P:(j + 1) * P], rows_of[:, slot, j, c * P:(c + 1) * P], m.ident[:, :])
                    last.then_inc(turned, 1)

                def product(k, slot):
                    g = 2 * k + slot
                    pe.wait_ge(xt_ready, done(g))
                    pe.wait_ge(res_ready, done(g - SLOTS))
                    for j in range(J):
                        for c in range(KC):
                            last = pe.matmul(ps_o[slot][:, j, :], lhsT=xt[:, slot, c, j * P:(j + 1) * P],
                                             rhs=m.w_gat[layer][:, c, 0:F], start=c == 0, stop=c == KC - 1)
                    last.then_inc(product_ready, 1)

                run(pe, pairs, [(product, 0), (turn, 2)])

            @block.scalar
            def _(act):
                def evacuate(k, slot):
                    g = 2 * k + slot
                    act.wait_ge(turned, done(g))
                    act.wait_ge(product_ready, done(g - SLOTS))
                    act.activation(xt[:, slot, :, :], ps_t[slot][:, :, :], ACT.Copy).then_inc(xt_ready, 1)

                def store(k, slot):
                    g = 2 * k + slot
                    act.wait_ge(res_ready, done(g))
                    if isinstance(g, int) and g == m.groups - 1:
                        act.wait_ge(stored[0], 16 * pairs)
                    act.dma_start(nodes_of(out, group_rows(m.nodes, g, m.groups)), res[:, slot, :, :]).then_inc(stored[slot], 16)

                def exps(k, slot):
                    g = 2 * k + slot
                    act.wait_ge(exp_ready, done(g - SLOTS))
                    act.wait_ge(z_ready, done(g))
                    act.activation(low[:, slot, :, :], z[:, slot, :, :], ACT.Relu, scale=-1.0).then_inc(low_ready, 1)
                    act.wait_ge(low_ready, done(g))
                    act.activation(ps_o[slot][:, :, :], low[:, slot, :, :], ACT.Exp, scale=-1.0).then_inc(exp_ready, 1)

                if norm:
                    run(act, pairs, [(exps, 0), (evacuate, 3), (store, 0)])
                else:
                    run(act, pairs, [(evacuate, 2), (store, 0)])
                for slot in range(SLOTS):
                    act.wait_ge(stored[slot], 16 * pairs)


def attend_edges(nc, m, layer, feed, resid, out):
    pairs = m.tiles // 2
    name = f"e{layer}_"
    norm = layer == 0
    W = H * (C + 1)
    with ExitStack() as ctx:
        def sb(n, shape, dt=F32):
            return ctx.enter_context(nc.sbuf_tensor(name + n, shape, dt))

        def ps(n, shape):
            return ctx.enter_context(nc.psum_tensor(name + n, shape, F32))

        semaphores = []

        def sem(n):
            semaphores.append(ctx.enter_context(nc.semaphore(name + n)))
            return semaphores[-1]

        def heads(ap):
            return ap.unsqueeze(2).broadcast_to([ap.shape[0], H, C])

        src_idx = sb("src_idx", [P, SLOTS, 1], I32)
        dst_idx = sb("dst_idx", [P, SLOTS, 1], I32)
        res_idx = sb("res_idx", [P, SLOTS, 1], I32)
        put_idx = sb("put_idx", [P, SLOTS, 1], I32)
        x = sb("x", [P, SLOTS, 2, F])
        rows = sb("rows", [P, SLOTS, 2, F]) if norm else x
        resid_rows = sb("resid_rows", [P, SLOTS, F])
        stats = sb("stats", [P, SLOTS, 2, 6])
        moments = sb("moments", [P, SLOTS, 2, 2])
        var = sb("var", [P, SLOTS, 2])
        rstd = sb("rstd", [P, SLOTS, 2])
        xt = sb("xt", [P, SLOTS, 2, KC, P])
        left = sb("left", [P, SLOTS, 2, F])
        fifth = sb("fifth", [P, 2 * F])
        scored = sb("scored", [P, 2, F])
        logits = sb("logits", [P, SLOTS, 2 * H])
        same = sb("same", [P, SLOTS, P])
        pen = sb("pen", [P, P])
        masked = sb("masked", [P, H, P])
        tile_max = sb("tile_max", [P, SLOTS, H])
        loop_max = sb("loop_max", [P, H])
        arg = sb("arg", [P, 4 * H])
        ex = sb("ex", [P, SLOTS, 4 * H])
        v = sb("v", [P, H, C + 1])
        carried = sb("carried", [P, H, C + 1])
        state = sb("state", [P, SLOTS, W + H])
        den = sb("den", [P, 2, H])
        coef = sb("coef", [P, SLOTS, 2 * H])
        loop_part = sb("loop_part", [P, SLOTS, F])
        sum_part = sb("sum_part", [P, F])
        both = sb("both", [P, F])
        z = sb("z", [P, SLOTS, F])
        low = sb("low", [P, SLOTS, F])
        res = sb("res", [P, SLOTS, F]) if norm else z
        ps_t = ps("ps_t", [P, 2, KC, P])
        ps_m = [ps(f"ps_m{i}", [P, 4, F]) for i in range(SLOTS)]
        ps_e = ps("ps_e", [P, 2 * F])
        ps_c = ps("ps_c", [P, W + H])
        ps_n = ps("ps_n", [P, W])

        gathered = [[sem(f"gathered_{w}{i}") for i in range(SLOTS)] for w in ("src", "dst", "resid")]
        scattered = [sem(f"scattered{i}") for i in range(SLOTS)]
        names = ("idx", "stats", "moments", "var", "rstd", "rows", "turned", "xt", "product", "left", "pre", "prelu", "leaky",
                 "scored", "logits", "spread", "same", "pen", "masked", "tile_max", "carry", "max", "arg0", "arg", "ex",
                 "v", "carried", "sums", "state", "den0", "den1", "den2", "coef", "loop_part", "sum_part", "both", "z",
                 "low", "exp", "res", "put", "resid_idx", "zb")
        s = {n: sem(n) for n in names}
        init = sem("init")

        def size(t):
            return m.edges - t * P if isinstance(t, int) and t == m.tiles - 1 else P

        start_counts(nc, semaphores, s.values())

        with nc.Block() as block:
            @block.gpsimd
            def _(pool):
                def gather(k, slot):
                    t = 2 * k + slot
                    p = size(t)
                    wait_apart(pool, m, s["rows"] if norm else s["turned"], done(t - SLOTS))
                    pool.tensor_copy(src_idx[:, slot, :], m.src_col[:, bass.ds(t, 1)])
                    pool.tensor_copy(dst_idx[:, slot, :], m.dst_col[:, bass.ds(t, 1)]).then_inc(s["idx"], 1)
                    wait_apart(pool, m, s["idx"], done(t))
                    for i, idx in ((0, src_idx), (1, dst_idx)):
                        pool.indirect_dma_start(out=x[0:p, slot, i, :], out_offset=None, in_=feed[:, :],
                                                in_offset=bass.IndirectOffsetOnAxis(ap=idx[0:p, slot, :], axis=0)
                                                ).then_inc(gathered[i][slot], 16)

                def scales(k, slot):
                    t = 2 * k + slot
                    p = size(t)
                    pool.wait_ge(s["moments"], done(t))
                    pool.tensor_tensor(var[0:p, slot, :], moments[0:p, slot, :, 1], m.ln_eps[0:p, 0:2], ALU.add).then_inc(s["var"], 1)
                    pool.wait_ge(s["rows"], done(t - SLOTS))
                    pool.wait_ge(s["var"], done(t))
                    pool.tensor_tensor(rstd[0:p, slot, :], var[0:p, slot, :], m.minus_half[0:p, 0:2], ALU.pow).then_inc(s["rstd"], 1)

                def gather_resid(k, slot):
                    t = 2 * k + slot
                    p = size(t)
                    wait_apart(pool, m, s["z"], done(t - SLOTS))
                    pool.tensor_copy(res_idx[:, slot, :], m.dst_col[:, bass.ds(t, 1)]).then_inc(s["resid_idx"], 1)
                    wait_apart(pool, m, s["resid_idx"], done(t))
                    pool.indirect_dma_start(out=resid_rows[0:p, slot, :], out_offset=None, in_=resid[:, :],
                                            in_offset=bass.IndirectOffsetOnAxis(ap=res_idx[0:p, slot, :], axis=0)
                                            ).then_inc(gathered[2][slot], 16)

                def combine(k, slot):
                    t = 2 * k + slot
                    p = size(t)
                    pool.wait_ge(s["coef"], done(t))
                    sums = state[0:p, slot, 0:W].rearrange("p (h c) -> p h c", h=H)[:, :, 0:C]
                    pool.tensor_tensor(sum_part[0:p, :].rearrange("p (h c) -> p h c", h=H), sums,
                                       heads(coef[0:p, slot, 0:H]), ALU.mult).then_inc(s["sum_part"], 1)
                    pool.wait_ge(s["loop_part"], done(t))
                    pool.wait_ge(s["sum_part"], done(t))
                    pool.tensor_tensor(both[0:p, :], sum_part[0:p, :], loop_part[0:p, slot, :], ALU.add).then_inc(s["both"], 1)
                    if norm:
                        pool.wait_ge(s["res"], done(t - SLOTS))
                    else:
                        pool.wait_ge(scattered[slot], 16 * k)
                    pool.wait_ge(s["both"], done(t))
                    target = z[0:p, slot, :]
                    if norm:
                        pool.tensor_tensor(target, both[0:p, :], m.b_gat[layer][0:p, :], ALU.add).then_inc(s["z"], 1)
                    else:
                        pool.tensor_tensor(low[0:p, slot, :], both[0:p, :], m.b_gat[layer][0:p, :], ALU.add).then_inc(s["zb"], 1)
                        pool.wait_ge(gathered[2][slot], 16 * k + 16)
                        pool.wait_ge(s["zb"], done(t))
                        pool.tensor_tensor(target, low[0:p, slot, :], resid_rows[0:p, slot, :], ALU.add).then_inc(s["z"], 1)

                def scatter(k, slot):
                    t = 2 * k + slot
                    p = size(t)
                    wait_apart(pool, m, scattered[slot], 16 * k)
                    pool.tensor_copy(put_idx[:, slot, :], m.put_col[:, bass.ds(t, 1)]).then_inc(s["put"], 1)
                    pool.wait_ge(s["res"] if norm else s["z"], done(t))
                    wait_apart(pool, m, s["put"], done(t))
                    pool.indirect_dma_start(out=out[:, :], out_offset=bass.IndirectOffsetOnAxis(ap=put_idx[0:p, slot, :], axis=0),
                                            in_=res[0:p, slot, :], in_offset=None, bounds_check=m.nodes - 1,
                                            oob_is_err=False).then_inc(scattered[slot], 16)

                if norm:
                    run(pool, pairs, [(gather, 4), (scatter, -2), (combine, 0), (scales, 3)])
                else:
                    run(pool, pairs, [(gather, 3), (scatter, -1), (gather_resid, 0), (combine, 0)])
                for slot in range(SLOTS):
                    pool.wait_ge(scattered[slot], 16 * pairs)

            @block.vector
            def _(dve):
                def statistics(k, slot):
                    t = 2 * k + slot
                    p = size(t)
                    for i in range(2):
                        dve.wait_ge(gathered[i][slot], 16 * k + 16)
                    for i in range(2):
                        last = dve.bn_stats(stats[0:p, slot, i, :], x[0:p, slot, i, :])
                    last.then_inc(s["stats"], 1)
                    dve.wait_ge(s["rstd"], done(t - SLOTS))
                    wait_apart(dve, m, s["stats"], done(t))
                    for i in range(2):
                        last = dve.bn_aggr(moments[0:p, slot, i, :], stats[0:p, slot, i, :])
                    last.then_inc(s["moments"], 1)

                def normalise(k, slot):
                    t = 2 * k + slot
                    p = size(t)
                    dve.wait_ge(s["turned"], done(t - SLOTS))
                    dve.wait_ge(s["rstd"], done(t))
                    for i in range(2):
                        last = dve.tensor_scalar(rows[0:p, slot, i, :], x[0:p, slot, i, :], moments[0:p, slot, i, 0:1],
                                                 rstd[0:p, slot, i:i + 1], ALU.subtract, ALU.mult)
                    last.then_inc(s["rows"], 1)

                def maxima(k, slot):
                    t = 2 * k + slot
                    p = size(t)
                    top = state[0:p, slot, W:W + H]
                    dve.wait_ge(s["carry"], done(t))
                    dve.wait_ge(s["tile_max"], done(t))
                    pen_t = m.carry_pen[0:p, bass.ds(t, 1)]
                    dve.scalar_tensor_tensor(out=top, in0=ps_c[0:p, W:W + H], scalar=pen_t, in1=tile_max[0:p, slot, :],
                                             op0=ALU.add, op1=ALU.max).then_inc(s["max"], 1)
                    dve.wait_ge(s["ex"], done(t - 1))
                    dve.wait_ge(s["max"], done(t))
                    dve.tensor_tensor(loop_max[0:p, :], top, logits[0:p, slot, H:2 * H], ALU.max).then_inc(s["arg0"], 1)
                    dve.tensor_tensor(arg[0:p, 0:H], logits[0:p, slot, 0:H], top, ALU.subtract)
                    dve.scalar_tensor_tensor(out=arg[0:p, H:2 * H], in0=ps_c[0:p, W:W + H], scalar=pen_t, in1=top,
                                             op0=ALU.add, op1=ALU.subtract)
                    dve.wait_ge(s["arg0"], done(t))
                    dve.tensor_tensor(arg[0:p, 2 * H:3 * H], top, loop_max[0:p, :], ALU.subtract)
                    dve.tensor_tensor(arg[0:p, 3 * H:4 * H], logits[0:p, slot, H:2 * H], loop_max[0:p, :],
                                      ALU.subtract).then_inc(s["arg"], 1)

                def pre_activations(k, slot):
                    t = 2 * k + slot
                    p = size(t)
                    dve.wait_ge(s["tile_max"], done(t - 1))
                    dve.wait_ge(s["left"], done(t))
                    right = ps_m[slot][0:p, 3, :].unsqueeze(1).broadcast_to([p, 2, F])
                    dve.tensor_tensor(ps_e[0:p, :].rearrange("p (i f) -> p i f", i=2), left[0:p, slot, :, :], right,
                                      ALU.add).then_inc(s["pre"], 1)

                def weigh(k, slot):
                    t = 2 * k + slot
                    p = size(t)
                    dve.wait_ge(s["sums"], done(t - 1))
                    dve.wait_ge(s["ex"], done(t))
                    dve.tensor_tensor(v[0:p, :, 0:C], ps_m[slot][0:p, 1, :].rearrange("p (h c) -> p h c", h=H),
                                      heads(ex[0:p, slot, 0:H]), ALU.mult)
                    dve.tensor_copy(v[0:p, :, C], ex[0:p, slot, 0:H]).then_inc(s["v"], 1)
                    dve.wait_ge(s["state"], done(t - 1))
                    dve.tensor_tensor(carried[0:p, :, :], ps_c[0:p, 0:W].rearrange("p (h c) -> p h c", h=H),
                                      ex[0:p, slot, H:2 * H].unsqueeze(2).broadcast_to([p, H, C + 1]), ALU.mult
                                      ).then_inc(s["carried"], 1)

                def score(k, slot):
                    t = 2 * k + slot
                    p = size(t)
                    att = m.att[layer][0:p, :].unsqueeze(1).broadcast_to([p, 2, F])
                    dve.wait_ge(s["logits"], done(t - 1))
                    dve.wait_ge(s["prelu"], done(t))
                    dve.tensor_tensor(ps_e[0:p, :], ps_e[0:p, :], fifth[0:p, :], ALU.max).then_inc(s["leaky"], 1)
                    dve.wait_ge(s["leaky"], done(t))
                    dve.tensor_tensor(scored[0:p, :, :], ps_e[0:p, :].rearrange("p (i f) -> p i f", i=2), att,
                                      ALU.mult).then_inc(s["scored"], 1)
                    dve.wait_ge(s["arg"], done(t - SLOTS))
                    dve.wait_ge(s["scored"], done(t))
                    dve.reduce_sum(logits[0:p, slot, :], scored[0:p, :, :].rearrange("p i (h c) -> p (i h) c", h=H),
                                   axis=AXX).then_inc(s["logits"], 1)

                def accumulate(k, slot):
                    t = 2 * k + slot
                    p = size(t)
                    dve.wait_ge(s["both"], done(t - SLOTS))
                    dve.wait_ge(s["carried"], done(t))
                    dve.wait_ge(s["sums"], done(t))
                    dve.tensor_tensor(state[0:p, slot, 0:W], ps_n[0:p, :], carried[0:p, :, :].rearrange("p h c -> p (h c)"),
                                      ALU.add).then_inc(s["state"], 1)
                    dve.wait_ge(s["state"], done(t))
                    a, b = ex[0:p, slot, 2 * H:3 * H], ex[0:p, slot, 3 * H:4 * H]
                    dens = state[0:p, slot, 0:W].rearrange("p (h c) -> p h c", h=H)[:, :, C]
                    dve.wait_ge(s["coef"], done(t - 1))
                    dve.tensor_tensor(den[0:p, 0, :], dens, a, ALU.mult).then_inc(s["den0"], 1)
                    dve.wait_ge(s["den0"], done(t))
                    dve.scalar_tensor_tensor(out=den[0:p, 1, :], in0=den[0:p, 0, :], scalar=DEN_EPS, in1=b,
                                             op0=ALU.add, op1=ALU.add).then_inc(s["den1"], 1)
                    dve.wait_ge(s["den1"], done(t))
                    dve.reciprocal(den[0:p, 0, :], den[0:p, 1, :]).then_inc(s["den2"], 1)
                    dve.wait_ge(s["den2"], done(t))
                    dve.tensor_tensor(coef[0:p, slot, 0:H], a, den[0:p, 0, :], ALU.mult)
                    dve.tensor_tensor(coef[0:p, slot, H:2 * H], b, den[0:p, 0, :], ALU.mult).then_inc(s["coef"], 1)
                    dve.wait_ge(s["coef"], done(t))
                    dve.tensor_tensor(loop_part[0:p, slot, :].rearrange("p (h c) -> p h c", h=H),
                                      ps_m[slot][0:p, 2, :].rearrange("p (h c) -> p h c", h=H),
                                      heads(coef[0:p, slot, H:2 * H]), ALU.mult).then_inc(s["loop_part"], 1)

                def group(k, slot):
                    t = 2 * k + slot
                    p = size(t)
                    dve.wait_ge(s["sums"], done(t - SLOTS))
                    dve.tensor_scalar(same[0:p, slot, 0:p], m.dst_row[0:p, bass.ds(t * P + 1, p)], m.dst_colf[0:p, bass.ds(t, 1)],
                                      None, ALU.is_equal).then_inc(s["same"], 1)
                    dve.wait_ge(s["masked"], done(t - 1))
                    dve.wait_ge(s["same"], done(t))
                    dve.tensor_scalar(pen[0:p, 0:p], same[0:p, slot, 0:p], -1.0, BIG, ALU.add, ALU.mult).then_inc(s["pen"], 1)
                    dve.wait_ge(s["spread"], done(t))
                    dve.wait_ge(s["pen"], done(t))
                    dve.tensor_tensor(masked[0:p, :, 0:p], ps_e[0:p, :].rearrange("p (h e) -> p h e", h=H)[:, :, 0:p],
                                      pen[0:p, 0:p].unsqueeze(1).broadcast_to([p, H, p]), ALU.add).then_inc(s["masked"], 1)
                    dve.wait_ge(s["masked"], done(t))
                    dve.reduce_max(tile_max[0:p, slot, :], masked[0:p, :, 0:p], axis=AXX).then_inc(s["tile_max"], 1)

                def low_part(k, slot):
                    t = 2 * k + slot
                    p = size(t)
                    dve.wait_ge(s["res"], done(t - SLOTS))
                    dve.wait_ge(s["z"], done(t))
                    dve.tensor_scalar(low[0:p, slot, :], z[0:p, slot, :], 0.0, None, ALU.min).then_inc(s["low"], 1)

                def elu(k, slot):
                    t = 2 * k + slot
                    p = size(t)
                    dve.wait_ge(scattered[slot], 16 * k)
                    dve.wait_ge(s["exp"], done(t))
                    dve.scalar_tensor_tensor(out=res[0:p, slot, :], in0=low[0:p, slot, :], scalar=-1.0, in1=z[0:p, slot, :],
                                             op0=ALU.add, op1=ALU.max).then_inc(s["res"], 1)

                dve.memset(state[:, SLOTS - 1, :], 0.0).then_inc(init, 1)
                if norm:
                    run(dve, pairs, [(maxima, 0), (normalise, 2), (pre_activations, 1), (weigh, 0), (score, 1), (accumulate, 0),
                                     (group, 1), (low_part, -1), (statistics, 3), (elu, -1)])
                else:
                    run(dve, pairs, [(maxima, 0), (pre_activations, 1), (weigh, 0), (score, 1), (accumulate, 0), (group, 1)])

            @block.tensor
            def _(pe):
                def carry(k, slot):
                    t = 2 * k + slot
                    pe.wait_ge(init, 1)
                    pe.wait_ge(s["carried"], done(t - 1))
                    pe.wait_ge(s["state"], done(t - 1))
                    pe.matmul(ps_c[:, :], lhsT=m.last_row_ones[:, :], rhs=state[:, 1 - slot, :], start=True,
                              stop=True).then_inc(s["carry"], 1)

                def turn(k, slot):
                    t = 2 * k + slot
                    p = size(t)
                    pe.wait_ge(s["xt"], done(t - 1))
                    if norm:
                        pe.wait_ge(s["rows"], done(t))
                    else:
                        for i in range(2):
                            pe.wait_ge(gathered[i][slot], 16 * k + 16)
                    for i in range(2):
                        for c in range(KC):
                            last = pe.transpose(ps_t[:, i, c, 0:p], rows[0:p, slot, i, c * P:(c + 1) * P], m.ident[0:p, 0:p])
                    last.then_inc(s["turned"], 1)

                def product(k, slot):
                    t = 2 * k + slot
                    p = size(t)
                    pe.wait_ge(s["loop_part"], done(t - SLOTS))
                    pe.wait_ge(s["xt"], done(t))
                    for i, (first, last_) in enumerate(((1, 2), (2, 4))):
                        for c in range(KC):
                            last = pe.matmul(ps_m[slot][0:p, first:last_, :], lhsT=xt[:, slot, i, c, 0:p],
                                             rhs=m.w_gat[layer][:, c, 0:(last_ - first) * F], start=c == 0, stop=c == KC - 1)
                    last.then_inc(s["product"], 1)

                def spread(k, slot):
                    t = 2 * k + slot
                    p = size(t)
                    pe.wait_ge(s["logits"], done(t))
                    for h in range(H):
                        last = pe.matmul(ps_e[0:p, h * P:h * P + p], lhsT=logits[0:p, slot, h:h + 1].broadcast_to([p, p]),
                                         rhs=m.ident[0:p, 0:p], start=True, stop=True)
                    last.then_inc(s["spread"], 1)

                def sums(k, slot):
                    t = 2 * k + slot
                    p = size(t)
                    pe.wait_ge(s["state"], done(t - 1))
                    pe.wait_ge(s["v"], done(t))
                    pe.matmul(ps_n[0:p, :], lhsT=same[0:p, slot, 0:p], rhs=v[0:p, :, :].rearrange("p h c -> p (h c)"),
                              start=True, stop=True).then_inc(s["sums"], 1)

                run(pe, pairs, [(carry, 0), (turn, 2), (sums, 0), (spread, 1), (product, 2)])

            @block.scalar
            def _(act):
                def weights(k, slot):
                    t = 2 * k + slot
                    p = size(t)
                    act.wait_ge(s["coef"], done(t - SLOTS))
                    act.wait_ge(s["arg"], done(t))
                    act.activation(ex[0:p, slot, :], arg[0:p, :], ACT.Exp).then_inc(s["ex"], 1)

                def leaky(k, slot):
                    t = 2 * k + slot
                    p = size(t)
                    act.wait_ge(s["pre"], done(t))
                    act.wait_ge(s["scored"], done(t - 1))
                    act.activation(fifth[0:p, :], ps_e[0:p, :], ACT.Copy, scale=SLOPE).then_inc(s["prelu"], 1)

                def evacuate_rows(k, slot):
                    t = 2 * k + slot
                    p = size(t)
                    act.wait_ge(s["product"], done(t - SLOTS))
                    act.wait_ge(s["turned"], done(t))
                    act.activation(xt[:, slot, :, :, 0:p], ps_t[:, :, :, 0:p], ACT.Copy).then_inc(s["xt"], 1)

                def evacuate_left(k, slot):
                    t = 2 * k + slot
                    p = size(t)
                    act.wait_ge(s["pre"], done(t - SLOTS))
                    act.wait_ge(s["product"], done(t))
                    act.activation(left[0:p, slot, :, :], ps_m[slot][0:p, 1:3, :], ACT.Copy).then_inc(s["left"], 1)

                def low_exp(k, slot):
                    t = 2 * k + slot
                    p = size(t)
                    act.wait_ge(s["low"], done(t))
                    act.activation(low[0:p, slot, :], low[0:p, slot, :], ACT.Exp).then_inc(s["exp"], 1)

                run(act, pairs, [(weights, 0), (leaky, 1), (evacuate_rows, 2)] + [(low_exp, -1)] * norm + [(evacuate_left, 2)])


def ffn(nc, m, feed, out):
    pairs = m.groups // 2
    name = "f_"
    with ExitStack() as ctx:
        def sb(n, shape, dt=F32):
            return ctx.enter_context(nc.sbuf_tensor(name + n, shape, dt))

        semaphores = []

        def sem(n):
            semaphores.append(ctx.enter_context(nc.semaphore(name + n)))
            return semaphores[-1]

        x = sb("x", [P, SLOTS, J, F])
        again = sb("again", [P, SLOTS, J, F])
        rows = sb("rows", [P, SLOTS, J, F])
        stats = sb("stats", [P, SLOTS, J, 6])
        moments = sb("moments", [P, SLOTS, J, 2])
        var = sb("var", [P, SLOTS, J])
        rstd = sb("rstd", [P, SLOTS, J])
        xt = sb("xt", [P, SLOTS, KC, G])
        act1 = sb("act1", [P, NC1, G])
        act2 = sb("act2", [P, 3, G])
        gated = sb("gated", [P, 2, G])
        gate_t = sb("gate_t", [NE + 1, G])
        logits = sb("logits", [P, J, NE])
        top = sb("top", [P, J])
        over = sb("over", [P, J, NE])
        shifted = sb("shifted", [P, J, NE])
        exps = sb("exps", [P, J, NE])
        total = sb("total", [P, J])
        inverse = sb("inverse", [P, J])
        gates = sb("gates", [P, J, NE])
        greater = sb("greater", [P, J, NE, NE])
        equal = sb("equal", [P, J, NE, NE])
        rank = sb("rank", [P, J, NE])
        chosen = sb("chosen", [P, J, NE])
        weight = sb("weight", [P, J, NE + 1])
        res = sb("res", [P, SLOTS, J, F])
        bank = [ctx.enter_context(nc.psum_tensor(f"{name}bank{i}", [P, G], F32)) for i in range(5)]
        ps_g = ctx.enter_context(nc.psum_tensor(f"{name}ps_g", [P, J, NE], F32))
        ps_y = ctx.enter_context(nc.psum_tensor(f"{name}ps_y", [P, J, F], F32))

        x_loaded = [sem(f"x_loaded{i}") for i in range(SLOTS)]
        again_loaded = [sem(f"again_loaded{i}") for i in range(SLOTS)]
        stored = [sem(f"stored{i}") for i in range(SLOTS)]
        s = {n: sem(n) for n in ("stats", "moments", "var", "rstd", "rows", "gate_product", "logits", "top", "shifted",
                                      "exps", "total", "inverse", "gates", "compared", "tied", "beaten", "rank", "chosen", "over",
                                      "exps2", "picked", "total2", "inverse2", "weight", "spread0", "spread1", "gate_rows",
                                      "gate_t", "gated0", "gated1", "y", "res")}
        turned, xt_kept = sem("turned"), sem("xt_kept")
        made1, kept1 = sem("made1"), sem("kept1")
        made2, kept2 = sem("made2"), sem("kept2")
        ones = sem("ones")
        start_counts(nc, semaphores, s.values())

        def over_experts(ap):
            return ap.unsqueeze(2).broadcast_to([P, J, NE])

        with nc.Block() as block:
            @block.sync
            def _(sp):
                def load(k, slot):
                    g = 2 * k + slot
                    sp.wait_ge(s["rows"], done(g - SLOTS))
                    sp.dma_start(x[:, slot, :, :], nodes_of(feed, group_rows(m.nodes, g, m.groups))).then_inc(x_loaded[slot], 16)

                def load_again(k, slot):
                    g = 2 * k + slot
                    sp.wait_ge(s["res"], done(g - SLOTS))
                    sp.dma_start(again[:, slot, :, :], nodes_of(feed, group_rows(m.nodes, g, m.groups))).then_inc(again_loaded[slot], 16)

                def store(k, slot):
                    g = 2 * k + slot
                    sp.wait_ge(s["res"], done(g))
                    if isinstance(g, int) and g == m.groups - 1:
                        sp.wait_ge(stored[0], 16 * pairs)
                    sp.dma_start(nodes_of(out, group_rows(m.nodes, g, m.groups)), res[:, slot, :, :]).then_inc(stored[slot], 16)

                run(sp, pairs, [(load, 3), (load_again, 0), (store, -1)])
                for slot in range(SLOTS):
                    sp.wait_ge(stored[slot], 16 * pairs)

            @block.gpsimd
            def _(pool):
                def scales(k, slot):
                    g = 2 * k + slot
                    pool.wait_ge(s["moments"], done(g))
                    pool.tensor_tensor(var[:, slot, :], moments[:, slot, :, 1], m.ln_eps[:, 0:J], ALU.add).then_inc(s["var"], 1)
                    pool.wait_ge(s["rows"], done(g - SLOTS))
                    pool.wait_ge(s["var"], done(g))
                    pool.tensor_tensor(rstd[:, slot, :], var[:, slot, :], m.minus_half[:, 0:J], ALU.pow).then_inc(s["rstd"], 1)

                run(pool, pairs, [(scales, 0)])

            @block.vector
            def _(dve):
                def statistics(k, slot):
                    g = 2 * k + slot
                    dve.wait_ge(x_loaded[slot], 16 * k + 16)
                    for j in range(J):
                        last = dve.bn_stats(stats[:, slot, j, :], x[:, slot, j, :])
                    last.then_inc(s["stats"], 1)
                    dve.wait_ge(s["rstd"], done(g - SLOTS))
                    wait_apart(dve, m, s["stats"], done(g))
                    for j in range(J):
                        last = dve.bn_aggr(moments[:, slot, j, :], stats[:, slot, j, :])
                    last.then_inc(s["moments"], 1)

                def normalise(k, slot):
                    g = 2 * k + slot
                    dve.wait_ge(turned, KC * g)
                    dve.wait_ge(s["rstd"], done(g))
                    for j in range(J):
                        last = dve.tensor_scalar(rows[:, slot, j, :], x[:, slot, j, :], moments[:, slot, j, 0:1],
                                                 rstd[:, slot, j:j + 1], ALU.subtract, ALU.mult)
                    last.then_inc(s["rows"], 1)

                def gate_logits(k, slot):
                    g = 2 * k + slot
                    dve.wait_ge(s["gate_product"], done(g))
                    dve.tensor_tensor(logits[:, :, :], ps_g[:, :, :], m.gb[:, :].unsqueeze(1).broadcast_to([P, J, NE]),
                                      ALU.add).then_inc(s["logits"], 1)
                    dve.wait_ge(s["logits"], done(g))
                    dve.reduce_max(top[:, :], logits[:, :, :], axis=AXX).then_inc(s["top"], 1)
                    dve.wait_ge(s["top"], done(g))
                    dve.tensor_tensor(shifted[:, :, :], logits[:, :, :], over_experts(top[:, :]), ALU.subtract).then_inc(s["shifted"], 1)

                def gates_and_ranks(k, slot):
                    g = 2 * k + slot
                    dve.wait_ge(s["exps"], done(g))
                    dve.reduce_sum(total[:, :], exps[:, :, :], axis=AXX).then_inc(s["total"], 1)
                    dve.wait_ge(s["total"], done(g))
                    dve.reciprocal(inverse[:, :], total[:, :]).then_inc(s["inverse"], 1)
                    dve.wait_ge(s["inverse"], done(g))
                    dve.tensor_tensor(gates[:, :, :], exps[:, :, :], over_experts(inverse[:, :]), ALU.mult).then_inc(s["gates"], 1)
                    dve.wait_ge(s["gates"], done(g))
                    dve.tensor_tensor(over[:, :, :], gates[:, :, :], over_experts(inverse[:, :]), ALU.subtract).then_inc(s["over"], 1)
                    rival = gates[:, :, :].unsqueeze(2).broadcast_to([P, J, NE, NE])
                    own = gates[:, :, :].unsqueeze(3).broadcast_to([P, J, NE, NE])
                    dve.tensor_tensor(greater[:, :, :, :], rival, own, ALU.is_gt)
                    dve.tensor_tensor(equal[:, :, :, :], rival, own, ALU.is_equal).then_inc(s["compared"], 1)
                    dve.wait_ge(s["compared"], done(g))
                    dve.tensor_tensor(equal[:, :, :, :], equal[:, :, :, :], m.tie[:, :, :].unsqueeze(1).broadcast_to([P, J, NE, NE]),
                                      ALU.mult).then_inc(s["tied"], 1)
                    dve.wait_ge(s["tied"], done(g))
                    dve.tensor_tensor(greater[:, :, :, :], greater[:, :, :, :], equal[:, :, :, :], ALU.add).then_inc(s["beaten"], 1)
                    dve.wait_ge(s["beaten"], done(g))
                    dve.reduce_sum(rank[:, :, :], greater[:, :, :, :], axis=AXX).then_inc(s["rank"], 1)
                    dve.wait_ge(s["rank"], done(g))
                    dve.tensor_scalar(chosen[:, :, :], rank[:, :, :], float(TOPK), None, ALU.is_lt).then_inc(s["chosen"], 1)

                def weights(k, slot):
                    g = 2 * k + slot
                    dve.wait_ge(s["chosen"], done(g))
                    dve.wait_ge(s["exps2"], done(g))
                    dve.tensor_tensor(chosen[:, :, :], exps[:, :, :], chosen[:, :, :], ALU.mult).then_inc(s["picked"], 1)
                    dve.wait_ge(s["picked"], done(g))
                    dve.reduce_sum(total[:, :], chosen[:, :, :], axis=AXX).then_inc(s["total2"], 1)
                    dve.wait_ge(s["total2"], done(g))
                    dve.reciprocal(inverse[:, :], total[:, :]).then_inc(s["inverse2"], 1)
                    dve.wait_ge(s["inverse2"], done(g))
                    dve.tensor_tensor(weight[:, :, 0:NE], chosen[:, :, :], over_experts(inverse[:, :]), ALU.mult).then_inc(s["weight"], 1)

                def gate_experts(k, slot):
                    g = 2 * k + slot
                    for q in range(2):
                        dve.wait_ge(s["y"], done(g - 1))
                        dve.wait_ge((s["spread0"], s["spread1"])[q], done(g))
                        dve.wait_ge(kept2, 3 * g + 2 + q)
                        dve.tensor_tensor(gated[:, q, :], act2[:, 1 + q, :], bank[1 + q][:, :],
                                          ALU.mult).then_inc((s["gated0"], s["gated1"])[q], 1)

                def add_up(k, slot):
                    g = 2 * k + slot
                    dve.wait_ge(again_loaded[slot], 16 * k + 16)
                    dve.wait_ge(stored[slot], 16 * k)
                    dve.wait_ge(s["y"], done(g))
                    dve.tensor_tensor(res[:, slot, :, :], ps_y[:, :, :], again[:, slot, :, :], ALU.add).then_inc(s["res"], 1)

                dve.memset(weight[:, :, :], 1.0).then_inc(ones, 1)
                dve.wait_ge(ones, 1)
                run(dve, pairs, [(gate_logits, 0), (add_up, -1), (gates_and_ranks, 0), (statistics, 2), (weights, 0),
                                 (normalise, 2), (gate_experts, 0)])

            @block.tensor
            def _(pe):
                def gate_product(k, slot):
                    g = 2 * k + slot
                    pe.wait_ge(xt_kept, KC * (g + 1))
                    pe.wait_ge(s["logits"], done(g - 1))
                    for j in range(J):
                        for c in range(KC):
                            last = pe.matmul(ps_g[:, j, :], lhsT=xt[:, slot, c, j * P:(j + 1) * P], rhs=m.gw[:, c, :],
                                             start=c == 0, stop=c == KC - 1)
                    last.then_inc(s["gate_product"], 1)

                def first_layer(k, slot, i):
                    g = 2 * k + slot
                    if i == 0:
                        pe.wait_ge(kept2, 3 * g)
                    elif i < 3:
                        pe.wait_ge((s["gated0"], s["gated1"])[i - 1], done(g - 1))
                    else:
                        pe.wait_ge(kept1, NC1 * g + i - 2)
                    for c in range(KC):
                        last = pe.matmul(bank[i % 3][:, :], lhsT=m.w1[:, c, i * P:(i + 1) * P], rhs=xt[:, slot, c, :],
                                         start=c == 0, stop=c == KC - 1)
                    last.then_inc(made1, 1)

                def first_layer_start(k, slot):
                    for i in range(2):
                        first_layer(k, slot, i)

                def first_layer_end(k, slot):
                    for i in range(2, NC1):
                        first_layer(k, slot, i)

                def third_layer(k, slot):
                    g = 2 * k + slot
                    pe.wait_ge(s["res"], done(g - 1))
                    pe.wait_ge(s["gate_t"], done(g))
                    pe.wait_ge(s["gated0"], done(g))
                    pe.wait_ge(s["gated1"], done(g))
                    for j in range(J):
                        js = slice(j * P, (j + 1) * P)
                        pe.matmul(ps_y[:, j, :], lhsT=act2[:, 0, js], rhs=m.sw3[:, :], start=True, stop=False)
                        for q in range(2):
                            pe.matmul(ps_y[:, j, :], lhsT=gated[:, q, js], rhs=m.ew3[:, q, :], start=False, stop=False)
                        last = pe.matmul(ps_y[:, j, :], lhsT=gate_t[:, js], rhs=m.b3[:, :], start=False, stop=True)
                    last.then_inc(s["y"], 1)

                def turn(k, slot):
                    g = 2 * k + slot
                    pe.wait_ge(s["rows"], done(g))
                    for c in range(KC):
                        if not isinstance(g, int) or g > 1:
                            pe.wait_ge(kept2, 3 * (g - 2) + c + 1)
                        for j in range(J):
                            last = pe.transpose(bank[3 + c][:, j * P:(j + 1) * P], rows[:, slot, j, c * P:(c + 1) * P], m.ident[:, :])
                        last.then_inc(turned, 1)

                def turn_gates(k, slot):
                    g = 2 * k + slot
                    pe.wait_ge(s["weight"], done(g))
                    pe.wait_ge(kept1, NC1 * g + 4)
                    for j in range(J):
                        last = pe.transpose(bank[0][0:NE + 1, j * P:(j + 1) * P], weight[:, j, :], m.ident[:, :])
                    last.then_inc(s["gate_rows"], 1)
                def second_layer(k, slot):
                    g = 2 * k + slot
                    pe.wait_ge(kept1, NC1 * (g + 1))
                    pe.wait_ge(xt_kept, KC * g + KC + 1 if not last_group(g) else KC * (g + 1))
                    for c in range(KC):
                        last = pe.matmul(bank[3][:, :], lhsT=m.sw2[:, c, :], rhs=act1[:, c, :], start=c == 0, stop=c == KC - 1)
                    last.then_inc(made2, 1)
                    pe.wait_ge(s["gate_t"], done(g))
                    for q in range(2):
                        pe.matmul(bank[1 + q][:, :], lhsT=m.over_features[:, q, :], rhs=gate_t[:, :], start=True,
                                  stop=True).then_inc((s["spread0"], s["spread1"])[q], 1)
                    for q in range(2):
                        if q == 0:
                            pe.wait_ge(xt_kept, KC * (g + 2) if not last_group(g) else KC * (g + 1))
                        for i in range(2):
                            e = 2 * q + i
                            last = pe.matmul(bank[4 if q == 0 else 0][i * EH2:(i + 1) * EH2, :], lhsT=m.ew2[:, e, :],
                                             rhs=act1[:, 2 + e, :], start=True, stop=True)
                        last.then_inc(made2, 1)

                def last_group(g):
                    return isinstance(g, int) and g == m.groups - 1

                run(pe, pairs, [(gate_product, 0), (first_layer_start, 0), (third_layer, -1), (first_layer_end, 0), (turn, 1),
                                (turn_gates, 0), (second_layer, 0)])

            @block.scalar
            def _(act):
                def keep_first(k, slot, chunks):
                    g = 2 * k + slot
                    for i in chunks:
                        act.wait_ge(made1, NC1 * g + i + 1)
                        act.activation(act1[:, i, :], bank[i % 3][:, :], ACT.Relu, bias=m.b1[:, i:i + 1]).then_inc(kept1, 1)

                def keep_first_a(k, slot):
                    keep_first(k, slot, (0, 1))

                def keep_first_b(k, slot):
                    keep_first(k, slot, (2, 3))

                def keep_first_c(k, slot):
                    keep_first(k, slot, (4, 5))

                def exp_logits(k, slot):
                    g = 2 * k + slot
                    act.wait_ge(s["picked"], done(g - 1))
                    act.wait_ge(s["shifted"], done(g))
                    act.activation(exps[:, :, :], shifted[:, :, :], ACT.Exp).then_inc(s["exps"], 1)

                def exp_gates(k, slot):
                    g = 2 * k + slot
                    act.wait_ge(s["over"], done(g))
                    act.activation(exps[:, :, :], over[:, :, :], ACT.Exp).then_inc(s["exps2"], 1)

                def keep_rows(k, slot):
                    g = 2 * k + slot
                    for c in range(KC):
                        act.wait_ge(turned, KC * g + c + 1)
                        act.activation(xt[:, slot, c, :], bank[3 + c][:, :], ACT.Copy).then_inc(xt_kept, 1)

                def keep_gates(k, slot):
                    g = 2 * k + slot
                    act.wait_ge(s["y"], done(g - 1))
                    act.wait_ge(s["gate_rows"], done(g))
                    act.activation(gate_t[:, :], bank[0][0:NE + 1, :], ACT.Copy).then_inc(s["gate_t"], 1)

                def keep_second(k, slot):
                    g = 2 * k + slot
                    for i in range(3):
                        act.wait_ge(made2, 3 * g + i + 1)
                        act.activation(act2[:, i, :], bank[(3, 4, 0)[i]][:, :], ACT.Relu, bias=m.b2[:, i:i + 1]).then_inc(kept2, 1)

                run(act, pairs, [(keep_first_a, 0), (exp_logits, 0), (keep_first_b, 0), (exp_gates, 0), (keep_first_c, 0),
                                 (keep_rows, 1), (keep_gates, 0), (keep_second, 0)])


_INS = ["x", "src", "dst", "L0_gnn_Wl1", "L0_gnn_Wr1", "L0_gnn_att1", "L0_gnn_b1", "L0_gnn_Wl2", "L0_gnn_Wr2",
        "L0_gnn_att2", "L0_gnn_b2", "L0_ffn_sW1", "L0_ffn_sb1", "L0_ffn_sW2", "L0_ffn_sb2", "L0_ffn_sW3",
        "L0_ffn_sb3", "L0_ffn_eW1", "L0_ffn_eb1", "L0_ffn_eW2", "L0_ffn_eb2", "L0_ffn_eW3", "L0_ffn_eb3",
        "L0_ffn_gW", "L0_ffn_gb"]


def gat_ffn_program(nc, inputs, out):
    a = inputs
    nodes, edges = a["x"].shape[0], a["src"].shape[0]
    m = Shared(nodes, edges)
    h1 = nc.dram_tensor("hidden", (nodes, F), F32, kind="Internal").ap()
    x1 = nc.dram_tensor("attended", (nodes, F), F32, kind="Internal").ap()
    with ExitStack() as ctx:
        setup(nc, m, a, ctx)
        dense(nc, m, 0, a["x"], None, h1)
        attend_edges(nc, m, 0, a["x"], None, h1)
        dense(nc, m, 1, h1, a["x"], x1)
        attend_edges(nc, m, 1, h1, a["x"], x1)
        ffn(nc, m, x1, out)


def kernel(**inputs):
    import concourse.bacc as bacc
    import numpy as np
    from concourse.bass_utils import run_bass_kernel_spmd

    nc = bacc.Bacc("TRN2", target_bir_lowering=False, num_devices=1)
    arrays, aps = {}, {}
    for name in _INS:
        v = np.ascontiguousarray(inputs[name])
        arrays[f"in_{name}_dram"] = v
        aps[name] = nc.dram_tensor(f"in_{name}_dram", v.shape, mybir.dt.from_np(v.dtype), kind="ExternalInput").ap()
    out = nc.dram_tensor("out_0_dram", inputs["x"].shape, F32, kind="ExternalOutput").ap()
    gat_ffn_program(nc, aps, out)
    result = run_bass_kernel_spmd(nc, [arrays], core_ids=[0])
    return result.results[0]["out_0_dram"]
```

```python
from contextlib import ExitStack

import concourse.bass as bass
from concourse import mybir

F32 = mybir.dt.float32
I32 = mybir.dt.int32
BF16 = mybir.dt.bfloat16
F16 = mybir.dt.float16
ALU = mybir.AluOpType
ACT = mybir.ActivationFunctionType
AXX = mybir.AxisListType.X

P = 128
F = 256
KC = F // P
J = 4
G = P * J
H, C = 4, 64
SLOTS = 2
EDGE_SLOTS = 4
BIG = 1e30
LN_EPS = 1e-5
DEN_EPS = 1e-16
SLOPE = 0.2
NE = 4
TOPK = 2
EH1, EH2 = 128, 64
NC1 = 2 + NE
GR = 2 * (NE + 1)
UP = 64.0


class Shared:

    def __init__(self, nodes, edges):
        self.nodes, self.edges = nodes, edges
        self.groups, self.tiles = -(-nodes // G), -(-edges // P)


def run(eng, groups, slots, steps):
    aheads = [ahead for _, ahead in steps]
    first = 1 - min(0, *aheads) // slots
    end = (groups - 1 - max(0, *aheads)) // slots

    def at(k, slot):
        for step, ahead in steps:
            step(k + (slot + ahead) // slots, (slot + ahead) % slots)

    def apart(g):
        for step, ahead in steps:
            if 0 <= g + ahead < groups:
                step((g + ahead) // slots, (g + ahead) % slots)

    for g in range(-max(aheads), slots * first):
        apart(g)
    assert first < end
    with eng.Fori(first, end) as k:
        for slot in range(slots):
            at(k, slot)
    for g in range(slots * end, groups - min(0, *aheads)):
        apart(g)


def done(g):
    return g + EDGE_SLOTS


def start_counts(nc, semaphores, counts):
    with nc.Block() as block:
        @block.sync
        def _(sp):
            for semaphore in semaphores:
                sp.sem_clear(semaphore)
            for count in counts:
                sp.sem_inc(count, EDGE_SLOTS - 1)


def wait_apart(eng, m, semaphore, value):
    eng.wait_ge(semaphore, value)
    eng.sem_inc(m.passed, 1)


def group_rows(n, g, groups):
    return n - G if isinstance(g, int) and g == groups - 1 else g * G


def last_group(m, g):
    return isinstance(g, int) and g == m.groups - 1


def nodes_of(dram, start):
    return dram[bass.ds(start, G), :].rearrange("(p j) f -> p j f", j=J)


def setup(nc, m, a, ctx):

    def sb(name, shape, dt=F32):
        return ctx.enter_context(nc.sbuf_tensor(name, shape, dt))

    nt = m.tiles
    m.ident = sb("ident", [P, P])
    m.minus_half = sb("minus_half", [P, 2 * J])
    m.ln_eps = sb("ln_eps", [P, 2 * J])
    m.last_row_ones = sb("last_row_ones", [P, P])
    m.w_gat = [sb(f"w_gat{i}", [P, KC, 2 * F]) for i in range(2)]
    m.att_cols = [sb(f"att_cols{i}", [P, KC, H]) for i in range(2)]
    m.ident_b = sb("ident_b", [P, P], BF16)
    m.b_gat = [sb(f"b_gat{i}", [P, F]) for i in range(2)]
    m.w1 = sb("w1", [P, KC, NC1 * P])
    m.b1 = sb("b1", [P, NC1])
    m.sw2 = sb("sw2", [P, KC, P])
    m.ew2 = sb("ew2", [P, NE, EH2])
    m.b2 = sb("b2", [P, 3])
    m.sw3 = sb("sw3", [P, F])
    m.ew3 = sb("ew3", [P, 2, F])
    m.b3 = sb("b3", [GR, F])
    m.gw = sb("gw", [P, KC, NE])
    m.gb = sb("gb", [P, NE])
    m.tie = sb("tie", [P, NE, NE])
    m.over_features = sb("over_features", [GR, 2, P])
    m.dst_row = sb("dst_row", [P, 1 + nt * P], I32)
    m.src_col = sb("src_col", [P, nt], I32)
    m.dst_col = sb("dst_col", [P, nt], I32)
    m.put_col = sb("put_col", [P, nt], I32)
    m.dst_colf = sb("dst_colf", [P, nt])
    m.carry_pen = sb("carry_pen", [P, nt])
    m.scr_rows = sb("scr_rows", [nt, 3, P], I32)
    m.scr_rowsf = sb("scr_rowsf", [nt, 3, P])
    m.scr_cols = sb("scr_cols", [P, 3, nt])
    m.scr_a = sb("scr_a", [P, nt])

    loaded = nc.alloc_semaphore("setup_loaded")
    idx_loaded = nc.alloc_semaphore("setup_idx_loaded")
    cleared = nc.alloc_semaphore("setup_cleared")
    m.passed = nc.alloc_semaphore("passed")
    ident_ready = nc.alloc_semaphore("setup_ident_ready")
    rows_ready = nc.alloc_semaphore("setup_rows_ready")
    cols_ready = nc.alloc_semaphore("setup_cols_ready")
    step = nc.alloc_semaphore("setup_step")
    full, tail = m.edges // P, m.edges % P
    onto_zeros = []
    plain = [
        (m.w_gat[i][:, :, s * F:(s + 1) * F], w.rearrange("(c p) n -> p c n", p=P))
        for i in range(2) for s, w in enumerate((a[f"L0_gnn_Wl{i + 1}"], a[f"L0_gnn_Wr{i + 1}"]))
    ]
    for i in range(2):
        plain.append((m.b_gat[i][:, :], a[f"L0_gnn_b{i + 1}"].partition_broadcast(P)))
    plain += [
        (m.w1[:, :, 0:2 * P], a["L0_ffn_sW1"].rearrange("(c p) n -> p c n", p=P)),
        (m.sw2[:, :, :], a["L0_ffn_sW2"].rearrange("(c p) n -> p c n", p=P)),
        (m.ew2[:, :, :], a["L0_ffn_eW2"].rearrange("e p n -> p e n")),
        (m.sw3[:, :], a["L0_ffn_sW3"]),
        (m.b3[0:NE, :], a["L0_ffn_eb3"]),
        (m.b3[NE:NE + 1, :], a["L0_ffn_sb3"].partition_broadcast(1)),
        (m.b3[NE + 1:GR - 1, :], a["L0_ffn_eb3"]),
        (m.b3[GR - 1:GR, :], a["L0_ffn_sb3"].partition_broadcast(1)),
        (m.gw[:, :, :], a["L0_ffn_gW"].rearrange("(c p) n -> p c n", p=P)),
        (m.gb[:, :], a["L0_ffn_gb"].partition_broadcast(P)),
        (m.b1[:, 0:2], a["L0_ffn_sb1"].rearrange("(c p) -> p c", p=P)),
        (m.b1[:, 2:NC1], a["L0_ffn_eb1"].rearrange("e p -> p e")),
        (m.b2[:, 0:1], a["L0_ffn_sb2"].rearrange("(c p) -> p c", p=P)),
    ]
    for e in range(NE):
        plain.append((m.w1[:, :, (2 + e) * P:(3 + e) * P], a["L0_ffn_eW1"][e].rearrange("(c p) n -> p c n", p=P)))
        half = slice((e % 2) * EH2, (e % 2 + 1) * EH2)
        plain.append((m.ew3[half, e // 2, :], a["L0_ffn_eW3"][e]))
        plain.append((m.b2[half, 1 + e // 2:2 + e // 2], a["L0_ffn_eb2"][e:e + 1, :].rearrange("e p -> p e")))
    for h in range(H):
        part = slice(h % 2 * C, (h % 2 + 1) * C)
        for i in range(2):
            onto_zeros.append((m.att_cols[i][part, h // 2, h:h + 1], a[f"L0_gnn_att{i + 1}"][h:h + 1, :].rearrange("h c -> c h")))
    src, dst = a["src"], a["dst"]
    indexes = [
        (m.scr_rows[0:full, 0, :], src[0:full * P].rearrange("(t p) -> t p", p=P)),
        (m.scr_rows[0:full, 1, :], dst[0:full * P].rearrange("(t p) -> t p", p=P)),
        (m.scr_rows[0:full, 2, :], dst[1:full * P + 1].rearrange("(t p) -> t p", p=P)),
        (m.scr_rows[full:full + 1, 0, 0:tail], src[full * P:m.edges].partition_broadcast(1)),
        (m.scr_rows[full:full + 1, 1, 0:tail], dst[full * P:m.edges].partition_broadcast(1)),
        (m.scr_rows[full:full + 1, 2, 0:tail - 1], dst[full * P + 1:m.edges].partition_broadcast(1)),
        (m.dst_row[:, 1:1 + m.edges], dst.partition_broadcast(P)),
    ]

    with nc.psum_tensor("ps_cols", [P, 3, nt], F32) as ps_cols, nc.Block() as block:
        @block.sync
        def _(sp):
            with nc.allow_non_contiguous_dma(reason="bias columns, once"):
                for out, in_ in plain:
                    sp.dma_start(out, in_).then_inc(loaded, 16)
            sp.wait_ge(cleared, 4)
            for out, in_ in indexes:
                sp.dma_start(out, in_).then_inc(idx_loaded, 16)
            with nc.allow_non_contiguous_dma(reason="attention vectors as columns, once"):
                for out, in_ in onto_zeros:
                    sp.dma_start(out, in_).then_inc(loaded, 16)
            sp.wait_ge(loaded, 16 * (len(plain) + len(onto_zeros)))

        @block.gpsimd
        def _(pool):
            pool.memset(m.ident[:, :], 0.0).then_inc(step, 1)
            pool.memset(m.last_row_ones[:, :], 0.0).then_inc(step, 1)
            pool.memset(m.tie[:, :, :], 1.0).then_inc(step, 1)
            pool.memset(m.over_features[:, :, :], 0.0).then_inc(step, 1)
            by_expert = m.over_features[:, :, :].rearrange("e q (i f) -> e q i f", i=2)
            for i, base in enumerate((0, -(NE + 1))):
                pool.wait_ge(step, 4 + i)
                pool.affine_select(out=by_expert, in_=by_expert, compare_op=ALU.not_equal, fill=1.0, base=base,
                                   pattern=[[-2, 2], [-1, 2], [0, EH2]], channel_multiplier=1).then_inc(step, 1)
            pool.affine_select(out=m.ident[:, :], in_=m.ident[:, :], compare_op=ALU.not_equal, fill=1.0, base=0,
                               pattern=[[-1, P]], channel_multiplier=1).then_inc(ident_ready, 1)
            pool.affine_select(out=m.last_row_ones[:, :], in_=m.last_row_ones[:, :], compare_op=ALU.not_equal,
                               fill=1.0, base=1 - P, pattern=[[0, P]], channel_multiplier=1).then_inc(step, 1)
            pool.affine_select(out=m.tie[:, :, :], in_=m.tie[:, :, :], compare_op=ALU.is_gt, fill=0.0, base=0,
                               pattern=[[1, NE], [-1, NE]], channel_multiplier=0).then_inc(step, 1)
            pool.wait_ge(step, 8)

        @block.vector
        def _(dve):
            dve.memset(m.scr_rows[:, :, :], -1).then_inc(cleared, 1)
            dve.memset(m.dst_row[:, :], -1).then_inc(cleared, 1)
            for i in range(2):
                dve.memset(m.att_cols[i][:, :, :], 0.0).then_inc(cleared, 1)
            dve.memset(m.ln_eps[:, :], LN_EPS)
            dve.memset(m.minus_half[:, :], -0.5).then_inc(rows_ready, 1)
            dve.wait_ge(ident_ready, 1)
            dve.tensor_copy(m.ident_b[:, :], m.ident[:, :])
            dve.wait_ge(idx_loaded, 16 * len(indexes))
            dve.tensor_copy(m.scr_rowsf[:, :, :], m.scr_rows[:, :, :]).then_inc(rows_ready, 1)
            dve.wait_ge(cols_ready, 1)
            dve.tensor_copy(m.scr_cols[:, :, :], ps_cols[:, :, :]).then_inc(cols_ready, 1)
            dve.wait_ge(cols_ready, 2)
            dve.tensor_copy(m.src_col[:, :], m.scr_cols[:, 0, :]).then_inc(cols_ready, 1)
            dve.tensor_copy(m.dst_col[:, :], m.scr_cols[:, 1, :]).then_inc(cols_ready, 1)
            dve.tensor_copy(m.dst_colf[:, :], m.scr_cols[:, 1, :]).then_inc(cols_ready, 1)
            dve.tensor_tensor(m.scr_a[:, :], m.scr_cols[:, 1, :], m.scr_cols[:, 2, :], ALU.is_equal).then_inc(cols_ready, 1)
            before = m.dst_row[:, 0:nt * P].rearrange("p (t e) -> p t e", e=P)[:, :, 0]
            dve.tensor_tensor(m.carry_pen[:, :], m.scr_cols[:, 1, :], before, ALU.is_equal).then_inc(cols_ready, 1)
            dve.wait_ge(cols_ready, 7)
            dve.scalar_tensor_tensor(out=m.put_col[:, :], in0=m.scr_a[:, :], scalar=float(m.nodes), in1=m.scr_cols[:, 1, :],
                                     op0=ALU.mult, op1=ALU.add).then_inc(cols_ready, 1)
            dve.tensor_scalar(m.carry_pen[:, :], m.carry_pen[:, :], -1.0, BIG, ALU.add, ALU.mult).then_inc(cols_ready, 1)
            dve.wait_ge(cols_ready, 9)

        @block.tensor
        def _(pe):
            pe.wait_ge(ident_ready, 1)
            pe.wait_ge(rows_ready, 2)
            for i in range(3):
                last = pe.transpose(ps_cols[:, i, :], m.scr_rowsf[:, i, :], m.ident[0:nt, 0:nt])
            last.then_inc(cols_ready, 1)


def dense(nc, m, layer, feed, resid, out, rows_out):
    pairs = m.groups // 2
    name = f"d{layer}_"
    norm = layer == 0
    with ExitStack() as ctx:
        def sb(n, shape, dt=F32):
            return ctx.enter_context(nc.sbuf_tensor(name + n, shape, dt))

        semaphores = []

        def sem(n):
            semaphores.append(ctx.enter_context(nc.semaphore(name + n)))
            return semaphores[-1]

        x = sb("x", [P, SLOTS, J, F])
        side = sb("side", [P, SLOTS, J, F])
        stats = sb("stats", [P, SLOTS, J, 6])
        moments = sb("moments", [P, SLOTS, J, 2])
        var = sb("var", [P, SLOTS, J])
        rstd = sb("rstd", [P, SLOTS, J])
        xt = sb("xt", [P, SLOTS, KC, G])
        z = sb("z", [P, SLOTS, J, F])
        low = sb("low", [P, SLOTS, J, F])
        res = sb("res", [P, SLOTS, J, F])
        ps_t = [ctx.enter_context(nc.psum_tensor(f"{name}ps_t{i}", [P, KC, G], F32)) for i in range(SLOTS)]
        ps_o = [ctx.enter_context(nc.psum_tensor(f"{name}ps_o{i}", [P, J, F], F32)) for i in range(SLOTS)]

        x_loaded = [sem(f"x_loaded{i}") for i in range(SLOTS)]
        r_loaded = [sem(f"r_loaded{i}") for i in range(SLOTS)]
        stored = [sem(f"stored{i}") for i in range(SLOTS)]
        rows_stored = [sem(f"rows_stored{i}") for i in range(SLOTS)]
        counts = [sem(n) for n in ("stats_ready", "moments_ready", "var_ready", "rstd_ready", "rows_ready", "turned",
                                   "xt_ready", "product_ready", "z_ready", "low_ready", "exp_ready", "res_ready")]
        (stats_ready, moments_ready, var_ready, rstd_ready, rows_ready, turned,
         xt_ready, product_ready, z_ready, low_ready, exp_ready, res_ready) = counts
        rows_of = side if norm else x
        start_counts(nc, semaphores, counts)

        with nc.Block() as block:
            @block.sync
            def _(sp):
                def load(k, slot):
                    g = 2 * k + slot
                    start = group_rows(m.nodes, g, m.groups)
                    sp.wait_ge(rows_ready if norm else turned, done(g - SLOTS))
                    sp.dma_start(x[:, slot, :, :], nodes_of(feed, start)).then_inc(x_loaded[slot], 16)
                    if not norm:
                        sp.wait_ge(z_ready, done(g - SLOTS))
                        sp.dma_start(side[:, slot, :, :], nodes_of(resid, start)).then_inc(r_loaded[slot], 16)

                def store_rows(k, slot):
                    g = 2 * k + slot
                    sp.wait_ge(rows_ready, done(g))
                    if last_group(m, g):
                        sp.wait_ge(rows_stored[0], 16 * pairs)
                    sp.dma_start(nodes_of(rows_out, group_rows(m.nodes, g, m.groups)), side[:, slot, :, :]).then_inc(rows_stored[slot], 16)

                if norm:
                    run(sp, m.groups, SLOTS, [(load, 2), (store_rows, 0)])
                    for slot in range(SLOTS):
                        sp.wait_ge(rows_stored[slot], 16 * pairs)
                else:
                    run(sp, m.groups, SLOTS, [(load, 0)])

            @block.vector
            def _(dve):
                def statistics(k, slot):
                    g = 2 * k + slot
                    dve.wait_ge(x_loaded[slot], 16 * k + 16)
                    for j in range(J):
                        last = dve.bn_stats(stats[:, slot, j, :], x[:, slot, j, :])
                    last.then_inc(stats_ready, 1)
                    dve.wait_ge(rstd_ready, done(g - SLOTS))
                    wait_apart(dve, m, stats_ready, done(g))
                    for j in range(J):
                        last = dve.bn_aggr(moments[:, slot, j, :], stats[:, slot, j, :])
                    last.then_inc(moments_ready, 1)

                def normalise(k, slot):
                    g = 2 * k + slot
                    dve.wait_ge(rstd_ready, done(g))
                    dve.wait_ge(turned, done(g - SLOTS))
                    dve.wait_ge(rows_stored[slot], 16 * k)
                    for j in range(J):
                        last = dve.tensor_scalar(side[:, slot, j, :], x[:, slot, j, :], moments[:, slot, j, 0:1],
                                                 rstd[:, slot, j:j + 1], ALU.subtract, ALU.mult)
                    last.then_inc(rows_ready, 1)

                def biased(k, slot):
                    g = 2 * k + slot
                    bias = m.b_gat[layer][:, :].unsqueeze(1).broadcast_to([P, J, F])
                    dve.wait_ge(res_ready, done(g - SLOTS))
                    dve.wait_ge(product_ready, done(g))
                    dve.tensor_tensor(z[:, slot, :, :], ps_o[slot][:, :, :], bias, ALU.add).then_inc(z_ready, 1)

                def elu(k, slot):
                    g = 2 * k + slot
                    dve.wait_ge(stored[slot], 16 * k)
                    dve.wait_ge(exp_ready, done(g))
                    dve.scalar_tensor_tensor(out=res[:, slot, :, :], in0=ps_o[slot][:, :, :], scalar=-1.0,
                                             in1=z[:, slot, :, :], op0=ALU.add, op1=ALU.max).then_inc(res_ready, 1)

                def sum_of_product(k, slot):
                    g = 2 * k + slot
                    dve.wait_ge(product_ready, done(g))
                    dve.wait_ge(z_ready, done(g))
                    dve.wait_ge(stored[slot], 16 * k)
                    dve.tensor_tensor(res[:, slot, :, :], ps_o[slot][:, :, :], z[:, slot, :, :], ALU.add).then_inc(res_ready, 1)

                if norm:
                    run(dve, m.groups, SLOTS, [(biased, 0), (statistics, 3), (elu, 0), (normalise, 3)])
                else:
                    run(dve, m.groups, SLOTS, [(sum_of_product, 0)])

            @block.gpsimd
            def _(pool):
                def scales(k, slot):
                    g = 2 * k + slot
                    pool.wait_ge(moments_ready, done(g))
                    pool.tensor_tensor(var[:, slot, :], moments[:, slot, :, 1], m.ln_eps[:, 0:J], ALU.add).then_inc(var_ready, 1)
                    pool.wait_ge(rows_ready, done(g - SLOTS))
                    pool.wait_ge(var_ready, done(g))
                    pool.tensor_tensor(rstd[:, slot, :], var[:, slot, :], m.minus_half[:, 0:J], ALU.pow).then_inc(rstd_ready, 1)

                def resid_bias(k, slot):
                    g = 2 * k + slot
                    pool.wait_ge(r_loaded[slot], 16 * k + 16)
                    pool.wait_ge(res_ready, done(g - SLOTS))
                    bias = m.b_gat[layer][:, :].unsqueeze(1).broadcast_to([P, J, F])
                    pool.tensor_tensor(z[:, slot, :, :], side[:, slot, :, :], bias, ALU.add).then_inc(z_ready, 1)

                run(pool, m.groups, SLOTS, [(scales if norm else resid_bias, 0)])

            @block.tensor
            def _(pe):
                def turn(k, slot):
                    g = 2 * k + slot
                    if norm:
                        pe.wait_ge(rows_ready, done(g))
                    else:
                        pe.wait_ge(x_loaded[slot], 16 * k + 16)
                    pe.wait_ge(xt_ready, done(g - SLOTS))
                    for c in range(KC):
                        for j in range(J):
                            last = pe.transpose(ps_t[slot][:, c, j * P:(j + 1) * P], rows_of[:, slot, j, c * P:(c + 1) * P], m.ident[:, :])
                    last.then_inc(turned, 1)

                def product(k, slot):
                    g = 2 * k + slot
                    pe.wait_ge(xt_ready, done(g))
                    pe.wait_ge(res_ready, done(g - SLOTS))
                    for j in range(J):
                        for c in range(KC):
                            last = pe.matmul(ps_o[slot][:, j, :], lhsT=xt[:, slot, c, j * P:(j + 1) * P],
                                             rhs=m.w_gat[layer][:, c, 0:F], start=c == 0, stop=c == KC - 1)
                    last.then_inc(product_ready, 1)

                run(pe, m.groups, SLOTS, [(product, 0), (turn, 2)])

            @block.scalar
            def _(act):
                def evacuate(k, slot):
                    g = 2 * k + slot
                    act.wait_ge(turned, done(g))
                    act.wait_ge(product_ready, done(g - SLOTS))
                    act.activation(xt[:, slot, :, :], ps_t[slot][:, :, :], ACT.Copy).then_inc(xt_ready, 1)

                def store(k, slot):
                    g = 2 * k + slot
                    act.wait_ge(res_ready, done(g))
                    if last_group(m, g):
                        act.wait_ge(stored[0], 16 * pairs)
                    act.dma_start(nodes_of(out, group_rows(m.nodes, g, m.groups)), res[:, slot, :, :]).then_inc(stored[slot], 16)

                def exps(k, slot):
                    g = 2 * k + slot
                    act.wait_ge(exp_ready, done(g - SLOTS))
                    act.wait_ge(z_ready, done(g))
                    act.activation(low[:, slot, :, :], z[:, slot, :, :], ACT.Relu, scale=-1.0).then_inc(low_ready, 1)
                    act.wait_ge(low_ready, done(g))
                    act.activation(ps_o[slot][:, :, :], low[:, slot, :, :], ACT.Exp, scale=-1.0).then_inc(exp_ready, 1)

                if norm:
                    run(act, m.groups, SLOTS, [(exps, 0), (evacuate, 3), (store, 0)])
                else:
                    run(act, m.groups, SLOTS, [(evacuate, 2), (store, 0)])
                for slot in range(SLOTS):
                    act.wait_ge(stored[slot], 16 * pairs)


def attend_edges(nc, m, layer, feed, resid, out):
    pairs = m.tiles // 2
    name = f"e{layer}_"
    norm = layer == 0
    W = H * (C + 1)
    with ExitStack() as ctx:
        def sb(n, shape, dt=F32):
            return ctx.enter_context(nc.sbuf_tensor(name + n, shape, dt))

        def ps(n, shape):
            return ctx.enter_context(nc.psum_tensor(name + n, shape, F32))

        semaphores = []

        def sem(n):
            semaphores.append(ctx.enter_context(nc.semaphore(name + n)))
            return semaphores[-1]

        def heads(ap):
            return ap.unsqueeze(2).broadcast_to([ap.shape[0], H, C])

        src_idx = sb("src_idx", [P, EDGE_SLOTS, 1], I32)
        dst_idx = sb("dst_idx", [P, EDGE_SLOTS, 1], I32)
        res_idx = sb("res_idx", [P, EDGE_SLOTS, 1], I32)
        put_idx = sb("put_idx", [P, EDGE_SLOTS, 1], I32)
        x = sb("x", [P, EDGE_SLOTS, 2, F])
        resid_rows = sb("resid_rows", [P, EDGE_SLOTS, F])
        xt = sb("xt", [P, EDGE_SLOTS, 2, KC, P])
        rows = sb("rows", [P, EDGE_SLOTS, 3, F])
        pre = sb("pre", [P, 2, F])
        leaky = sb("leaky", [P, 2, KC, P])
        leaky_t = sb("leaky_t", [P, EDGE_SLOTS, 2, KC, P])
        logits = sb("logits", [P, EDGE_SLOTS, 2 * H])
        same = sb("same", [P, EDGE_SLOTS, P])
        pen = sb("pen", [P, EDGE_SLOTS, P], BF16)
        tile_max = sb("tile_max", [P, EDGE_SLOTS, H])
        loop_max = sb("loop_max", [P, H])
        arg = sb("arg", [P, 4 * H])
        ex = sb("ex", [P, EDGE_SLOTS, 4 * H])
        v = sb("v", [P, H, C + 1])
        carried = sb("carried", [P, H, C + 1])
        state = sb("state", [P, EDGE_SLOTS, W + H])
        den = sb("den", [P, 2, H])
        coef = sb("coef", [P, EDGE_SLOTS, 2 * H])
        loop_part = sb("loop_part", [P, EDGE_SLOTS, F])
        sum_part = sb("sum_part", [P, F])
        both = sb("both", [P, EDGE_SLOTS, F])
        z = sb("z", [P, EDGE_SLOTS, F])
        low = sb("low", [P, EDGE_SLOTS, F])
        res = sb("res", [P, EDGE_SLOTS, F]) if norm else z
        ps_t = ps("ps_t", [P, 2, KC, P])
        ps_m = ps("ps_m", [P, 4, F])
        ps_x = ps("ps_x", [P, 2, KC, P])
        ps_l = ps("ps_l", [P, 2 * H])
        ps_s = ps("ps_s", [P, H, P])
        ps_c = ps("ps_c", [P, W + H])
        ps_n = ps("ps_n", [P, W])

        gathered = [[sem(f"gathered_{w}{i}") for i in range(EDGE_SLOTS)] for w in ("src", "dst", "resid")]
        scattered = [sem(f"scattered{i}") for i in range(EDGE_SLOTS)]
        names = ("idx", "turned", "xt", "product", "projected", "pre", "leaky",
                 "leaky_turned", "leaky_t", "logit_product", "logits", "spread", "same", "pen", "tile_max", "carry", "max", "arg0", "arg", "ex",
                 "v", "carried", "sums", "state", "den0", "den1", "den2", "coef", "loop_part", "sum_part", "both", "z",
                 "low", "exp", "res", "put", "resid_idx", "zb")
        s = {n: sem(n) for n in names}
        init = sem("init")

        def size(t):
            return m.edges - t * P if isinstance(t, int) and t == m.tiles - 1 else P

        start_counts(nc, semaphores, s.values())

        with nc.Block() as block:
            @block.gpsimd
            def _(pool):
                def gather(k, slot):
                    t = EDGE_SLOTS * k + slot
                    p = size(t)
                    wait_apart(pool, m, s["turned"], done(t - EDGE_SLOTS))
                    pool.tensor_copy(src_idx[:, slot, :], m.src_col[:, bass.ds(t, 1)])
                    pool.tensor_copy(dst_idx[:, slot, :], m.dst_col[:, bass.ds(t, 1)]).then_inc(s["idx"], 1)
                    wait_apart(pool, m, s["idx"], done(t))
                    for i, idx in ((0, src_idx), (1, dst_idx)):
                        pool.indirect_dma_start(out=x[0:p, slot, i, :], out_offset=None, in_=feed[:, :],
                                                in_offset=bass.IndirectOffsetOnAxis(ap=idx[0:p, slot, :], axis=0)
                                                ).then_inc(gathered[i][slot], 16)

                def gather_resid(k, slot):
                    t = EDGE_SLOTS * k + slot
                    p = size(t)
                    wait_apart(pool, m, s["z"], done(t - EDGE_SLOTS))
                    pool.tensor_copy(res_idx[:, slot, :], m.dst_col[:, bass.ds(t, 1)]).then_inc(s["resid_idx"], 1)
                    wait_apart(pool, m, s["resid_idx"], done(t))
                    pool.indirect_dma_start(out=resid_rows[0:p, slot, :], out_offset=None, in_=resid[:, :],
                                            in_offset=bass.IndirectOffsetOnAxis(ap=res_idx[0:p, slot, :], axis=0)
                                            ).then_inc(gathered[2][slot], 16)

                def combine(k, slot):
                    t = EDGE_SLOTS * k + slot
                    p = size(t)
                    pool.wait_ge(s["z"], done(t - EDGE_SLOTS))
                    pool.wait_ge(s["coef"], done(t))
                    sums = state[0:p, slot, 0:W].rearrange("p (h c) -> p h c", h=H)[:, :, 0:C]
                    pool.tensor_tensor(sum_part[0:p, :].rearrange("p (h c) -> p h c", h=H), sums,
                                       heads(coef[0:p, slot, 0:H]), ALU.mult).then_inc(s["sum_part"], 1)
                    pool.wait_ge(s["loop_part"], done(t))
                    pool.wait_ge(s["sum_part"], done(t))
                    pool.tensor_tensor(both[0:p, slot, :], sum_part[0:p, :], loop_part[0:p, slot, :], ALU.add).then_inc(s["both"], 1)
                    if norm:
                        pool.wait_ge(s["res"], done(t - EDGE_SLOTS))
                        pool.wait_ge(s["both"], done(t))
                        pool.tensor_tensor(z[0:p, slot, :], both[0:p, slot, :], m.b_gat[layer][0:p, :], ALU.add).then_inc(s["z"], 1)

                def scatter(k, slot):
                    t = EDGE_SLOTS * k + slot
                    p = size(t)
                    wait_apart(pool, m, scattered[slot], 16 * k)
                    pool.tensor_copy(put_idx[:, slot, :], m.put_col[:, bass.ds(t, 1)]).then_inc(s["put"], 1)
                    pool.wait_ge(s["res"] if norm else s["z"], done(t))
                    wait_apart(pool, m, s["put"], done(t))
                    pool.indirect_dma_start(out=out[:, :], out_offset=bass.IndirectOffsetOnAxis(ap=put_idx[0:p, slot, :], axis=0),
                                            in_=res[0:p, slot, :], in_offset=None, bounds_check=m.nodes - 1,
                                            oob_is_err=False).then_inc(scattered[slot], 16)

                if norm:
                    run(pool, m.tiles, EDGE_SLOTS, [(gather, 6), (scatter, -3), (combine, 0)])
                else:
                    run(pool, m.tiles, EDGE_SLOTS, [(gather, 6), (scatter, -2), (gather_resid, 1), (combine, 0)])
                for slot in range(EDGE_SLOTS):
                    pool.wait_ge(scattered[slot], 16 * len(range(slot, m.tiles, EDGE_SLOTS)))

            @block.vector
            def _(dve):
                def maxima(k, slot):
                    t = EDGE_SLOTS * k + slot
                    p = size(t)
                    top = state[0:p, slot, W:W + H]
                    dve.wait_ge(s["carry"], done(t))
                    dve.wait_ge(s["tile_max"], done(t))
                    pen_t = m.carry_pen[0:p, bass.ds(t, 1)]
                    dve.scalar_tensor_tensor(out=top, in0=ps_c[0:p, W:W + H], scalar=pen_t, in1=tile_max[0:p, slot, :],
                                             op0=ALU.add, op1=ALU.max).then_inc(s["max"], 1)
                    dve.wait_ge(s["ex"], done(t - 1))
                    dve.wait_ge(s["max"], done(t))
                    dve.tensor_tensor(loop_max[0:p, :], top, logits[0:p, slot, H:2 * H], ALU.max).then_inc(s["arg0"], 1)
                    dve.tensor_tensor(arg[0:p, 0:H], logits[0:p, slot, 0:H], top, ALU.subtract)
                    dve.scalar_tensor_tensor(out=arg[0:p, H:2 * H], in0=ps_c[0:p, W:W + H], scalar=pen_t, in1=top,
                                             op0=ALU.add, op1=ALU.subtract)
                    dve.wait_ge(s["arg0"], done(t))
                    dve.tensor_tensor(arg[0:p, 2 * H:3 * H], top, loop_max[0:p, :], ALU.subtract)
                    dve.tensor_tensor(arg[0:p, 3 * H:4 * H], logits[0:p, slot, H:2 * H], loop_max[0:p, :],
                                      ALU.subtract).then_inc(s["arg"], 1)

                def pre_activations(k, slot):
                    t = EDGE_SLOTS * k + slot
                    p = size(t)
                    dve.wait_ge(s["leaky"], done(t - 1))
                    dve.wait_ge(s["projected"], done(t))
                    right = rows[0:p, slot, 2, :].unsqueeze(1).broadcast_to([p, 2, F])
                    dve.tensor_tensor(pre[0:p, :, :], rows[0:p, slot, 0:2, :], right, ALU.add).then_inc(s["pre"], 1)

                def weigh(k, slot):
                    t = EDGE_SLOTS * k + slot
                    p = size(t)
                    dve.wait_ge(s["sums"], done(t - 1))
                    dve.wait_ge(s["ex"], done(t))
                    dve.tensor_tensor(v[0:p, :, 0:C], rows[0:p, slot, 0, :].rearrange("p (h c) -> p h c", h=H),
                                      heads(ex[0:p, slot, 0:H]), ALU.mult)
                    dve.tensor_copy(v[0:p, :, C], ex[0:p, slot, 0:H]).then_inc(s["v"], 1)
                    dve.wait_ge(s["state"], done(t - 1))
                    dve.tensor_tensor(carried[0:p, :, :], ps_c[0:p, 0:W].rearrange("p (h c) -> p h c", h=H),
                                      ex[0:p, slot, H:2 * H].unsqueeze(2).broadcast_to([p, H, C + 1]), ALU.mult
                                      ).then_inc(s["carried"], 1)

                def leaky_rows(k, slot):
                    t = EDGE_SLOTS * k + slot
                    p = size(t)
                    dve.wait_ge(s["leaky_turned"], done(t - 1))
                    dve.wait_ge(s["pre"], done(t))
                    dve.scalar_tensor_tensor(out=leaky[0:p, :, :, :].rearrange("p i c f -> p (i c f)"),
                                             in0=pre[0:p, :, :].rearrange("p i f -> p (i f)"), scalar=SLOPE,
                                             in1=pre[0:p, :, :].rearrange("p i f -> p (i f)"), op0=ALU.mult,
                                             op1=ALU.max).then_inc(s["leaky"], 1)

                def keep_logits(k, slot):
                    t = EDGE_SLOTS * k + slot
                    p = size(t)
                    dve.wait_ge(s["arg"], done(t - EDGE_SLOTS))
                    dve.wait_ge(s["logit_product"], done(t))
                    dve.tensor_copy(logits[0:p, slot, :], ps_l[0:p, :]).then_inc(s["logits"], 1)

                def accumulate(k, slot):
                    t = EDGE_SLOTS * k + slot
                    p = size(t)
                    dve.wait_ge(s["both"], done(t - EDGE_SLOTS))
                    dve.wait_ge(s["carried"], done(t))
                    dve.wait_ge(s["sums"], done(t))
                    dve.tensor_tensor(state[0:p, slot, 0:W], ps_n[0:p, 0:W], carried[0:p, :, :].rearrange("p h c -> p (h c)"),
                                      ALU.add).then_inc(s["state"], 1)

                def coefficients(k, slot):
                    t = EDGE_SLOTS * k + slot
                    p = size(t)
                    dve.wait_ge(s["state"], done(t))
                    a, b = ex[0:p, slot, 2 * H:3 * H], ex[0:p, slot, 3 * H:4 * H]
                    dens = state[0:p, slot, 0:W].rearrange("p (h c) -> p h c", h=H)[:, :, C]
                    dve.wait_ge(s["coef"], done(t - 1))
                    dve.tensor_tensor(den[0:p, 0, :], dens, a, ALU.mult).then_inc(s["den0"], 1)
                    dve.wait_ge(s["den0"], done(t))
                    dve.scalar_tensor_tensor(out=den[0:p, 1, :], in0=den[0:p, 0, :], scalar=DEN_EPS, in1=b,
                                             op0=ALU.add, op1=ALU.add).then_inc(s["den1"], 1)
                    dve.wait_ge(s["den1"], done(t))
                    dve.reciprocal(den[0:p, 0, :], den[0:p, 1, :]).then_inc(s["den2"], 1)
                    dve.wait_ge(s["den2"], done(t))
                    dve.tensor_tensor(coef[0:p, slot, 0:H], a, den[0:p, 0, :], ALU.mult)
                    dve.tensor_tensor(coef[0:p, slot, H:2 * H], b, den[0:p, 0, :], ALU.mult).then_inc(s["coef"], 1)
                    dve.wait_ge(s["coef"], done(t))
                    dve.tensor_tensor(loop_part[0:p, slot, :].rearrange("p (h c) -> p h c", h=H),
                                      rows[0:p, slot, 1, :].rearrange("p (h c) -> p h c", h=H),
                                      heads(coef[0:p, slot, H:2 * H]), ALU.mult).then_inc(s["loop_part"], 1)

                def group(k, slot):
                    t = EDGE_SLOTS * k + slot
                    p = size(t)
                    dve.wait_ge(s["sums"], done(t - EDGE_SLOTS))
                    dve.tensor_scalar(same[0:p, slot, 0:p], m.dst_row[0:p, bass.ds(t * P + 1, p)], m.dst_colf[0:p, bass.ds(t, 1)],
                                      None, ALU.is_equal).then_inc(s["same"], 1)
                    dve.wait_ge(s["spread"], done(t - EDGE_SLOTS))
                    dve.wait_ge(s["same"], done(t))
                    dve.tensor_scalar(pen[0:p, slot, 0:p], same[0:p, slot, 0:p], -1.0, BIG, ALU.add, ALU.mult).then_inc(s["pen"], 1)

                def group_maxima(k, slot):
                    t = EDGE_SLOTS * k + slot
                    p = size(t)
                    dve.wait_ge(s["max"], done(t - EDGE_SLOTS))
                    dve.wait_ge(s["spread"], done(t))
                    dve.reduce_max(tile_max[0:p, slot, :], ps_s[0:p, :, 0:p],
                                   axis=AXX).then_inc(s["tile_max"], 1)

                def low_part(k, slot):
                    t = EDGE_SLOTS * k + slot
                    p = size(t)
                    dve.wait_ge(s["res"], done(t - EDGE_SLOTS))
                    dve.wait_ge(s["z"], done(t))
                    dve.tensor_scalar(low[0:p, slot, :], z[0:p, slot, :], 0.0, None, ALU.min).then_inc(s["low"], 1)

                def elu(k, slot):
                    t = EDGE_SLOTS * k + slot
                    p = size(t)
                    dve.wait_ge(scattered[slot], 16 * k)
                    dve.wait_ge(s["exp"], done(t))
                    dve.scalar_tensor_tensor(out=res[0:p, slot, :], in0=low[0:p, slot, :], scalar=-1.0, in1=z[0:p, slot, :],
                                             op0=ALU.add, op1=ALU.max).then_inc(s["res"], 1)

                def add_residual(k, slot):
                    t = EDGE_SLOTS * k + slot
                    p = size(t)
                    dve.wait_ge(s["both"], done(t))
                    dve.tensor_tensor(low[0:p, slot, :], both[0:p, slot, :], m.b_gat[layer][0:p, :], ALU.add).then_inc(s["zb"], 1)
                    dve.wait_ge(gathered[2][slot], 16 * k + 16)
                    dve.wait_ge(scattered[slot], 16 * k)
                    dve.wait_ge(s["zb"], done(t))
                    dve.tensor_tensor(z[0:p, slot, :], low[0:p, slot, :], resid_rows[0:p, slot, :], ALU.add).then_inc(s["z"], 1)

                dve.memset(state[:, EDGE_SLOTS - 1, :], 0.0).then_inc(init, 1)
                run(dve, m.tiles, EDGE_SLOTS,
                    [(maxima, 0), (pre_activations, 2), (weigh, 0), (leaky_rows, 2), (keep_logits, 1), (group, 2), (group_maxima, 1),
                     (accumulate, 0), (coefficients, 0)] + ([(low_part, -1), (elu, -2)] if norm else [(add_residual, -1)]))

            @block.tensor
            def _(pe):
                def carry(k, slot):
                    t = EDGE_SLOTS * k + slot
                    pe.wait_ge(init, 1)
                    pe.wait_ge(s["carried"], done(t - 1))
                    pe.wait_ge(s["state"], done(t - 1))
                    pe.matmul(ps_c[:, :], lhsT=m.last_row_ones[:, :], rhs=state[:, (slot - 1) % EDGE_SLOTS, :], start=True,
                              stop=True).then_inc(s["carry"], 1)

                def turn(k, slot):
                    t = EDGE_SLOTS * k + slot
                    p = size(t)
                    pe.wait_ge(s["xt"], done(t - 1))
                    for i in range(2):
                        pe.wait_ge(gathered[i][slot], 16 * k + 16)
                    for i in range(2):
                        for c in range(KC):
                            last = pe.transpose(ps_t[:, i, c, 0:p], x[0:p, slot, i, c * P:(c + 1) * P], m.ident[0:p, 0:p])
                    last.then_inc(s["turned"], 1)

                def product(k, slot):
                    t = EDGE_SLOTS * k + slot
                    p = size(t)
                    pe.wait_ge(s["projected"], done(t - 1))
                    pe.wait_ge(s["xt"], done(t))
                    for i, (first, last_) in enumerate(((1, 2), (2, 4))):
                        for c in range(KC):
                            last = pe.matmul(ps_m[0:p, first:last_, :], lhsT=xt[:, slot, i, c, 0:p],
                                             rhs=m.w_gat[layer][:, c, 0:(last_ - first) * F], start=c == 0, stop=c == KC - 1)
                    last.then_inc(s["product"], 1)

                def turn_leaky(k, slot):
                    t = EDGE_SLOTS * k + slot
                    p = size(t)
                    pe.wait_ge(s["leaky_t"], done(t - 1))
                    pe.wait_ge(s["leaky"], done(t))
                    for i in range(2):
                        for c in range(KC):
                            last = pe.transpose(ps_x[:, i, c, 0:p], leaky[0:p, i, c, :], m.ident[0:p, 0:p])
                    last.then_inc(s["leaky_turned"], 1)

                def score(k, slot):
                    t = EDGE_SLOTS * k + slot
                    p = size(t)
                    pe.wait_ge(s["logits"], done(t - 1))
                    pe.wait_ge(s["leaky_t"], done(t))
                    for i in range(2):
                        for c in range(KC):
                            last = pe.matmul(ps_l[0:p, i * H:(i + 1) * H], lhsT=leaky_t[:, slot, i, c, 0:p],
                                             rhs=m.att_cols[layer][:, c, :], start=c == 0, stop=c == KC - 1)
                    last.then_inc(s["logit_product"], 1)

                def spread(k, slot):
                    t = EDGE_SLOTS * k + slot
                    p = size(t)
                    pe.wait_ge(s["tile_max"], done(t - 1))
                    pe.wait_ge(s["pen"], done(t))
                    pe.wait_ge(s["leaky_t"], done(t))
                    pe.matmul(ps_s[0:p, :, 0:p], lhsT=m.ident_b[0:p, 0:p],
                              rhs=pen[0:p, slot, 0:p].unsqueeze(1).broadcast_to([p, H, p]),
                              start=True, stop=False, skip_group_check=True)
                    for h in range(H):
                        att = m.att_cols[layer][:, h // 2, h:h + 1].broadcast_to([P, p])
                        last = pe.matmul(ps_s[0:p, h, 0:p], lhsT=att, rhs=leaky_t[:, slot, 0, h // 2, 0:p],
                                         start=False, stop=h == H - 1, skip_group_check=True)
                    last.then_inc(s["spread"], 1)

                def sums(k, slot):
                    t = EDGE_SLOTS * k + slot
                    p = size(t)
                    pe.wait_ge(s["state"], done(t - 1))
                    pe.wait_ge(s["v"], done(t))
                    pe.matmul(ps_n[0:p, 0:W], lhsT=same[0:p, slot, 0:p], rhs=v[0:p, :, :].rearrange("p h c -> p (h c)"),
                              start=True, stop=True).then_inc(s["sums"], 1)

                run(pe, m.tiles, EDGE_SLOTS, [(spread, 1), (product, 3), (sums, 0), (turn_leaky, 2), (carry, 1), (turn, 4), (score, 2)])

            @block.scalar
            def _(act):
                def weights(k, slot):
                    t = EDGE_SLOTS * k + slot
                    p = size(t)
                    act.wait_ge(s["coef"], done(t - EDGE_SLOTS))
                    act.wait_ge(s["arg"], done(t))
                    act.activation(ex[0:p, slot, :], arg[0:p, :], ACT.Exp).then_inc(s["ex"], 1)

                def evacuate_leaky(k, slot):
                    t = EDGE_SLOTS * k + slot
                    p = size(t)
                    act.wait_ge(s["spread"], done(t - EDGE_SLOTS))
                    act.wait_ge(s["leaky_turned"], done(t))
                    act.activation(leaky_t[:, slot, :, :, 0:p], ps_x[:, :, :, 0:p], ACT.Copy).then_inc(s["leaky_t"], 1)

                def evacuate_rows(k, slot):
                    t = EDGE_SLOTS * k + slot
                    p = size(t)
                    act.wait_ge(s["product"], done(t - EDGE_SLOTS))
                    act.wait_ge(s["turned"], done(t))
                    act.activation(xt[:, slot, :, :, 0:p], ps_t[:, :, :, 0:p], ACT.Copy).then_inc(s["xt"], 1)

                def evacuate_product(k, slot):
                    t = EDGE_SLOTS * k + slot
                    p = size(t)
                    act.wait_ge(s["loop_part"], done(t - EDGE_SLOTS))
                    act.wait_ge(s["product"], done(t))
                    act.activation(rows[0:p, slot, :, :], ps_m[0:p, 1:4, :], ACT.Copy).then_inc(s["projected"], 1)

                def low_exp(k, slot):
                    t = EDGE_SLOTS * k + slot
                    p = size(t)
                    act.wait_ge(s["low"], done(t))
                    act.activation(low[0:p, slot, :], low[0:p, slot, :], ACT.Exp).then_inc(s["exp"], 1)

                run(act, m.tiles, EDGE_SLOTS, [(weights, 0), (evacuate_product, 3), (evacuate_leaky, 2), (evacuate_rows, 4)]
                    + [(low_exp, -1)] * norm)


def ffn(nc, m, feed, out):
    pairs = m.groups // 2
    name = "f_"
    with ExitStack() as ctx:
        def sb(n, shape, dt=F32):
            return ctx.enter_context(nc.sbuf_tensor(name + n, shape, dt))

        semaphores = []

        def sem(n):
            semaphores.append(ctx.enter_context(nc.semaphore(name + n)))
            return semaphores[-1]

        x = sb("x", [P, SLOTS, J, F])
        again = sb("again", [P, SLOTS, J, F])
        rows = sb("rows", [P, SLOTS, J, F])
        stats = sb("stats", [P, SLOTS, J, 6])
        moments = sb("moments", [P, SLOTS, J, 2])
        var = sb("var", [P, SLOTS, J])
        rstd = sb("rstd", [P, SLOTS, J])
        act1_f = sb("act1_f", [P, NC1, G])
        act2_f = sb("act2_f", [P, 3, G])
        gated_f = sb("gated_f", [P, 2, G])
        xt = [sb(f"xt{i}", [P, SLOTS, KC, G], F16) for i in range(2)]
        act1 = [sb(f"act1_{i}", [P, NC1, G], F16) for i in range(2)]
        act2 = [sb(f"act2_{i}", [P, 3, G], F16) for i in range(2)]
        gate_t = sb("gate_t", [GR, G], F16)
        over_features = sb("over_features", [GR, 2, P], F16)
        parts = {}
        for n, w in (("w1", m.w1), ("sw2", m.sw2), ("ew2", m.ew2), ("sw3", m.sw3), ("ew3", m.ew3), ("b3", m.b3), ("gw", m.gw)):
            parts[n] = [sb(f"{n}_{i}", list(w.shape), F16) for i in range(2)]
        weight_h = sb("weight_h", [P, J, NE], F16)
        weight_f = sb("weight_f", [P, J, NE])
        logits = sb("logits", [P, J, NE])
        top = sb("top", [P, J])
        over = sb("over", [P, J, NE])
        shifted = sb("shifted", [P, J, NE])
        exps = sb("exps", [P, J, NE])
        total = sb("total", [P, J])
        inverse = sb("inverse", [P, J])
        gates = sb("gates", [P, J, NE])
        greater = sb("greater", [P, J, NE, NE])
        equal = sb("equal", [P, J, NE, NE])
        rank = sb("rank", [P, J, NE])
        chosen = sb("chosen", [P, J, NE])
        weight = sb("weight", [P, J, GR])
        res = sb("res", [P, SLOTS, J, F])
        bank = [ctx.enter_context(nc.psum_tensor(f"{name}bank{i}", [P, G], F32)) for i in range(5)]
        ps_g = ctx.enter_context(nc.psum_tensor(f"{name}ps_g", [P, J, NE], F32))
        ps_y = ctx.enter_context(nc.psum_tensor(f"{name}ps_y", [P, J, F], F32))

        x_loaded = [sem(f"x_loaded{i}") for i in range(SLOTS)]
        again_loaded = [sem(f"again_loaded{i}") for i in range(SLOTS)]
        stored = [sem(f"stored{i}") for i in range(SLOTS)]
        s = {n: sem(n) for n in ("stats", "moments", "var", "rstd", "rows", "gate_product", "logits", "top", "shifted",
                                      "exps", "total", "inverse", "gates", "compared", "tied", "beaten", "rank", "chosen", "over",
                                      "exps2", "picked", "total2", "inverse2", "weight_f", "weight_h", "weight", "spread0", "spread1", "gate_rows",
                                      "gate_t", "gated0", "gated1", "high_g0", "high_g1", "gated", "y", "res")}
        turned, xt_kept = sem("turned"), sem("xt_kept")
        made1, kept1 = sem("made1"), sem("kept1")
        made2, kept2 = sem("made2"), sem("kept2")
        high1 = sem("high1")
        split_pool, split_dve = sem("split_pool"), sem("split_dve")
        xt_high = sem("xt_high")
        high2, split2 = sem("high2"), sem("split2")
        ones, halved = sem("ones"), sem("halved")
        start_counts(nc, semaphores, s.values())

        def over_experts(ap):
            return ap.unsqueeze(2).broadcast_to([P, J, NE])

        def all_of(w):
            return w[tuple(slice(None) for _ in w.shape)]

        with nc.Block() as block:
            @block.vector
            def _(dve):
                whole = ((m.w1, "w1"), (m.sw2, "sw2"), (m.ew2, "ew2"), (m.sw3, "sw3"), (m.ew3, "ew3"), (m.b3, "b3"), (m.gw, "gw"))
                for w, n in whole:
                    dve.tensor_scalar(all_of(parts[n][0]), all_of(w), UP, None, ALU.mult).then_inc(halved, 1)
                dve.tensor_copy(over_features[:, :, :], m.over_features[:, :, :])
                dve.wait_ge(halved, len(whole))
                for w, n in whole:
                    dve.scalar_tensor_tensor(out=all_of(parts[n][1]), in0=all_of(w), scalar=UP, in1=all_of(parts[n][0]),
                                             op0=ALU.mult, op1=ALU.subtract)

        with nc.Block() as block:
            @block.sync
            def _(sp):
                def load(k, slot):
                    g = 2 * k + slot
                    sp.wait_ge(s["rows"], done(g - SLOTS))
                    sp.dma_start(x[:, slot, :, :], nodes_of(feed, group_rows(m.nodes, g, m.groups))).then_inc(x_loaded[slot], 16)

                def load_again(k, slot):
                    g = 2 * k + slot
                    sp.wait_ge(s["res"], done(g - SLOTS))
                    sp.dma_start(again[:, slot, :, :], nodes_of(feed, group_rows(m.nodes, g, m.groups))).then_inc(again_loaded[slot], 16)

                def store(k, slot):
                    g = 2 * k + slot
                    sp.wait_ge(s["res"], done(g))
                    if last_group(m, g):
                        sp.wait_ge(stored[0], 16 * pairs)
                    sp.dma_start(nodes_of(out, group_rows(m.nodes, g, m.groups)), res[:, slot, :, :]).then_inc(stored[slot], 16)

                run(sp, m.groups, SLOTS, [(load, 3), (load_again, 0), (store, -1)])
                for slot in range(SLOTS):
                    sp.wait_ge(stored[slot], 16 * pairs)

            @block.gpsimd
            def _(pool):
                def scales(k, slot):
                    g = 2 * k + slot
                    pool.wait_ge(s["moments"], done(g))
                    pool.tensor_tensor(var[:, slot, :], moments[:, slot, :, 1], m.ln_eps[:, 0:J], ALU.add).then_inc(s["var"], 1)
                    pool.wait_ge(s["rows"], done(g - SLOTS))
                    pool.wait_ge(s["var"], done(g))
                    pool.tensor_tensor(rstd[:, slot, :], var[:, slot, :], m.minus_half[:, 0:J], ALU.pow).then_inc(s["rstd"], 1)

                def low_first(k, slot):
                    g = 2 * k + slot
                    for i in range(0, NC1, 2):
                        pool.wait_ge(high1, NC1 * g + i + 1)
                        pool.tensor_tensor(act1[1][:, i, :], act1_f[:, i, :], act1[0][:, i, :], ALU.subtract).then_inc(split_pool, 1)

                def low_second(k, slot):
                    g = 2 * k + slot
                    pool.wait_ge(high2, g + 1)
                    pool.tensor_tensor(act2[1][:, 0, :], act2_f[:, 0, :], act2[0][:, 0, :], ALU.subtract).then_inc(split2, 1)

                run(pool, m.groups, SLOTS, [(scales, 2), (low_first, 0), (low_second, 0)])

            @block.vector
            def _(dve):
                def statistics(k, slot):
                    g = 2 * k + slot
                    dve.wait_ge(x_loaded[slot], 16 * k + 16)
                    for j in range(J):
                        last = dve.bn_stats(stats[:, slot, j, :], x[:, slot, j, :])
                    last.then_inc(s["stats"], 1)
                    dve.wait_ge(s["rstd"], done(g - SLOTS))
                    wait_apart(dve, m, s["stats"], done(g))
                    for j in range(J):
                        last = dve.bn_aggr(moments[:, slot, j, :], stats[:, slot, j, :])
                    last.then_inc(s["moments"], 1)

                def normalise(k, slot):
                    g = 2 * k + slot
                    dve.wait_ge(turned, KC * g)
                    dve.wait_ge(s["rstd"], done(g))
                    for j in range(J):
                        last = dve.tensor_scalar(rows[:, slot, j, :], x[:, slot, j, :], moments[:, slot, j, 0:1],
                                                 rstd[:, slot, j:j + 1], ALU.subtract, ALU.mult)
                    last.then_inc(s["rows"], 1)

                def gate_logits(k, slot):
                    g = 2 * k + slot
                    dve.wait_ge(s["gate_product"], done(g))
                    dve.scalar_tensor_tensor(out=logits[:, :, :], in0=ps_g[:, :, :], scalar=1 / UP,
                                             in1=m.gb[:, :].unsqueeze(1).broadcast_to([P, J, NE]), op0=ALU.mult,
                                             op1=ALU.add).then_inc(s["logits"], 1)
                    dve.wait_ge(s["logits"], done(g))
                    dve.reduce_max(top[:, :], logits[:, :, :], axis=AXX).then_inc(s["top"], 1)
                    dve.wait_ge(s["top"], done(g))
                    dve.tensor_tensor(shifted[:, :, :], logits[:, :, :], over_experts(top[:, :]), ALU.subtract).then_inc(s["shifted"], 1)

                def gates_and_ranks(k, slot):
                    g = 2 * k + slot
                    dve.wait_ge(s["exps"], done(g))
                    dve.reduce_sum(total[:, :], exps[:, :, :], axis=AXX).then_inc(s["total"], 1)
                    dve.wait_ge(s["total"], done(g))
                    dve.reciprocal(inverse[:, :], total[:, :]).then_inc(s["inverse"], 1)
                    dve.wait_ge(s["inverse"], done(g))
                    dve.tensor_tensor(gates[:, :, :], exps[:, :, :], over_experts(inverse[:, :]), ALU.mult).then_inc(s["gates"], 1)
                    dve.wait_ge(s["gates"], done(g))
                    dve.tensor_tensor(over[:, :, :], gates[:, :, :], over_experts(inverse[:, :]), ALU.subtract).then_inc(s["over"], 1)
                    rival = gates[:, :, :].unsqueeze(2).broadcast_to([P, J, NE, NE])
                    own = gates[:, :, :].unsqueeze(3).broadcast_to([P, J, NE, NE])
                    dve.tensor_tensor(greater[:, :, :, :], rival, own, ALU.is_gt)
                    dve.tensor_tensor(equal[:, :, :, :], rival, own, ALU.is_equal).then_inc(s["compared"], 1)
                    dve.wait_ge(s["compared"], done(g))
                    dve.tensor_tensor(equal[:, :, :, :], equal[:, :, :, :], m.tie[:, :, :].unsqueeze(1).broadcast_to([P, J, NE, NE]),
                                      ALU.mult).then_inc(s["tied"], 1)
                    dve.wait_ge(s["tied"], done(g))
                    dve.tensor_tensor(greater[:, :, :, :], greater[:, :, :, :], equal[:, :, :, :], ALU.add).then_inc(s["beaten"], 1)
                    dve.wait_ge(s["beaten"], done(g))
                    dve.reduce_sum(rank[:, :, :], greater[:, :, :, :], axis=AXX).then_inc(s["rank"], 1)
                    dve.wait_ge(s["rank"], done(g))
                    dve.tensor_scalar(chosen[:, :, :], rank[:, :, :], float(TOPK), None, ALU.is_lt).then_inc(s["chosen"], 1)

                def weights(k, slot):
                    g = 2 * k + slot
                    dve.wait_ge(s["chosen"], done(g))
                    dve.wait_ge(s["exps2"], done(g))
                    dve.tensor_tensor(chosen[:, :, :], exps[:, :, :], chosen[:, :, :], ALU.mult).then_inc(s["picked"], 1)
                    dve.wait_ge(s["picked"], done(g))
                    dve.reduce_sum(total[:, :], chosen[:, :, :], axis=AXX).then_inc(s["total2"], 1)
                    dve.wait_ge(s["total2"], done(g))
                    dve.reciprocal(inverse[:, :], total[:, :]).then_inc(s["inverse2"], 1)
                    dve.wait_ge(s["inverse2"], done(g))
                    dve.tensor_tensor(weight_f[:, :, :], chosen[:, :, :], over_experts(inverse[:, :]), ALU.mult).then_inc(s["weight_f"], 1)
                    dve.wait_ge(s["weight_f"], done(g))
                    dve.tensor_copy(weight_h[:, :, :], weight_f[:, :, :]).then_inc(s["weight_h"], 1)
                    dve.wait_ge(s["weight_h"], done(g))
                    dve.tensor_copy(weight[:, :, 0:NE], weight_h[:, :, :])
                    dve.tensor_tensor(weight[:, :, NE + 1:GR - 1], weight_f[:, :, :], weight_h[:, :, :], ALU.subtract).then_inc(s["weight"], 1)

                def low_rows(k, slot):
                    g = 2 * k + slot
                    for c in range(KC):
                        dve.wait_ge(xt_high, KC * g + c + 1)
                        dve.tensor_tensor(xt[1][:, slot, c, :], bank[3 + c][:, :], xt[0][:, slot, c, :], ALU.subtract).then_inc(xt_kept, 1)

                def low_first(k, slot):
                    g = 2 * k + slot
                    for i in range(1, NC1, 2):
                        dve.wait_ge(high1, NC1 * g + i + 1)
                        dve.tensor_tensor(act1[1][:, i, :], act1_f[:, i, :], act1[0][:, i, :], ALU.subtract).then_inc(split_dve, 1)

                def gate_experts(k, slot):
                    g = 2 * k + slot
                    for q in range(2):
                        dve.wait_ge(s["y"], done(g - 1))
                        dve.wait_ge((s["spread0"], s["spread1"])[q], done(g))
                        dve.wait_ge(kept2, 3 * g + 2 + q)
                        dve.tensor_tensor(gated_f[:, q, :], act2_f[:, 1 + q, :], bank[1 + q][:, :],
                                          ALU.mult).then_inc((s["gated0"], s["gated1"])[q], 1)
                    for q in range(2):
                        dve.wait_ge((s["gated0"], s["gated1"])[q], done(g))
                        dve.tensor_copy(act2[0][:, 1 + q, :], gated_f[:, q, :]).then_inc((s["high_g0"], s["high_g1"])[q], 1)
                    for q in range(2):
                        dve.wait_ge((s["high_g0"], s["high_g1"])[q], done(g))
                        last = dve.tensor_tensor(act2[1][:, 1 + q, :], gated_f[:, q, :], act2[0][:, 1 + q, :], ALU.subtract)
                    last.then_inc(s["gated"], 1)

                def add_up(k, slot):
                    g = 2 * k + slot
                    dve.wait_ge(again_loaded[slot], 16 * k + 16)
                    dve.wait_ge(stored[slot], 16 * k)
                    dve.wait_ge(s["y"], done(g))
                    dve.scalar_tensor_tensor(out=res[:, slot, :, :], in0=ps_y[:, :, :], scalar=1 / UP, in1=again[:, slot, :, :],
                                             op0=ALU.mult, op1=ALU.add).then_inc(s["res"], 1)

                dve.memset(weight[:, :, :], 1.0).then_inc(ones, 1)
                dve.wait_ge(ones, 1)
                dve.memset(weight[:, :, GR - 1], 0.0).then_inc(ones, 1)
                dve.wait_ge(ones, 2)
                run(dve, m.groups, SLOTS, [(gate_logits, 0), (gates_and_ranks, 0), (weights, 0), (statistics, 2),
                                 (low_first, 0), (low_rows, 1), (normalise, 2), (add_up, -1), (gate_experts, 0)])

            @block.tensor
            def _(pe):
                def product(out, lhs, rhs, first, final):
                    for i, (l, r) in enumerate(((0, 0), (0, 1), (1, 0))):
                        last = pe.matmul(out, lhsT=lhs[l], rhs=rhs[r], start=first and i == 0, stop=final and i == 2)
                    return last

                def gate_product(k, slot):
                    g = 2 * k + slot
                    pe.wait_ge(xt_kept, KC * (g + 1))
                    pe.wait_ge(s["logits"], done(g - 1))
                    for j in range(J):
                        for c in range(KC):
                            last = product(ps_g[:, j, :], [q[:, slot, c, j * P:(j + 1) * P] for q in xt],
                                           [q[:, c, :] for q in parts["gw"]], c == 0, c == KC - 1)
                    last.then_inc(s["gate_product"], 1)

                def first_layer(k, slot, i):
                    g = 2 * k + slot
                    if i == 0:
                        pe.wait_ge(kept2, 3 * g)
                    elif i < 3:
                        pe.wait_ge((s["gated0"], s["gated1"])[i - 1], done(g - 1))
                    else:
                        pe.wait_ge(kept1, NC1 * g + i - 2)
                    for c in range(KC):
                        last = product(bank[i % 3][:, :], [q[:, c, i * P:(i + 1) * P] for q in parts["w1"]],
                                       [q[:, slot, c, :] for q in xt], c == 0, c == KC - 1)
                    last.then_inc(made1, 1)

                def first_layer_start(k, slot):
                    for i in range(2):
                        first_layer(k, slot, i)

                def first_layer_end(k, slot):
                    for i in range(2, NC1):
                        first_layer(k, slot, i)

                def third_layer(k, slot):
                    g = 2 * k + slot
                    pe.wait_ge(s["res"], done(g - 1))
                    pe.wait_ge(s["gate_t"], done(g))
                    pe.wait_ge(split2, g + 1)
                    pe.wait_ge(s["gated"], done(g))
                    for j in range(J):
                        js = slice(j * P, (j + 1) * P)
                        for i in range(3):
                            product(ps_y[:, j, :], [q[:, i, js] for q in act2],
                                    [q[:, :] for q in parts["sw3"]] if i == 0 else [q[:, i - 1, :] for q in parts["ew3"]],
                                    i == 0, False)
                        for b3 in parts["b3"]:
                            last = pe.matmul(ps_y[:, j, :], lhsT=gate_t[:, js], rhs=b3[:, :], start=False, stop=b3 is parts["b3"][1])
                    last.then_inc(s["y"], 1)

                def turn(k, slot):
                    g = 2 * k + slot
                    pe.wait_ge(s["rows"], done(g))
                    for c in range(KC):
                        if not isinstance(g, int) or g > 1:
                            pe.wait_ge(kept2, 3 * (g - 2) + c + 1)
                        for j in range(J):
                            last = pe.transpose(bank[3 + c][:, j * P:(j + 1) * P], rows[:, slot, j, c * P:(c + 1) * P], m.ident[:, :])
                        last.then_inc(turned, 1)

                def turn_gates(k, slot):
                    g = 2 * k + slot
                    pe.wait_ge(s["weight"], done(g))
                    pe.wait_ge(kept1, NC1 * g + 4)
                    for j in range(J):
                        last = pe.transpose(bank[0][0:GR, j * P:(j + 1) * P], weight[:, j, :], m.ident[:, :])
                    last.then_inc(s["gate_rows"], 1)

                def second_layer(k, slot):
                    g = 2 * k + slot
                    pe.wait_ge(split_pool, NC1 // 2 * (g + 1))
                    pe.wait_ge(split_dve, NC1 // 2 * (g + 1))
                    pe.wait_ge(xt_kept, KC * g + KC + 1 if not last_group(m, g) else KC * (g + 1))
                    for c in range(KC):
                        last = product(bank[3][:, :], [q[:, c, :] for q in parts["sw2"]], [q[:, c, :] for q in act1], c == 0, c == KC - 1)
                    last.then_inc(made2, 1)
                    pe.wait_ge(s["gate_t"], done(g))
                    for q in range(2):
                        pe.matmul(bank[1 + q][:, :], lhsT=over_features[:, q, :], rhs=gate_t[:, :], start=True,
                                  stop=True).then_inc((s["spread0"], s["spread1"])[q], 1)
                    for q in range(2):
                        if q == 0:
                            pe.wait_ge(xt_kept, KC * (g + 2) if not last_group(m, g) else KC * (g + 1))
                        for i in range(2):
                            e = 2 * q + i
                            last = product(bank[4 if q == 0 else 0][i * EH2:(i + 1) * EH2, :], [w[:, e, :] for w in parts["ew2"]],
                                           [w[:, 2 + e, :] for w in act1], True, True)
                        last.then_inc(made2, 1)

                run(pe, m.groups, SLOTS, [(gate_product, 0), (first_layer_start, 0), (first_layer_end, 0), (turn, 1),
                                (turn_gates, 0), (third_layer, -1), (second_layer, 0)])

            @block.scalar
            def _(act):
                def keep_first(k, slot, chunks):
                    g = 2 * k + slot
                    for i in chunks:
                        act.wait_ge(made1, NC1 * g + i + 1)
                        if not isinstance(g, int) or g > 0:
                            act.wait_ge((split_pool, split_dve)[i % 2], NC1 // 2 * (g - 1) + i // 2 + 1)
                        act.activation(act1_f[:, i, :], bank[i % 3][:, :], ACT.Relu, bias=m.b1[:, i:i + 1], scale=1 / UP).then_inc(kept1, 1)
                    for i in chunks:
                        act.wait_ge(kept1, NC1 * g + i + 1)
                        act.activation(act1[0][:, i, :], act1_f[:, i, :], ACT.Copy).then_inc(high1, 1)

                def keep_first_a(k, slot):
                    keep_first(k, slot, (0, 1))

                def keep_first_b(k, slot):
                    keep_first(k, slot, (2, 3))

                def keep_first_c(k, slot):
                    keep_first(k, slot, (4, 5))

                def exp_logits(k, slot):
                    g = 2 * k + slot
                    act.wait_ge(s["picked"], done(g - 1))
                    act.wait_ge(s["shifted"], done(g))
                    act.activation(exps[:, :, :], shifted[:, :, :], ACT.Exp).then_inc(s["exps"], 1)

                def exp_gates(k, slot):
                    g = 2 * k + slot
                    act.wait_ge(s["over"], done(g))
                    act.activation(exps[:, :, :], over[:, :, :], ACT.Exp).then_inc(s["exps2"], 1)

                def keep_rows(k, slot):
                    g = 2 * k + slot
                    for c in range(KC):
                        act.wait_ge(turned, KC * g + c + 1)
                        act.activation(xt[0][:, slot, c, :], bank[3 + c][:, :], ACT.Copy).then_inc(xt_high, 1)

                def keep_gates(k, slot):
                    g = 2 * k + slot
                    act.wait_ge(s["y"], done(g - 1))
                    act.wait_ge(s["gate_rows"], done(g))
                    act.activation(gate_t[:, :], bank[0][0:GR, :], ACT.Copy).then_inc(s["gate_t"], 1)

                def keep_second(k, slot):
                    g = 2 * k + slot
                    for i in range(3):
                        act.wait_ge(made2, 3 * g + i + 1)
                        if i == 0:
                            if not isinstance(g, int) or g > 0:
                                act.wait_ge(split2, g)
                        else:
                            act.wait_ge((s["gated0"], s["gated1"])[i - 1], done(g - 1))
                        act.activation(act2_f[:, i, :], bank[(3, 4, 0)[i]][:, :], ACT.Relu, bias=m.b2[:, i:i + 1],
                                       scale=1 / UP).then_inc(kept2, 1)
                    act.wait_ge(kept2, 3 * g + 1)
                    act.activation(act2[0][:, 0, :], act2_f[:, 0, :], ACT.Copy).then_inc(high2, 1)

                run(act, m.groups, SLOTS, [(exp_logits, 0), (keep_first_a, 0), (exp_gates, 0), (keep_first_b, 0), (keep_first_c, 0),
                                 (keep_rows, 1), (keep_gates, 0), (keep_second, 0)])


_INS = ["x", "src", "dst", "L0_gnn_Wl1", "L0_gnn_Wr1", "L0_gnn_att1", "L0_gnn_b1", "L0_gnn_Wl2", "L0_gnn_Wr2",
        "L0_gnn_att2", "L0_gnn_b2", "L0_ffn_sW1", "L0_ffn_sb1", "L0_ffn_sW2", "L0_ffn_sb2", "L0_ffn_sW3",
        "L0_ffn_sb3", "L0_ffn_eW1", "L0_ffn_eb1", "L0_ffn_eW2", "L0_ffn_eb2", "L0_ffn_eW3", "L0_ffn_eb3",
        "L0_ffn_gW", "L0_ffn_gb"]


def gat_ffn_program(nc, inputs, out):
    a = inputs
    nodes, edges = a["x"].shape[0], a["src"].shape[0]
    m = Shared(nodes, edges)
    h1 = nc.dram_tensor("hidden", (nodes, F), F32, kind="Internal").ap()
    normed = nc.dram_tensor("normed", (nodes, F), F32, kind="Internal").ap()
    x1 = nc.dram_tensor("attended", (nodes, F), F32, kind="Internal").ap()
    with ExitStack() as ctx:
        setup(nc, m, a, ctx)
        dense(nc, m, 0, a["x"], None, h1, normed)
        attend_edges(nc, m, 0, normed, None, h1)
        dense(nc, m, 1, h1, a["x"], x1, None)
        attend_edges(nc, m, 1, h1, a["x"], x1)
        ffn(nc, m, x1, out)


def kernel(**inputs):
    import concourse.bacc as bacc
    import numpy as np
    from concourse.bass_utils import run_bass_kernel_spmd

    nc = bacc.Bacc("TRN2", target_bir_lowering=False, num_devices=1)
    arrays, aps = {}, {}
    for name in _INS:
        v = np.ascontiguousarray(inputs[name])
        arrays[f"in_{name}_dram"] = v
        aps[name] = nc.dram_tensor(f"in_{name}_dram", v.shape, mybir.dt.from_np(v.dtype), kind="ExternalInput").ap()
    out = nc.dram_tensor("out_0_dram", inputs["x"].shape, F32, kind="ExternalOutput").ap()
    gat_ffn_program(nc, aps, out)
    result = run_bass_kernel_spmd(nc, [arrays], core_ids=[0])
    return result.results[0]["out_0_dram"]
```

```python
from contextlib import ExitStack

import concourse.bass as bass
from concourse import mybir

F32 = mybir.dt.float32
I32 = mybir.dt.int32
BF16 = mybir.dt.bfloat16
F16 = mybir.dt.float16
ALU = mybir.AluOpType
ACT = mybir.ActivationFunctionType
AXX = mybir.AxisListType.X

P = 128
F = 256
KC = F // P
J = 4
G = P * J
H, C = 4, 64
SLOTS = 2
EDGE_SLOTS = 4
NODE_SLOTS = 6
BIG = 1e30
LN_EPS = 1e-5
DEN_EPS = 1e-16
SLOPE = 0.2
NE = 4
TOPK = 2
EH1, EH2 = 128, 64
NC1 = 2 + NE
GR = 2 * (NE + 1)
UP = 64.0


class Shared:

    def __init__(self, nodes, edges):
        self.nodes, self.edges = nodes, edges
        self.groups, self.tiles = -(-nodes // G), -(-edges // P)


def run(eng, groups, slots, steps):
    aheads = [ahead for _, ahead in steps]
    first = 1 - min(0, *aheads) // slots
    end = (groups - 1 - max(0, *aheads)) // slots

    def at(k, slot):
        for step, ahead in steps:
            step(k + (slot + ahead) // slots, (slot + ahead) % slots)

    def apart(g):
        for step, ahead in steps:
            if 0 <= g + ahead < groups:
                step((g + ahead) // slots, (g + ahead) % slots)

    for g in range(-max(aheads), slots * first):
        apart(g)
    assert first < end
    with eng.Fori(first, end) as k:
        for slot in range(slots):
            at(k, slot)
    for g in range(slots * end, groups - min(0, *aheads)):
        apart(g)


def done(g):
    return g + EDGE_SLOTS


def start_counts(nc, semaphores, counts):
    with nc.Block() as block:
        @block.sync
        def _(sp):
            for semaphore in semaphores:
                sp.sem_clear(semaphore)
            for count in counts:
                sp.sem_inc(count, EDGE_SLOTS - 1)


def wait_apart(eng, m, semaphore, value):
    eng.wait_ge(semaphore, value)
    eng.sem_inc(m.passed, 1)


def group_rows(n, g, groups):
    return n - G if isinstance(g, int) and g == groups - 1 else g * G


def last_group(m, g):
    return isinstance(g, int) and g == m.groups - 1


def nodes_of(dram, start):
    return dram[bass.ds(start, G), :].rearrange("(p j) f -> p j f", j=J)


def product(pe, out, lhs, rhs, first, final):
    for i, (l, r) in enumerate(((0, 0), (0, 1), (1, 0))):
        last = pe.matmul(out, lhsT=lhs[l], rhs=rhs[r], start=first and i == 0, stop=final and i == 2)
    return last


def split_weights(nc, halved, weights):
    with nc.Block() as block:
        @block.vector
        def _(dve):
            for w, high, low in weights:
                dve.tensor_scalar(high, w, UP, None, ALU.mult).then_inc(halved, 1)
            dve.wait_ge(halved, len(weights))
            for w, high, low in weights:
                dve.scalar_tensor_tensor(out=low, in0=w, scalar=UP, in1=high, op0=ALU.mult, op1=ALU.subtract)


def setup(nc, m, a, ctx):

    def sb(name, shape, dt=F32):
        return ctx.enter_context(nc.sbuf_tensor(name, shape, dt))

    nt = m.tiles
    m.ident = sb("ident", [P, P])
    m.minus_half = sb("minus_half", [P, 2 * J])
    m.minus_one = sb("minus_one", [P, J])
    m.ln_eps = sb("ln_eps", [P, 2 * J])
    m.last_row_ones = sb("last_row_ones", [P, P])
    m.w_gat = [sb(f"w_gat{i}", [P, KC, 2 * F]) for i in range(2)]
    m.att_cols = [sb(f"att_cols{i}", [P, KC, H]) for i in range(2)]
    m.ident_b = sb("ident_b", [P, P], BF16)
    m.b_gat = [sb(f"b_gat{i}", [P, F]) for i in range(2)]
    m.w1 = sb("w1", [P, KC, NC1 * P])
    m.b1 = sb("b1", [P, NC1])
    m.sw2 = sb("sw2", [P, KC, P])
    m.ew2 = sb("ew2", [P, NE, EH2])
    m.b2 = sb("b2", [P, 3])
    m.sw3 = sb("sw3", [P, F])
    m.ew3 = sb("ew3", [P, 2, F])
    m.b3 = sb("b3", [GR, F])
    m.gw = sb("gw", [P, KC, NE])
    m.gb = sb("gb", [P, NE])
    m.tie = sb("tie", [P, NE, NE])
    m.over_features = sb("over_features", [GR, 2, P])
    m.dst_row = sb("dst_row", [P, 1 + nt * P], I32)
    m.src_col = sb("src_col", [P, nt], I32)
    m.dst_col = sb("dst_col", [P, nt], I32)
    m.put_col = sb("put_col", [P, nt], I32)
    m.dst_colf = sb("dst_colf", [P, nt])
    m.carry_pen = sb("carry_pen", [P, nt])
    m.scr_rows = sb("scr_rows", [nt, 3, P], I32)
    m.scr_rowsf = sb("scr_rowsf", [nt, 3, P])
    m.scr_cols = sb("scr_cols", [P, 3, nt])
    m.scr_a = sb("scr_a", [P, nt])

    loaded = nc.alloc_semaphore("setup_loaded")
    idx_loaded = nc.alloc_semaphore("setup_idx_loaded")
    cleared = nc.alloc_semaphore("setup_cleared")
    m.passed = nc.alloc_semaphore("passed")
    ident_ready = nc.alloc_semaphore("setup_ident_ready")
    rows_ready = nc.alloc_semaphore("setup_rows_ready")
    cols_ready = nc.alloc_semaphore("setup_cols_ready")
    step = nc.alloc_semaphore("setup_step")
    full, tail = m.edges // P, m.edges % P
    onto_zeros = []
    plain = [
        (m.w_gat[i][:, :, s * F:(s + 1) * F], w.rearrange("(c p) n -> p c n", p=P))
        for i in range(2) for s, w in enumerate((a[f"L0_gnn_Wl{i + 1}"], a[f"L0_gnn_Wr{i + 1}"]))
    ]
    for i in range(2):
        plain.append((m.b_gat[i][:, :], a[f"L0_gnn_b{i + 1}"].partition_broadcast(P)))
    plain += [
        (m.w1[:, :, 0:2 * P], a["L0_ffn_sW1"].rearrange("(c p) n -> p c n", p=P)),
        (m.sw2[:, :, :], a["L0_ffn_sW2"].rearrange("(c p) n -> p c n", p=P)),
        (m.ew2[:, :, :], a["L0_ffn_eW2"].rearrange("e p n -> p e n")),
        (m.sw3[:, :], a["L0_ffn_sW3"]),
        (m.b3[0:NE, :], a["L0_ffn_eb3"]),
        (m.b3[NE:NE + 1, :], a["L0_ffn_sb3"].partition_broadcast(1)),
        (m.b3[NE + 1:GR - 1, :], a["L0_ffn_eb3"]),
        (m.b3[GR - 1:GR, :], a["L0_ffn_sb3"].partition_broadcast(1)),
        (m.gw[:, :, :], a["L0_ffn_gW"].rearrange("(c p) n -> p c n", p=P)),
        (m.gb[:, :], a["L0_ffn_gb"].partition_broadcast(P)),
        (m.b1[:, 0:2], a["L0_ffn_sb1"].rearrange("(c p) -> p c", p=P)),
        (m.b1[:, 2:NC1], a["L0_ffn_eb1"].rearrange("e p -> p e")),
        (m.b2[:, 0:1], a["L0_ffn_sb2"].rearrange("(c p) -> p c", p=P)),
    ]
    for e in range(NE):
        plain.append((m.w1[:, :, (2 + e) * P:(3 + e) * P], a["L0_ffn_eW1"][e].rearrange("(c p) n -> p c n", p=P)))
        half = slice((e % 2) * EH2, (e % 2 + 1) * EH2)
        plain.append((m.ew3[half, e // 2, :], a["L0_ffn_eW3"][e]))
        plain.append((m.b2[half, 1 + e // 2:2 + e // 2], a["L0_ffn_eb2"][e:e + 1, :].rearrange("e p -> p e")))
    for h in range(H):
        part = slice(h % 2 * C, (h % 2 + 1) * C)
        for i in range(2):
            onto_zeros.append((m.att_cols[i][part, h // 2, h:h + 1], a[f"L0_gnn_att{i + 1}"][h:h + 1, :].rearrange("h c -> c h")))
    src, dst = a["src"], a["dst"]
    indexes = [
        (m.scr_rows[0:full, 0, :], src[0:full * P].rearrange("(t p) -> t p", p=P)),
        (m.scr_rows[0:full, 1, :], dst[0:full * P].rearrange("(t p) -> t p", p=P)),
        (m.scr_rows[0:full, 2, :], dst[1:full * P + 1].rearrange("(t p) -> t p", p=P)),
        (m.scr_rows[full:full + 1, 0, 0:tail], src[full * P:m.edges].partition_broadcast(1)),
        (m.scr_rows[full:full + 1, 1, 0:tail], dst[full * P:m.edges].partition_broadcast(1)),
        (m.scr_rows[full:full + 1, 2, 0:tail - 1], dst[full * P + 1:m.edges].partition_broadcast(1)),
        (m.dst_row[:, 1:1 + m.edges], dst.partition_broadcast(P)),
    ]

    with nc.psum_tensor("ps_cols", [P, 3, nt], F32) as ps_cols, nc.Block() as block:
        @block.sync
        def _(sp):
            with nc.allow_non_contiguous_dma(reason="bias columns, once"):
                for out, in_ in plain:
                    sp.dma_start(out, in_).then_inc(loaded, 16)
            sp.wait_ge(cleared, 4)
            for out, in_ in indexes:
                sp.dma_start(out, in_).then_inc(idx_loaded, 16)
            with nc.allow_non_contiguous_dma(reason="attention vectors as columns, once"):
                for out, in_ in onto_zeros:
                    sp.dma_start(out, in_).then_inc(loaded, 16)
            sp.wait_ge(loaded, 16 * (len(plain) + len(onto_zeros)))

        @block.gpsimd
        def _(pool):
            pool.memset(m.ident[:, :], 0.0).then_inc(step, 1)
            pool.memset(m.last_row_ones[:, :], 0.0).then_inc(step, 1)
            pool.memset(m.tie[:, :, :], 1.0).then_inc(step, 1)
            pool.memset(m.over_features[:, :, :], 0.0).then_inc(step, 1)
            by_expert = m.over_features[:, :, :].rearrange("e q (i f) -> e q i f", i=2)
            for i, base in enumerate((0, -(NE + 1))):
                pool.wait_ge(step, 4 + i)
                pool.affine_select(out=by_expert, in_=by_expert, compare_op=ALU.not_equal, fill=1.0, base=base,
                                   pattern=[[-2, 2], [-1, 2], [0, EH2]], channel_multiplier=1).then_inc(step, 1)
            pool.affine_select(out=m.ident[:, :], in_=m.ident[:, :], compare_op=ALU.not_equal, fill=1.0, base=0,
                               pattern=[[-1, P]], channel_multiplier=1).then_inc(ident_ready, 1)
            pool.affine_select(out=m.last_row_ones[:, :], in_=m.last_row_ones[:, :], compare_op=ALU.not_equal,
                               fill=1.0, base=1 - P, pattern=[[0, P]], channel_multiplier=1).then_inc(step, 1)
            pool.affine_select(out=m.tie[:, :, :], in_=m.tie[:, :, :], compare_op=ALU.is_gt, fill=0.0, base=0,
                               pattern=[[1, NE], [-1, NE]], channel_multiplier=0).then_inc(step, 1)
            pool.wait_ge(step, 8)

        @block.vector
        def _(dve):
            dve.memset(m.scr_rows[:, :, :], -1).then_inc(cleared, 1)
            dve.memset(m.dst_row[:, :], -1).then_inc(cleared, 1)
            for i in range(2):
                dve.memset(m.att_cols[i][:, :, :], 0.0).then_inc(cleared, 1)
            dve.memset(m.ln_eps[:, :], LN_EPS)
            dve.memset(m.minus_one[:, :], -1.0)
            dve.memset(m.minus_half[:, :], -0.5).then_inc(rows_ready, 1)
            dve.wait_ge(ident_ready, 1)
            dve.tensor_copy(m.ident_b[:, :], m.ident[:, :])
            dve.wait_ge(idx_loaded, 16 * len(indexes))
            dve.tensor_copy(m.scr_rowsf[:, :, :], m.scr_rows[:, :, :]).then_inc(rows_ready, 1)
            dve.wait_ge(cols_ready, 1)
            dve.tensor_copy(m.scr_cols[:, :, :], ps_cols[:, :, :]).then_inc(cols_ready, 1)
            dve.wait_ge(cols_ready, 2)
            dve.tensor_copy(m.src_col[:, :], m.scr_cols[:, 0, :]).then_inc(cols_ready, 1)
            dve.tensor_copy(m.dst_col[:, :], m.scr_cols[:, 1, :]).then_inc(cols_ready, 1)
            dve.tensor_copy(m.dst_colf[:, :], m.scr_cols[:, 1, :]).then_inc(cols_ready, 1)
            dve.tensor_tensor(m.scr_a[:, :], m.scr_cols[:, 1, :], m.scr_cols[:, 2, :], ALU.is_equal).then_inc(cols_ready, 1)
            before = m.dst_row[:, 0:nt * P].rearrange("p (t e) -> p t e", e=P)[:, :, 0]
            dve.tensor_tensor(m.carry_pen[:, :], m.scr_cols[:, 1, :], before, ALU.is_equal).then_inc(cols_ready, 1)
            dve.wait_ge(cols_ready, 7)
            dve.scalar_tensor_tensor(out=m.put_col[:, :], in0=m.scr_a[:, :], scalar=float(m.nodes), in1=m.scr_cols[:, 1, :],
                                     op0=ALU.mult, op1=ALU.add).then_inc(cols_ready, 1)
            dve.tensor_scalar(m.carry_pen[:, :], m.carry_pen[:, :], -1.0, BIG, ALU.add, ALU.mult).then_inc(cols_ready, 1)
            dve.wait_ge(cols_ready, 9)

        @block.tensor
        def _(pe):
            pe.wait_ge(ident_ready, 1)
            pe.wait_ge(rows_ready, 2)
            for i in range(3):
                last = pe.transpose(ps_cols[:, i, :], m.scr_rowsf[:, i, :], m.ident[0:nt, 0:nt])
            last.then_inc(cols_ready, 1)


def dense_layers(nc, m, feed, normed, hidden, attended):
    with ExitStack() as ctx:
        def sb(n, shape, dt=F32):
            return ctx.enter_context(nc.sbuf_tensor("d_" + n, shape, dt))

        def ps(n, shape):
            return ctx.enter_context(nc.psum_tensor("d_" + n, shape, F32))

        semaphores = []

        def sem(n):
            semaphores.append(ctx.enter_context(nc.semaphore("d_" + n)))
            return semaphores[-1]

        x = sb("x", [P, NODE_SLOTS, J, F])
        stats = sb("stats", [P, NODE_SLOTS, J, 6])
        moments = sb("moments", [P, NODE_SLOTS, J, 2])
        var = sb("var", [P, NODE_SLOTS, J])
        rstd = sb("rstd", [P, NODE_SLOTS, J])
        minus_mean = sb("minus_mean", [P, NODE_SLOTS, J])
        rows = sb("rows", [P, SLOTS, J, F])
        rows_t = [sb(f"rows_t{i}", [P, SLOTS, KC, G], F16) for i in range(2)]
        z = sb("z", [P, SLOTS, J, F])
        low = sb("low", [P, SLOTS, J, F])
        h = sb("h", [P, SLOTS, J, F])
        h_t = [sb(f"h_t{i}", [P, SLOTS, KC, G], F16) for i in range(2)]
        res = sb("res", [P, SLOTS, J, F])
        w = [[sb(f"w{layer}_{i}", [P, KC, F], F16) for i in range(2)] for layer in range(2)]
        ps_rows, ps_h = ps("ps_rows", [P, KC, G]), ps("ps_h", [P, KC, G])
        ps_1, ps_2 = ps("ps_1", [P, J, F]), ps("ps_2", [P, J, F])

        loaded = [sem(f"loaded{i}") for i in range(NODE_SLOTS)]
        rows_stored, h_stored, stored = ([sem(f"{n}{i}") for i in range(NODE_SLOTS)] for n in ("rows_stored", "h_stored", "stored"))
        s = {n: sem(n) for n in ("stats", "moments", "var", "rstd", "centred", "rows", "resid", "rows_turned", "rows_high", "rows_t",
                                 "product1", "z", "low", "exp", "h", "h_turned", "h_high", "h_t", "product2", "res")}
        halved = sem("halved")
        start_counts(nc, semaphores, s.values())
        split_weights(nc, halved, [(m.w_gat[layer][:, :, 0:F], w[layer][0][:, :, :], w[layer][1][:, :, :]) for layer in range(2)])

        def stores_before(eng, k, slot, counts):
            before = (slot - SLOTS) % NODE_SLOTS
            eng.wait_ge(counts[before], 16 * (k + 1 if slot >= SLOTS else k))

        def store_rows_of(eng, k, slot, dram, rows_in_sbuf, counts):
            g = NODE_SLOTS * k + slot
            if last_group(m, g):
                eng.wait_ge(counts[(slot - 1) % NODE_SLOTS], 16 * len(range((slot - 1) % NODE_SLOTS, m.groups, NODE_SLOTS)))
            eng.dma_start(nodes_of(dram, group_rows(m.nodes, g, m.groups)), rows_in_sbuf).then_inc(counts[slot], 16)

        def all_stored(eng, counts):
            for slot in range(NODE_SLOTS):
                eng.wait_ge(counts[slot], 16 * len(range(slot, m.groups, NODE_SLOTS)))

        with nc.Block() as block:
            @block.sync
            def _(sp):
                def load(k, slot):
                    g = NODE_SLOTS * k + slot
                    if not isinstance(g, int) or g >= NODE_SLOTS:
                        sp.wait_ge(s["res"], done(g - NODE_SLOTS))
                    sp.dma_start(x[:, slot, :, :], nodes_of(feed, group_rows(m.nodes, g, m.groups))).then_inc(loaded[slot], 16)

                def store_rows(k, slot):
                    g = NODE_SLOTS * k + slot
                    sp.wait_ge(s["rows"], done(g))
                    store_rows_of(sp, k, slot, normed, rows[:, slot % SLOTS, :, :], rows_stored)

                def store_hidden(k, slot):
                    g = NODE_SLOTS * k + slot
                    sp.wait_ge(s["h"], done(g))
                    store_rows_of(sp, k, slot, hidden, h[:, slot % SLOTS, :, :], h_stored)

                run(sp, m.groups, NODE_SLOTS, [(store_hidden, 0), (load, 4), (store_rows, 2)])
                all_stored(sp, rows_stored)
                all_stored(sp, h_stored)

            @block.vector
            def _(dve):
                def statistics(k, slot):
                    g = NODE_SLOTS * k + slot
                    dve.wait_ge(loaded[slot], 16 * k + 16)
                    for j in range(J):
                        last = dve.bn_stats(stats[:, slot, j, :], x[:, slot, j, :])
                    last.then_inc(s["stats"], 1)
                    wait_apart(dve, m, s["stats"], done(g))
                    for j in range(J):
                        last = dve.bn_aggr(moments[:, slot, j, :], stats[:, slot, j, :])
                    last.then_inc(s["moments"], 1)

                def biased(k, slot):
                    g = NODE_SLOTS * k + slot
                    two = slot % SLOTS
                    dve.wait_ge(s["h"], done(g - SLOTS))
                    dve.wait_ge(s["product1"], done(g))
                    dve.scalar_tensor_tensor(out=z[:, two, :, :], in0=ps_1[:, :, :], scalar=1 / UP,
                                             in1=m.b_gat[0][:, :].unsqueeze(1).broadcast_to([P, J, F]), op0=ALU.mult,
                                             op1=ALU.add).then_inc(s["z"], 1)

                def elu(k, slot):
                    g = NODE_SLOTS * k + slot
                    two = slot % SLOTS
                    dve.wait_ge(s["h_turned"], done(g - SLOTS))
                    if not isinstance(g, int) or g >= SLOTS:
                        stores_before(dve, k, slot, h_stored)
                    dve.wait_ge(s["exp"], done(g))
                    dve.scalar_tensor_tensor(out=h[:, two, :, :], in0=low[:, two, :, :], scalar=-1.0,
                                             in1=z[:, two, :, :], op0=ALU.add, op1=ALU.max).then_inc(s["h"], 1)

                def low_rows(k, slot):
                    g = NODE_SLOTS * k + slot
                    two = slot % SLOTS
                    dve.wait_ge(s["rows_high"], done(g))
                    dve.tensor_tensor(rows_t[1][:, two, :, :], ps_rows[:, :, :], rows_t[0][:, two, :, :], ALU.subtract).then_inc(s["rows_t"], 1)

                def low_hidden(k, slot):
                    g = NODE_SLOTS * k + slot
                    two = slot % SLOTS
                    dve.wait_ge(s["h_high"], done(g))
                    dve.tensor_tensor(h_t[1][:, two, :, :], ps_h[:, :, :], h_t[0][:, two, :, :], ALU.subtract).then_inc(s["h_t"], 1)

                def add_up(k, slot):
                    g = NODE_SLOTS * k + slot
                    if not isinstance(g, int) or g >= SLOTS:
                        stores_before(dve, k, slot, stored)
                    dve.wait_ge(s["resid"], done(g))
                    dve.wait_ge(s["product2"], done(g))
                    dve.scalar_tensor_tensor(out=res[:, slot % SLOTS, :, :], in0=ps_2[:, :, :], scalar=1 / UP, in1=x[:, slot, :, :],
                                             op0=ALU.mult, op1=ALU.add).then_inc(s["res"], 1)

                run(dve, m.groups, NODE_SLOTS, [(elu, 0), (add_up, -1), (statistics, 3), (biased, 1), (low_hidden, 0), (low_rows, 2)])

            @block.gpsimd
            def _(pool):
                def scales(k, slot):
                    g = NODE_SLOTS * k + slot
                    pool.wait_ge(s["moments"], done(g))
                    pool.tensor_tensor(minus_mean[:, slot, :], moments[:, slot, :, 0], m.minus_one[:, :], ALU.mult)
                    pool.tensor_tensor(var[:, slot, :], moments[:, slot, :, 1], m.ln_eps[:, 0:J], ALU.add).then_inc(s["var"], 1)
                    pool.wait_ge(s["var"], done(g))
                    pool.tensor_tensor(rstd[:, slot, :], var[:, slot, :], m.minus_half[:, 0:J], ALU.pow).then_inc(s["rstd"], 1)

                def rescale(k, slot):
                    g = NODE_SLOTS * k + slot
                    pool.wait_ge(s["rstd"], done(g))
                    pool.wait_ge(s["centred"], done(g))
                    mid = rows[:, slot % SLOTS, :, :]
                    pool.tensor_tensor(mid, mid, rstd[:, slot, :].unsqueeze(2).broadcast_to([P, J, F]), ALU.mult).then_inc(s["rows"], 1)

                def resid_bias(k, slot):
                    g = NODE_SLOTS * k + slot
                    pool.wait_ge(s["centred"], done(g))
                    pool.tensor_tensor(x[:, slot, :, :], x[:, slot, :, :], m.b_gat[1][:, :].unsqueeze(1).broadcast_to([P, J, F]),
                                       ALU.add).then_inc(s["resid"], 1)

                run(pool, m.groups, NODE_SLOTS, [(rescale, 2), (resid_bias, 2), (scales, 3)])

            @block.tensor
            def _(pe):
                def turn_rows(k, slot):
                    g = NODE_SLOTS * k + slot
                    pe.wait_ge(s["rows_t"], done(g - 1))
                    pe.wait_ge(s["rows"], done(g))
                    for c in range(KC):
                        for j in range(J):
                            last = pe.transpose(ps_rows[:, c, j * P:(j + 1) * P], rows[:, slot % SLOTS, j, c * P:(c + 1) * P], m.ident[:, :])
                    last.then_inc(s["rows_turned"], 1)

                def turn_hidden(k, slot):
                    g = NODE_SLOTS * k + slot
                    pe.wait_ge(s["h_t"], done(g - 1))
                    pe.wait_ge(s["h"], done(g))
                    for c in range(KC):
                        for j in range(J):
                            last = pe.transpose(ps_h[:, c, j * P:(j + 1) * P], h[:, slot % SLOTS, j, c * P:(c + 1) * P], m.ident[:, :])
                    last.then_inc(s["h_turned"], 1)

                def by_weights(out, rows_t, w, two, sub_tiles):
                    for j in sub_tiles:
                        for c in range(KC):
                            last = product(pe, out[:, j, :], [q[:, two, c, j * P:(j + 1) * P] for q in rows_t],
                                           [q[:, c, :] for q in w], c == 0, c == KC - 1)
                    return last

                def product1_start(k, slot):
                    g = NODE_SLOTS * k + slot
                    pe.wait_ge(s["z"], done(g - 1))
                    pe.wait_ge(s["rows_t"], done(g))
                    by_weights(ps_1, rows_t, w[0], slot % SLOTS, range(J // 2))

                def product1_end(k, slot):
                    by_weights(ps_1, rows_t, w[0], slot % SLOTS, range(J // 2, J)).then_inc(s["product1"], 1)

                def product2(k, slot):
                    g = NODE_SLOTS * k + slot
                    pe.wait_ge(s["res"], done(g - 1))
                    pe.wait_ge(s["h_t"], done(g))
                    by_weights(ps_2, h_t, w[1], slot % SLOTS, range(J)).then_inc(s["product2"], 1)

                run(pe, m.groups, NODE_SLOTS, [(product1_start, 1), (product1_end, 1), (turn_hidden, 0), (turn_rows, 2), (product2, 0)])

            @block.scalar
            def _(act):
                def centre(k, slot):
                    g = NODE_SLOTS * k + slot
                    act.wait_ge(s["rows_turned"], done(g - SLOTS))
                    if not isinstance(g, int) or g >= SLOTS:
                        stores_before(act, k, slot, rows_stored)
                    act.wait_ge(s["rstd"], done(g))
                    for j in range(J):
                        last = act.activation(rows[:, slot % SLOTS, j, :], x[:, slot, j, :], ACT.Identity,
                                              bias=minus_mean[:, slot, j:j + 1])
                    last.then_inc(s["centred"], 1)

                def high_rows(k, slot):
                    g = NODE_SLOTS * k + slot
                    act.wait_ge(s["product1"], done(g - SLOTS))
                    act.wait_ge(s["rows_turned"], done(g))
                    act.activation(rows_t[0][:, slot % SLOTS, :, :], ps_rows[:, :, :], ACT.Copy).then_inc(s["rows_high"], 1)

                def high_hidden(k, slot):
                    g = NODE_SLOTS * k + slot
                    act.wait_ge(s["product2"], done(g - SLOTS))
                    act.wait_ge(s["h_turned"], done(g))
                    act.activation(h_t[0][:, slot % SLOTS, :, :], ps_h[:, :, :], ACT.Copy).then_inc(s["h_high"], 1)

                def exps(k, slot):
                    g = NODE_SLOTS * k + slot
                    two = slot % SLOTS
                    act.wait_ge(s["h"], done(g - SLOTS))
                    act.wait_ge(s["z"], done(g))
                    act.activation(low[:, two, :, :], z[:, two, :, :], ACT.Relu, scale=-1.0).then_inc(s["low"], 1)
                    act.wait_ge(s["low"], done(g))
                    act.activation(low[:, two, :, :], low[:, two, :, :], ACT.Exp, scale=-1.0).then_inc(s["exp"], 1)

                def store(k, slot):
                    g = NODE_SLOTS * k + slot
                    act.wait_ge(s["res"], done(g))
                    store_rows_of(act, k, slot, attended, res[:, slot % SLOTS, :, :], stored)

                run(act, m.groups, NODE_SLOTS, [(centre, 2), (high_hidden, 0), (high_rows, 2), (store, -1), (exps, 1)])
                all_stored(act, stored)


def attend_edges(nc, m, layer, feed, resid, out):
    pairs = m.tiles // 2
    name = f"e{layer}_"
    norm = layer == 0
    W = H * (C + 1)
    with ExitStack() as ctx:
        def sb(n, shape, dt=F32):
            return ctx.enter_context(nc.sbuf_tensor(name + n, shape, dt))

        def ps(n, shape):
            return ctx.enter_context(nc.psum_tensor(name + n, shape, F32))

        semaphores = []

        def sem(n):
            semaphores.append(ctx.enter_context(nc.semaphore(name + n)))
            return semaphores[-1]

        def heads(ap):
            return ap.unsqueeze(2).broadcast_to([ap.shape[0], H, C])

        src_idx = sb("src_idx", [P, EDGE_SLOTS, 1], I32)
        dst_idx = sb("dst_idx", [P, EDGE_SLOTS, 1], I32)
        res_idx = sb("res_idx", [P, EDGE_SLOTS, 1], I32)
        put_idx = sb("put_idx", [P, EDGE_SLOTS, 1], I32)
        x = sb("x", [P, EDGE_SLOTS, 2, F])
        resid_rows = sb("resid_rows", [P, EDGE_SLOTS, F])
        xt = sb("xt", [P, EDGE_SLOTS, 2, KC, P])
        rows = sb("rows", [P, EDGE_SLOTS, 3, F])
        pre = sb("pre", [P, 2, F])
        leaky = sb("leaky", [P, 2, KC, P])
        leaky_t = sb("leaky_t", [P, EDGE_SLOTS, 2, KC, P])
        logits = sb("logits", [P, EDGE_SLOTS, 2 * H])
        same = sb("same", [P, EDGE_SLOTS, P])
        pen = sb("pen", [P, EDGE_SLOTS, P], BF16)
        tile_max = sb("tile_max", [P, EDGE_SLOTS, H])
        loop_max = sb("loop_max", [P, H])
        arg = sb("arg", [P, 4 * H])
        ex = sb("ex", [P, EDGE_SLOTS, 4 * H])
        v = sb("v", [P, H, C + 1])
        carried = sb("carried", [P, H, C + 1])
        state = sb("state", [P, EDGE_SLOTS, W + H])
        den = sb("den", [P, 2, H])
        coef = sb("coef", [P, EDGE_SLOTS, 2 * H])
        loop_part = sb("loop_part", [P, EDGE_SLOTS, F])
        sum_part = sb("sum_part", [P, F])
        both = sb("both", [P, EDGE_SLOTS, F])
        z = sb("z", [P, EDGE_SLOTS, F])
        low = sb("low", [P, EDGE_SLOTS, F])
        res = sb("res", [P, EDGE_SLOTS, F]) if norm else z
        ps_t = ps("ps_t", [P, 2, KC, P])
        ps_m = ps("ps_m", [P, 4, F])
        ps_x = ps("ps_x", [P, 2, KC, P])
        ps_l = ps("ps_l", [P, 2 * H])
        ps_s = ps("ps_s", [P, H, P])
        ps_c = ps("ps_c", [P, W + H])
        ps_n = ps("ps_n", [P, W])

        gathered = [[sem(f"gathered_{w}{i}") for i in range(EDGE_SLOTS)] for w in ("src", "dst", "resid")]
        scattered = [sem(f"scattered{i}") for i in range(EDGE_SLOTS)]
        names = ("idx", "turned", "xt", "product", "projected", "pre", "leaky",
                 "leaky_turned", "leaky_t", "logit_product", "logits", "spread", "same", "pen", "tile_max", "carry", "max", "arg0", "arg", "ex",
                 "v", "carried", "sums", "state", "den0", "den1", "den2", "coef", "loop_part", "sum_part", "both", "z",
                 "low", "exp", "res", "put", "resid_idx", "zb")
        s = {n: sem(n) for n in names}
        init = sem("init")

        def size(t):
            return m.edges - t * P if isinstance(t, int) and t == m.tiles - 1 else P

        start_counts(nc, semaphores, s.values())

        with nc.Block() as block:
            @block.gpsimd
            def _(pool):
                def gather(k, slot):
                    t = EDGE_SLOTS * k + slot
                    p = size(t)
                    wait_apart(pool, m, s["turned"], done(t - EDGE_SLOTS))
                    pool.tensor_copy(src_idx[:, slot, :], m.src_col[:, bass.ds(t, 1)])
                    pool.tensor_copy(dst_idx[:, slot, :], m.dst_col[:, bass.ds(t, 1)]).then_inc(s["idx"], 1)
                    wait_apart(pool, m, s["idx"], done(t))
                    for i, idx in ((0, src_idx), (1, dst_idx)):
                        pool.indirect_dma_start(out=x[0:p, slot, i, :], out_offset=None, in_=feed[:, :],
                                                in_offset=bass.IndirectOffsetOnAxis(ap=idx[0:p, slot, :], axis=0)
                                                ).then_inc(gathered[i][slot], 16)

                def gather_resid(k, slot):
                    t = EDGE_SLOTS * k + slot
                    p = size(t)
                    wait_apart(pool, m, s["z"], done(t - EDGE_SLOTS))
                    pool.tensor_copy(res_idx[:, slot, :], m.dst_col[:, bass.ds(t, 1)]).then_inc(s["resid_idx"], 1)
                    wait_apart(pool, m, s["resid_idx"], done(t))
                    pool.indirect_dma_start(out=resid_rows[0:p, slot, :], out_offset=None, in_=resid[:, :],
                                            in_offset=bass.IndirectOffsetOnAxis(ap=res_idx[0:p, slot, :], axis=0)
                                            ).then_inc(gathered[2][slot], 16)

                def combine(k, slot):
                    t = EDGE_SLOTS * k + slot
                    p = size(t)
                    pool.wait_ge(s["z"], done(t - EDGE_SLOTS))
                    pool.wait_ge(s["coef"], done(t))
                    sums = state[0:p, slot, 0:W].rearrange("p (h c) -> p h c", h=H)[:, :, 0:C]
                    pool.tensor_tensor(sum_part[0:p, :].rearrange("p (h c) -> p h c", h=H), sums,
                                       heads(coef[0:p, slot, 0:H]), ALU.mult).then_inc(s["sum_part"], 1)
                    pool.wait_ge(s["loop_part"], done(t))
                    pool.wait_ge(s["sum_part"], done(t))
                    pool.tensor_tensor(both[0:p, slot, :], sum_part[0:p, :], loop_part[0:p, slot, :], ALU.add).then_inc(s["both"], 1)
                    if norm:
                        pool.wait_ge(s["res"], done(t - EDGE_SLOTS))
                        pool.wait_ge(s["both"], done(t))
                        pool.tensor_tensor(z[0:p, slot, :], both[0:p, slot, :], m.b_gat[layer][0:p, :], ALU.add).then_inc(s["z"], 1)

                def scatter(k, slot):
                    t = EDGE_SLOTS * k + slot
                    p = size(t)
                    wait_apart(pool, m, scattered[slot], 16 * k)
                    pool.tensor_copy(put_idx[:, slot, :], m.put_col[:, bass.ds(t, 1)]).then_inc(s["put"], 1)
                    pool.wait_ge(s["res"] if norm else s["z"], done(t))
                    wait_apart(pool, m, s["put"], done(t))
                    pool.indirect_dma_start(out=out[:, :], out_offset=bass.IndirectOffsetOnAxis(ap=put_idx[0:p, slot, :], axis=0),
                                            in_=res[0:p, slot, :], in_offset=None, bounds_check=m.nodes - 1,
                                            oob_is_err=False).then_inc(scattered[slot], 16)

                if norm:
                    run(pool, m.tiles, EDGE_SLOTS, [(gather, 6), (scatter, -3), (combine, 0)])
                else:
                    run(pool, m.tiles, EDGE_SLOTS, [(gather, 6), (scatter, -2), (gather_resid, 1), (combine, 0)])
                for slot in range(EDGE_SLOTS):
                    pool.wait_ge(scattered[slot], 16 * len(range(slot, m.tiles, EDGE_SLOTS)))

            @block.vector
            def _(dve):
                def maxima(k, slot):
                    t = EDGE_SLOTS * k + slot
                    p = size(t)
                    top = state[0:p, slot, W:W + H]
                    dve.wait_ge(s["carry"], done(t))
                    dve.wait_ge(s["tile_max"], done(t))
                    pen_t = m.carry_pen[0:p, bass.ds(t, 1)]
                    dve.scalar_tensor_tensor(out=top, in0=ps_c[0:p, W:W + H], scalar=pen_t, in1=tile_max[0:p, slot, :],
                                             op0=ALU.add, op1=ALU.max).then_inc(s["max"], 1)
                    dve.wait_ge(s["ex"], done(t - 1))
                    dve.wait_ge(s["max"], done(t))
                    dve.tensor_tensor(loop_max[0:p, :], top, logits[0:p, slot, H:2 * H], ALU.max).then_inc(s["arg0"], 1)
                    dve.tensor_tensor(arg[0:p, 0:H], logits[0:p, slot, 0:H], top, ALU.subtract)
                    dve.scalar_tensor_tensor(out=arg[0:p, H:2 * H], in0=ps_c[0:p, W:W + H], scalar=pen_t, in1=top,
                                             op0=ALU.add, op1=ALU.subtract)
                    dve.wait_ge(s["arg0"], done(t))
                    dve.tensor_tensor(arg[0:p, 2 * H:3 * H], top, loop_max[0:p, :], ALU.subtract)
                    dve.tensor_tensor(arg[0:p, 3 * H:4 * H], logits[0:p, slot, H:2 * H], loop_max[0:p, :],
                                      ALU.subtract).then_inc(s["arg"], 1)

                def pre_activations(k, slot):
                    t = EDGE_SLOTS * k + slot
                    p = size(t)
                    dve.wait_ge(s["leaky"], done(t - 1))
                    dve.wait_ge(s["projected"], done(t))
                    right = rows[0:p, slot, 2, :].unsqueeze(1).broadcast_to([p, 2, F])
                    dve.tensor_tensor(pre[0:p, :, :], rows[0:p, slot, 0:2, :], right, ALU.add).then_inc(s["pre"], 1)

                def weigh(k, slot):
                    t = EDGE_SLOTS * k + slot
                    p = size(t)
                    dve.wait_ge(s["sums"], done(t - 1))
                    dve.wait_ge(s["ex"], done(t))
                    dve.tensor_tensor(v[0:p, :, 0:C], rows[0:p, slot, 0, :].rearrange("p (h c) -> p h c", h=H),
                                      heads(ex[0:p, slot, 0:H]), ALU.mult)
                    dve.tensor_copy(v[0:p, :, C], ex[0:p, slot, 0:H]).then_inc(s["v"], 1)
                    dve.wait_ge(s["state"], done(t - 1))
                    dve.tensor_tensor(carried[0:p, :, :], ps_c[0:p, 0:W].rearrange("p (h c) -> p h c", h=H),
                                      ex[0:p, slot, H:2 * H].unsqueeze(2).broadcast_to([p, H, C + 1]), ALU.mult
                                      ).then_inc(s["carried"], 1)

                def leaky_rows(k, slot):
                    t = EDGE_SLOTS * k + slot
                    p = size(t)
                    dve.wait_ge(s["leaky_turned"], done(t - 1))
                    dve.wait_ge(s["pre"], done(t))
                    dve.scalar_tensor_tensor(out=leaky[0:p, :, :, :].rearrange("p i c f -> p (i c f)"),
                                             in0=pre[0:p, :, :].rearrange("p i f -> p (i f)"), scalar=SLOPE,
                                             in1=pre[0:p, :, :].rearrange("p i f -> p (i f)"), op0=ALU.mult,
                                             op1=ALU.max).then_inc(s["leaky"], 1)

                def keep_logits(k, slot):
                    t = EDGE_SLOTS * k + slot
                    p = size(t)
                    dve.wait_ge(s["arg"], done(t - EDGE_SLOTS))
                    dve.wait_ge(s["logit_product"], done(t))
                    dve.tensor_copy(logits[0:p, slot, :], ps_l[0:p, :]).then_inc(s["logits"], 1)

                def accumulate(k, slot):
                    t = EDGE_SLOTS * k + slot
                    p = size(t)
                    dve.wait_ge(s["both"], done(t - EDGE_SLOTS))
                    dve.wait_ge(s["carried"], done(t))
                    dve.wait_ge(s["sums"], done(t))
                    dve.tensor_tensor(state[0:p, slot, 0:W], ps_n[0:p, 0:W], carried[0:p, :, :].rearrange("p h c -> p (h c)"),
                                      ALU.add).then_inc(s["state"], 1)

                def coefficients(k, slot):
                    t = EDGE_SLOTS * k + slot
                    p = size(t)
                    dve.wait_ge(s["state"], done(t))
                    a, b = ex[0:p, slot, 2 * H:3 * H], ex[0:p, slot, 3 * H:4 * H]
                    dens = state[0:p, slot, 0:W].rearrange("p (h c) -> p h c", h=H)[:, :, C]
                    dve.wait_ge(s["coef"], done(t - 1))
                    dve.tensor_tensor(den[0:p, 0, :], dens, a, ALU.mult).then_inc(s["den0"], 1)
                    dve.wait_ge(s["den0"], done(t))
                    dve.scalar_tensor_tensor(out=den[0:p, 1, :], in0=den[0:p, 0, :], scalar=DEN_EPS, in1=b,
                                             op0=ALU.add, op1=ALU.add).then_inc(s["den1"], 1)
                    dve.wait_ge(s["den1"], done(t))
                    dve.reciprocal(den[0:p, 0, :], den[0:p, 1, :]).then_inc(s["den2"], 1)
                    dve.wait_ge(s["den2"], done(t))
                    dve.tensor_tensor(coef[0:p, slot, 0:H], a, den[0:p, 0, :], ALU.mult)
                    dve.tensor_tensor(coef[0:p, slot, H:2 * H], b, den[0:p, 0, :], ALU.mult).then_inc(s["coef"], 1)
                    dve.wait_ge(s["coef"], done(t))
                    dve.tensor_tensor(loop_part[0:p, slot, :].rearrange("p (h c) -> p h c", h=H),
                                      rows[0:p, slot, 1, :].rearrange("p (h c) -> p h c", h=H),
                                      heads(coef[0:p, slot, H:2 * H]), ALU.mult).then_inc(s["loop_part"], 1)

                def group(k, slot):
                    t = EDGE_SLOTS * k + slot
                    p = size(t)
                    dve.wait_ge(s["sums"], done(t - EDGE_SLOTS))
                    dve.tensor_scalar(same[0:p, slot, 0:p], m.dst_row[0:p, bass.ds(t * P + 1, p)], m.dst_colf[0:p, bass.ds(t, 1)],
                                      None, ALU.is_equal).then_inc(s["same"], 1)
                    dve.wait_ge(s["spread"], done(t - EDGE_SLOTS))
                    dve.wait_ge(s["same"], done(t))
                    dve.tensor_scalar(pen[0:p, slot, 0:p], same[0:p, slot, 0:p], -1.0, BIG, ALU.add, ALU.mult).then_inc(s["pen"], 1)

                def group_maxima(k, slot):
                    t = EDGE_SLOTS * k + slot
                    p = size(t)
                    dve.wait_ge(s["max"], done(t - EDGE_SLOTS))
                    dve.wait_ge(s["spread"], done(t))
                    dve.reduce_max(tile_max[0:p, slot, :], ps_s[0:p, :, 0:p],
                                   axis=AXX).then_inc(s["tile_max"], 1)

                def low_part(k, slot):
                    t = EDGE_SLOTS * k + slot
                    p = size(t)
                    dve.wait_ge(s["res"], done(t - EDGE_SLOTS))
                    dve.wait_ge(s["z"], done(t))
                    dve.tensor_scalar(low[0:p, slot, :], z[0:p, slot, :], 0.0, None, ALU.min).then_inc(s["low"], 1)

                def elu(k, slot):
                    t = EDGE_SLOTS * k + slot
                    p = size(t)
                    dve.wait_ge(scattered[slot], 16 * k)
                    dve.wait_ge(s["exp"], done(t))
                    dve.scalar_tensor_tensor(out=res[0:p, slot, :], in0=low[0:p, slot, :], scalar=-1.0, in1=z[0:p, slot, :],
                                             op0=ALU.add, op1=ALU.max).then_inc(s["res"], 1)

                def add_residual(k, slot):
                    t = EDGE_SLOTS * k + slot
                    p = size(t)
                    dve.wait_ge(s["both"], done(t))
                    dve.tensor_tensor(low[0:p, slot, :], both[0:p, slot, :], m.b_gat[layer][0:p, :], ALU.add).then_inc(s["zb"], 1)
                    dve.wait_ge(gathered[2][slot], 16 * k + 16)
                    dve.wait_ge(scattered[slot], 16 * k)
                    dve.wait_ge(s["zb"], done(t))
                    dve.tensor_tensor(z[0:p, slot, :], low[0:p, slot, :], resid_rows[0:p, slot, :], ALU.add).then_inc(s["z"], 1)

                dve.memset(state[:, EDGE_SLOTS - 1, :], 0.0).then_inc(init, 1)
                run(dve, m.tiles, EDGE_SLOTS,
                    [(maxima, 0), (pre_activations, 2), (weigh, 0), (leaky_rows, 2), (keep_logits, 1), (group, 2), (group_maxima, 1),
                     (accumulate, 0), (coefficients, 0)] + ([(low_part, -1), (elu, -2)] if norm else [(add_residual, -1)]))

            @block.tensor
            def _(pe):
                def carry(k, slot):
                    t = EDGE_SLOTS * k + slot
                    pe.wait_ge(init, 1)
                    pe.wait_ge(s["carried"], done(t - 1))
                    pe.wait_ge(s["state"], done(t - 1))
                    pe.matmul(ps_c[:, :], lhsT=m.last_row_ones[:, :], rhs=state[:, (slot - 1) % EDGE_SLOTS, :], start=True,
                              stop=True).then_inc(s["carry"], 1)

                def turn(k, slot):
                    t = EDGE_SLOTS * k + slot
                    p = size(t)
                    pe.wait_ge(s["xt"], done(t - 1))
                    for i in range(2):
                        pe.wait_ge(gathered[i][slot], 16 * k + 16)
                    for i in range(2):
                        for c in range(KC):
                            last = pe.transpose(ps_t[:, i, c, 0:p], x[0:p, slot, i, c * P:(c + 1) * P], m.ident[0:p, 0:p])
                    last.then_inc(s["turned"], 1)

                def product(k, slot):
                    t = EDGE_SLOTS * k + slot
                    p = size(t)
                    pe.wait_ge(s["projected"], done(t - 1))
                    pe.wait_ge(s["xt"], done(t))
                    for i, (first, last_) in enumerate(((1, 2), (2, 4))):
                        for c in range(KC):
                            last = pe.matmul(ps_m[0:p, first:last_, :], lhsT=xt[:, slot, i, c, 0:p],
                                             rhs=m.w_gat[layer][:, c, 0:(last_ - first) * F], start=c == 0, stop=c == KC - 1)
                    last.then_inc(s["product"], 1)

                def turn_leaky(k, slot):
                    t = EDGE_SLOTS * k + slot
                    p = size(t)
                    pe.wait_ge(s["leaky_t"], done(t - 1))
                    pe.wait_ge(s["leaky"], done(t))
                    for i in range(2):
                        for c in range(KC):
                            last = pe.transpose(ps_x[:, i, c, 0:p], leaky[0:p, i, c, :], m.ident[0:p, 0:p])
                    last.then_inc(s["leaky_turned"], 1)

                def score(k, slot):
                    t = EDGE_SLOTS * k + slot
                    p = size(t)
                    pe.wait_ge(s["logits"], done(t - 1))
                    pe.wait_ge(s["leaky_t"], done(t))
                    for i in range(2):
                        for c in range(KC):
                            last = pe.matmul(ps_l[0:p, i * H:(i + 1) * H], lhsT=leaky_t[:, slot, i, c, 0:p],
                                             rhs=m.att_cols[layer][:, c, :], start=c == 0, stop=c == KC - 1)
                    last.then_inc(s["logit_product"], 1)

                def spread(k, slot):
                    t = EDGE_SLOTS * k + slot
                    p = size(t)
                    pe.wait_ge(s["tile_max"], done(t - 1))
                    pe.wait_ge(s["pen"], done(t))
                    pe.wait_ge(s["leaky_t"], done(t))
                    pe.matmul(ps_s[0:p, :, 0:p], lhsT=m.ident_b[0:p, 0:p],
                              rhs=pen[0:p, slot, 0:p].unsqueeze(1).broadcast_to([p, H, p]),
                              start=True, stop=False, skip_group_check=True)
                    for h in range(H):
                        att = m.att_cols[layer][:, h // 2, h:h + 1].broadcast_to([P, p])
                        last = pe.matmul(ps_s[0:p, h, 0:p], lhsT=att, rhs=leaky_t[:, slot, 0, h // 2, 0:p],
                                         start=False, stop=h == H - 1, skip_group_check=True)
                    last.then_inc(s["spread"], 1)

                def sums(k, slot):
                    t = EDGE_SLOTS * k + slot
                    p = size(t)
                    pe.wait_ge(s["state"], done(t - 1))
                    pe.wait_ge(s["v"], done(t))
                    pe.matmul(ps_n[0:p, 0:W], lhsT=same[0:p, slot, 0:p], rhs=v[0:p, :, :].rearrange("p h c -> p (h c)"),
                              start=True, stop=True).then_inc(s["sums"], 1)

                run(pe, m.tiles, EDGE_SLOTS, [(spread, 1), (product, 3), (sums, 0), (turn_leaky, 2), (carry, 1), (turn, 4), (score, 2)])

            @block.scalar
            def _(act):
                def weights(k, slot):
                    t = EDGE_SLOTS * k + slot
                    p = size(t)
                    act.wait_ge(s["coef"], done(t - EDGE_SLOTS))
                    act.wait_ge(s["arg"], done(t))
                    act.activation(ex[0:p, slot, :], arg[0:p, :], ACT.Exp).then_inc(s["ex"], 1)

                def evacuate_leaky(k, slot):
                    t = EDGE_SLOTS * k + slot
                    p = size(t)
                    act.wait_ge(s["spread"], done(t - EDGE_SLOTS))
                    act.wait_ge(s["leaky_turned"], done(t))
                    act.activation(leaky_t[:, slot, :, :, 0:p], ps_x[:, :, :, 0:p], ACT.Copy).then_inc(s["leaky_t"], 1)

                def evacuate_rows(k, slot):
                    t = EDGE_SLOTS * k + slot
                    p = size(t)
                    act.wait_ge(s["product"], done(t - EDGE_SLOTS))
                    act.wait_ge(s["turned"], done(t))
                    act.activation(xt[:, slot, :, :, 0:p], ps_t[:, :, :, 0:p], ACT.Copy).then_inc(s["xt"], 1)

                def evacuate_product(k, slot):
                    t = EDGE_SLOTS * k + slot
                    p = size(t)
                    act.wait_ge(s["loop_part"], done(t - EDGE_SLOTS))
                    act.wait_ge(s["product"], done(t))
                    act.activation(rows[0:p, slot, :, :], ps_m[0:p, 1:4, :], ACT.Copy).then_inc(s["projected"], 1)

                def low_exp(k, slot):
                    t = EDGE_SLOTS * k + slot
                    p = size(t)
                    act.wait_ge(s["low"], done(t))
                    act.activation(low[0:p, slot, :], low[0:p, slot, :], ACT.Exp).then_inc(s["exp"], 1)

                run(act, m.tiles, EDGE_SLOTS, [(weights, 0), (evacuate_product, 3), (evacuate_leaky, 2), (evacuate_rows, 4)]
                    + [(low_exp, -1)] * norm)


def ffn(nc, m, feed, out):
    pairs = m.groups // 2
    name = "f_"
    with ExitStack() as ctx:
        def sb(n, shape, dt=F32):
            return ctx.enter_context(nc.sbuf_tensor(name + n, shape, dt))

        semaphores = []

        def sem(n):
            semaphores.append(ctx.enter_context(nc.semaphore(name + n)))
            return semaphores[-1]

        x = sb("x", [P, SLOTS, J, F])
        again = sb("again", [P, SLOTS, J, F])
        rows = sb("rows", [P, SLOTS, J, F])
        stats = sb("stats", [P, SLOTS, J, 6])
        moments = sb("moments", [P, SLOTS, J, 2])
        var = sb("var", [P, SLOTS, J])
        rstd = sb("rstd", [P, SLOTS, J])
        act1_f = sb("act1_f", [P, NC1, G])
        act2_f = sb("act2_f", [P, 3, G])
        gated_f = sb("gated_f", [P, 2, G])
        xt = [sb(f"xt{i}", [P, SLOTS, KC, G], F16) for i in range(2)]
        act1 = [sb(f"act1_{i}", [P, NC1, G], F16) for i in range(2)]
        act2 = [sb(f"act2_{i}", [P, 3, G], F16) for i in range(2)]
        gate_t = sb("gate_t", [GR, G], F16)
        over_features = sb("over_features", [GR, 2, P], F16)
        parts = {}
        for n, w in (("w1", m.w1), ("sw2", m.sw2), ("ew2", m.ew2), ("sw3", m.sw3), ("ew3", m.ew3), ("b3", m.b3), ("gw", m.gw)):
            parts[n] = [sb(f"{n}_{i}", list(w.shape), F16) for i in range(2)]
        weight_h = sb("weight_h", [P, J, NE], F16)
        weight_f = sb("weight_f", [P, J, NE])
        logits = sb("logits", [P, J, NE])
        top = sb("top", [P, J])
        over = sb("over", [P, J, NE])
        shifted = sb("shifted", [P, J, NE])
        exps = sb("exps", [P, J, NE])
        total = sb("total", [P, J])
        inverse = sb("inverse", [P, J])
        gates = sb("gates", [P, J, NE])
        greater = sb("greater", [P, J, NE, NE])
        equal = sb("equal", [P, J, NE, NE])
        rank = sb("rank", [P, J, NE])
        chosen = sb("chosen", [P, J, NE])
        weight = sb("weight", [P, J, GR])
        res = sb("res", [P, SLOTS, J, F])
        bank = [ctx.enter_context(nc.psum_tensor(f"{name}bank{i}", [P, G], F32)) for i in range(5)]
        ps_g = ctx.enter_context(nc.psum_tensor(f"{name}ps_g", [P, J, NE], F32))
        ps_y = ctx.enter_context(nc.psum_tensor(f"{name}ps_y", [P, J, F], F32))

        x_loaded = [sem(f"x_loaded{i}") for i in range(SLOTS)]
        again_loaded = [sem(f"again_loaded{i}") for i in range(SLOTS)]
        stored = [sem(f"stored{i}") for i in range(SLOTS)]
        s = {n: sem(n) for n in ("stats", "moments", "var", "rstd", "rows", "gate_product", "logits", "top", "shifted",
                                      "exps", "total", "inverse", "gates", "compared", "tied", "beaten", "rank", "chosen", "over",
                                      "exps2", "picked", "total2", "inverse2", "weight_f", "weight_h", "weight", "spread0", "spread1", "gate_rows",
                                      "gate_t", "gated0", "gated1", "high_g0", "high_g1", "gated", "y", "res")}
        turned, xt_kept = sem("turned"), sem("xt_kept")
        made1, kept1 = sem("made1"), sem("kept1")
        made2, kept2 = sem("made2"), sem("kept2")
        high1 = sem("high1")
        split_pool, split_dve = sem("split_pool"), sem("split_dve")
        xt_high = sem("xt_high")
        high2, split2 = sem("high2"), sem("split2")
        ones, halved = sem("ones"), sem("halved")
        start_counts(nc, semaphores, s.values())

        def over_experts(ap):
            return ap.unsqueeze(2).broadcast_to([P, J, NE])

        def all_of(w):
            return w[tuple(slice(None) for _ in w.shape)]

        whole = [(m.w1, "w1"), (m.sw2, "sw2"), (m.ew2, "ew2"), (m.sw3, "sw3"), (m.ew3, "ew3"), (m.b3, "b3"), (m.gw, "gw")]
        split_weights(nc, halved, [(all_of(w), all_of(parts[n][0]), all_of(parts[n][1])) for w, n in whole])

        with nc.Block() as block:
            @block.sync
            def _(sp):
                def load(k, slot):
                    g = 2 * k + slot
                    sp.wait_ge(s["rows"], done(g - SLOTS))
                    sp.dma_start(x[:, slot, :, :], nodes_of(feed, group_rows(m.nodes, g, m.groups))).then_inc(x_loaded[slot], 16)

                def load_again(k, slot):
                    g = 2 * k + slot
                    sp.wait_ge(s["res"], done(g - SLOTS))
                    sp.dma_start(again[:, slot, :, :], nodes_of(feed, group_rows(m.nodes, g, m.groups))).then_inc(again_loaded[slot], 16)

                def store(k, slot):
                    g = 2 * k + slot
                    sp.wait_ge(s["res"], done(g))
                    if last_group(m, g):
                        sp.wait_ge(stored[0], 16 * pairs)
                    sp.dma_start(nodes_of(out, group_rows(m.nodes, g, m.groups)), res[:, slot, :, :]).then_inc(stored[slot], 16)

                run(sp, m.groups, SLOTS, [(load, 3), (load_again, 0), (store, -1)])
                for slot in range(SLOTS):
                    sp.wait_ge(stored[slot], 16 * pairs)

            @block.gpsimd
            def _(pool):
                def scales(k, slot):
                    g = 2 * k + slot
                    pool.wait_ge(s["moments"], done(g))
                    pool.tensor_tensor(var[:, slot, :], moments[:, slot, :, 1], m.ln_eps[:, 0:J], ALU.add).then_inc(s["var"], 1)
                    pool.wait_ge(s["rows"], done(g - SLOTS))
                    pool.wait_ge(s["var"], done(g))
                    pool.tensor_tensor(rstd[:, slot, :], var[:, slot, :], m.minus_half[:, 0:J], ALU.pow).then_inc(s["rstd"], 1)

                def low_first(k, slot):
                    g = 2 * k + slot
                    for i in range(0, NC1, 2):
                        pool.wait_ge(high1, NC1 * g + i + 1)
                        pool.tensor_tensor(act1[1][:, i, :], act1_f[:, i, :], act1[0][:, i, :], ALU.subtract).then_inc(split_pool, 1)

                def low_second(k, slot):
                    g = 2 * k + slot
                    pool.wait_ge(high2, g + 1)
                    pool.tensor_tensor(act2[1][:, 0, :], act2_f[:, 0, :], act2[0][:, 0, :], ALU.subtract).then_inc(split2, 1)

                run(pool, m.groups, SLOTS, [(scales, 2), (low_first, 0), (low_second, 0)])

            @block.vector
            def _(dve):
                def statistics(k, slot):
                    g = 2 * k + slot
                    dve.wait_ge(x_loaded[slot], 16 * k + 16)
                    for j in range(J):
                        last = dve.bn_stats(stats[:, slot, j, :], x[:, slot, j, :])
                    last.then_inc(s["stats"], 1)
                    dve.wait_ge(s["rstd"], done(g - SLOTS))
                    wait_apart(dve, m, s["stats"], done(g))
                    for j in range(J):
                        last = dve.bn_aggr(moments[:, slot, j, :], stats[:, slot, j, :])
                    last.then_inc(s["moments"], 1)

                def normalise(k, slot):
                    g = 2 * k + slot
                    dve.wait_ge(turned, KC * g)
                    dve.wait_ge(s["rstd"], done(g))
                    for j in range(J):
                        last = dve.tensor_scalar(rows[:, slot, j, :], x[:, slot, j, :], moments[:, slot, j, 0:1],
                                                 rstd[:, slot, j:j + 1], ALU.subtract, ALU.mult)
                    last.then_inc(s["rows"], 1)

                def gate_logits(k, slot):
                    g = 2 * k + slot
                    dve.wait_ge(s["gate_product"], done(g))
                    dve.scalar_tensor_tensor(out=logits[:, :, :], in0=ps_g[:, :, :], scalar=1 / UP,
                                             in1=m.gb[:, :].unsqueeze(1).broadcast_to([P, J, NE]), op0=ALU.mult,
                                             op1=ALU.add).then_inc(s["logits"], 1)
                    dve.wait_ge(s["logits"], done(g))
                    dve.reduce_max(top[:, :], logits[:, :, :], axis=AXX).then_inc(s["top"], 1)
                    dve.wait_ge(s["top"], done(g))
                    dve.tensor_tensor(shifted[:, :, :], logits[:, :, :], over_experts(top[:, :]), ALU.subtract).then_inc(s["shifted"], 1)

                def gates_and_ranks(k, slot):
                    g = 2 * k + slot
                    dve.wait_ge(s["exps"], done(g))
                    dve.reduce_sum(total[:, :], exps[:, :, :], axis=AXX).then_inc(s["total"], 1)
                    dve.wait_ge(s["total"], done(g))
                    dve.reciprocal(inverse[:, :], total[:, :]).then_inc(s["inverse"], 1)
                    dve.wait_ge(s["inverse"], done(g))
                    dve.tensor_tensor(gates[:, :, :], exps[:, :, :], over_experts(inverse[:, :]), ALU.mult).then_inc(s["gates"], 1)
                    dve.wait_ge(s["gates"], done(g))
                    dve.tensor_tensor(over[:, :, :], gates[:, :, :], over_experts(inverse[:, :]), ALU.subtract).then_inc(s["over"], 1)
                    rival = gates[:, :, :].unsqueeze(2).broadcast_to([P, J, NE, NE])
                    own = gates[:, :, :].unsqueeze(3).broadcast_to([P, J, NE, NE])
                    dve.tensor_tensor(greater[:, :, :, :], rival, own, ALU.is_gt)
                    dve.tensor_tensor(equal[:, :, :, :], rival, own, ALU.is_equal).then_inc(s["compared"], 1)
                    dve.wait_ge(s["compared"], done(g))
                    dve.tensor_tensor(equal[:, :, :, :], equal[:, :, :, :], m.tie[:, :, :].unsqueeze(1).broadcast_to([P, J, NE, NE]),
                                      ALU.mult).then_inc(s["tied"], 1)
                    dve.wait_ge(s["tied"], done(g))
                    dve.tensor_tensor(greater[:, :, :, :], greater[:, :, :, :], equal[:, :, :, :], ALU.add).then_inc(s["beaten"], 1)
                    dve.wait_ge(s["beaten"], done(g))
                    dve.reduce_sum(rank[:, :, :], greater[:, :, :, :], axis=AXX).then_inc(s["rank"], 1)
                    dve.wait_ge(s["rank"], done(g))
                    dve.tensor_scalar(chosen[:, :, :], rank[:, :, :], float(TOPK), None, ALU.is_lt).then_inc(s["chosen"], 1)

                def weights(k, slot):
                    g = 2 * k + slot
                    dve.wait_ge(s["chosen"], done(g))
                    dve.wait_ge(s["exps2"], done(g))
                    dve.tensor_tensor(chosen[:, :, :], exps[:, :, :], chosen[:, :, :], ALU.mult).then_inc(s["picked"], 1)
                    dve.wait_ge(s["picked"], done(g))
                    dve.reduce_sum(total[:, :], chosen[:, :, :], axis=AXX).then_inc(s["total2"], 1)
                    dve.wait_ge(s["total2"], done(g))
                    dve.reciprocal(inverse[:, :], total[:, :]).then_inc(s["inverse2"], 1)
                    dve.wait_ge(s["inverse2"], done(g))
                    dve.tensor_tensor(weight_f[:, :, :], chosen[:, :, :], over_experts(inverse[:, :]), ALU.mult).then_inc(s["weight_f"], 1)
                    dve.wait_ge(s["weight_f"], done(g))
                    dve.tensor_copy(weight_h[:, :, :], weight_f[:, :, :]).then_inc(s["weight_h"], 1)
                    dve.wait_ge(s["weight_h"], done(g))
                    dve.tensor_copy(weight[:, :, 0:NE], weight_h[:, :, :])
                    dve.tensor_tensor(weight[:, :, NE + 1:GR - 1], weight_f[:, :, :], weight_h[:, :, :], ALU.subtract).then_inc(s["weight"], 1)

                def low_rows(k, slot):
                    g = 2 * k + slot
                    for c in range(KC):
                        dve.wait_ge(xt_high, KC * g + c + 1)
                        dve.tensor_tensor(xt[1][:, slot, c, :], bank[3 + c][:, :], xt[0][:, slot, c, :], ALU.subtract).then_inc(xt_kept, 1)

                def low_first(k, slot):
                    g = 2 * k + slot
                    for i in range(1, NC1, 2):
                        dve.wait_ge(high1, NC1 * g + i + 1)
                        dve.tensor_tensor(act1[1][:, i, :], act1_f[:, i, :], act1[0][:, i, :], ALU.subtract).then_inc(split_dve, 1)

                def gate_experts(k, slot):
                    g = 2 * k + slot
                    for q in range(2):
                        dve.wait_ge(s["y"], done(g - 1))
                        dve.wait_ge((s["spread0"], s["spread1"])[q], done(g))
                        dve.wait_ge(kept2, 3 * g + 2 + q)
                        dve.tensor_tensor(gated_f[:, q, :], act2_f[:, 1 + q, :], bank[1 + q][:, :],
                                          ALU.mult).then_inc((s["gated0"], s["gated1"])[q], 1)
                    for q in range(2):
                        dve.wait_ge((s["gated0"], s["gated1"])[q], done(g))
                        dve.tensor_copy(act2[0][:, 1 + q, :], gated_f[:, q, :]).then_inc((s["high_g0"], s["high_g1"])[q], 1)
                    for q in range(2):
                        dve.wait_ge((s["high_g0"], s["high_g1"])[q], done(g))
                        last = dve.tensor_tensor(act2[1][:, 1 + q, :], gated_f[:, q, :], act2[0][:, 1 + q, :], ALU.subtract)
                    last.then_inc(s["gated"], 1)

                def add_up(k, slot):
                    g = 2 * k + slot
                    dve.wait_ge(again_loaded[slot], 16 * k + 16)
                    dve.wait_ge(stored[slot], 16 * k)
                    dve.wait_ge(s["y"], done(g))
                    dve.scalar_tensor_tensor(out=res[:, slot, :, :], in0=ps_y[:, :, :], scalar=1 / UP, in1=again[:, slot, :, :],
                                             op0=ALU.mult, op1=ALU.add).then_inc(s["res"], 1)

                dve.tensor_copy(over_features[:, :, :], m.over_features[:, :, :])
                dve.memset(weight[:, :, :], 1.0).then_inc(ones, 1)
                dve.wait_ge(ones, 1)
                dve.memset(weight[:, :, GR - 1], 0.0).then_inc(ones, 1)
                dve.wait_ge(ones, 2)
                run(dve, m.groups, SLOTS, [(gate_logits, 0), (gates_and_ranks, 0), (weights, 0), (statistics, 2),
                                 (low_first, 0), (low_rows, 1), (normalise, 2), (add_up, -1), (gate_experts, 0)])

            @block.tensor
            def _(pe):
                def gate_product(k, slot):
                    g = 2 * k + slot
                    pe.wait_ge(xt_kept, KC * (g + 1))
                    pe.wait_ge(s["logits"], done(g - 1))
                    for j in range(J):
                        for c in range(KC):
                            last = product(pe, ps_g[:, j, :], [q[:, slot, c, j * P:(j + 1) * P] for q in xt],
                                           [q[:, c, :] for q in parts["gw"]], c == 0, c == KC - 1)
                    last.then_inc(s["gate_product"], 1)

                def first_layer(k, slot, i):
                    g = 2 * k + slot
                    if i == 0:
                        pe.wait_ge(kept2, 3 * g)
                    elif i < 3:
                        pe.wait_ge((s["gated0"], s["gated1"])[i - 1], done(g - 1))
                    else:
                        pe.wait_ge(kept1, NC1 * g + i - 2)
                    for c in range(KC):
                        last = product(pe, bank[i % 3][:, :], [q[:, c, i * P:(i + 1) * P] for q in parts["w1"]],
                                       [q[:, slot, c, :] for q in xt], c == 0, c == KC - 1)
                    last.then_inc(made1, 1)

                def first_layer_start(k, slot):
                    for i in range(2):
                        first_layer(k, slot, i)

                def first_layer_end(k, slot):
                    for i in range(2, NC1):
                        first_layer(k, slot, i)

                def third_layer(k, slot):
                    g = 2 * k + slot
                    pe.wait_ge(s["res"], done(g - 1))
                    pe.wait_ge(s["gate_t"], done(g))
                    pe.wait_ge(split2, g + 1)
                    pe.wait_ge(s["gated"], done(g))
                    for j in range(J):
                        js = slice(j * P, (j + 1) * P)
                        for i in range(3):
                            product(pe, ps_y[:, j, :], [q[:, i, js] for q in act2],
                                    [q[:, :] for q in parts["sw3"]] if i == 0 else [q[:, i - 1, :] for q in parts["ew3"]],
                                    i == 0, False)
                        for b3 in parts["b3"]:
                            last = pe.matmul(ps_y[:, j, :], lhsT=gate_t[:, js], rhs=b3[:, :], start=False, stop=b3 is parts["b3"][1])
                    last.then_inc(s["y"], 1)

                def turn(k, slot):
                    g = 2 * k + slot
                    pe.wait_ge(s["rows"], done(g))
                    for c in range(KC):
                        if not isinstance(g, int) or g > 1:
                            pe.wait_ge(kept2, 3 * (g - 2) + c + 1)
                        for j in range(J):
                            last = pe.transpose(bank[3 + c][:, j * P:(j + 1) * P], rows[:, slot, j, c * P:(c + 1) * P], m.ident[:, :])
                        last.then_inc(turned, 1)

                def turn_gates(k, slot):
                    g = 2 * k + slot
                    pe.wait_ge(s["weight"], done(g))
                    pe.wait_ge(kept1, NC1 * g + 4)
                    for j in range(J):
                        last = pe.transpose(bank[0][0:GR, j * P:(j + 1) * P], weight[:, j, :], m.ident[:, :])
                    last.then_inc(s["gate_rows"], 1)

                def second_layer(k, slot):
                    g = 2 * k + slot
                    pe.wait_ge(split_pool, NC1 // 2 * (g + 1))
                    pe.wait_ge(split_dve, NC1 // 2 * (g + 1))
                    pe.wait_ge(xt_kept, KC * g + KC + 1 if not last_group(m, g) else KC * (g + 1))
                    for c in range(KC):
                        last = product(pe, bank[3][:, :], [q[:, c, :] for q in parts["sw2"]], [q[:, c, :] for q in act1], c == 0, c == KC - 1)
                    last.then_inc(made2, 1)
                    pe.wait_ge(s["gate_t"], done(g))
                    for q in range(2):
                        pe.matmul(bank[1 + q][:, :], lhsT=over_features[:, q, :], rhs=gate_t[:, :], start=True,
                                  stop=True).then_inc((s["spread0"], s["spread1"])[q], 1)
                    for q in range(2):
                        if q == 0:
                            pe.wait_ge(xt_kept, KC * (g + 2) if not last_group(m, g) else KC * (g + 1))
                        for i in range(2):
                            e = 2 * q + i
                            last = product(pe, bank[4 if q == 0 else 0][i * EH2:(i + 1) * EH2, :], [w[:, e, :] for w in parts["ew2"]],
                                           [w[:, 2 + e, :] for w in act1], True, True)
                        last.then_inc(made2, 1)

                run(pe, m.groups, SLOTS, [(gate_product, 0), (first_layer_start, 0), (first_layer_end, 0), (turn, 1),
                                (turn_gates, 0), (third_layer, -1), (second_layer, 0)])

            @block.scalar
            def _(act):
                def keep_first(k, slot, chunks):
                    g = 2 * k + slot
                    for i in chunks:
                        act.wait_ge(made1, NC1 * g + i + 1)
                        if not isinstance(g, int) or g > 0:
                            act.wait_ge((split_pool, split_dve)[i % 2], NC1 // 2 * (g - 1) + i // 2 + 1)
                        act.activation(act1_f[:, i, :], bank[i % 3][:, :], ACT.Relu, bias=m.b1[:, i:i + 1], scale=1 / UP).then_inc(kept1, 1)
                    for i in chunks:
                        act.wait_ge(kept1, NC1 * g + i + 1)
                        act.activation(act1[0][:, i, :], act1_f[:, i, :], ACT.Copy).then_inc(high1, 1)

                def keep_first_a(k, slot):
                    keep_first(k, slot, (0, 1))

                def keep_first_b(k, slot):
                    keep_first(k, slot, (2, 3))

                def keep_first_c(k, slot):
                    keep_first(k, slot, (4, 5))

                def exp_logits(k, slot):
                    g = 2 * k + slot
                    act.wait_ge(s["picked"], done(g - 1))
                    act.wait_ge(s["shifted"], done(g))
                    act.activation(exps[:, :, :], shifted[:, :, :], ACT.Exp).then_inc(s["exps"], 1)

                def exp_gates(k, slot):
                    g = 2 * k + slot
                    act.wait_ge(s["over"], done(g))
                    act.activation(exps[:, :, :], over[:, :, :], ACT.Exp).then_inc(s["exps2"], 1)

                def keep_rows(k, slot):
                    g = 2 * k + slot
                    for c in range(KC):
                        act.wait_ge(turned, KC * g + c + 1)
                        act.activation(xt[0][:, slot, c, :], bank[3 + c][:, :], ACT.Copy).then_inc(xt_high, 1)

                def keep_gates(k, slot):
                    g = 2 * k + slot
                    act.wait_ge(s["y"], done(g - 1))
                    act.wait_ge(s["gate_rows"], done(g))
                    act.activation(gate_t[:, :], bank[0][0:GR, :], ACT.Copy).then_inc(s["gate_t"], 1)

                def keep_second(k, slot):
                    g = 2 * k + slot
                    for i in range(3):
                        act.wait_ge(made2, 3 * g + i + 1)
                        if i == 0:
                            if not isinstance(g, int) or g > 0:
                                act.wait_ge(split2, g)
                        else:
                            act.wait_ge((s["gated0"], s["gated1"])[i - 1], done(g - 1))
                        act.activation(act2_f[:, i, :], bank[(3, 4, 0)[i]][:, :], ACT.Relu, bias=m.b2[:, i:i + 1],
                                       scale=1 / UP).then_inc(kept2, 1)
                    act.wait_ge(kept2, 3 * g + 1)
                    act.activation(act2[0][:, 0, :], act2_f[:, 0, :], ACT.Copy).then_inc(high2, 1)

                run(act, m.groups, SLOTS, [(exp_logits, 0), (keep_first_a, 0), (exp_gates, 0), (keep_first_b, 0), (keep_first_c, 0),
                                 (keep_rows, 1), (keep_gates, 0), (keep_second, 0)])


_INS = ["x", "src", "dst", "L0_gnn_Wl1", "L0_gnn_Wr1", "L0_gnn_att1", "L0_gnn_b1", "L0_gnn_Wl2", "L0_gnn_Wr2",
        "L0_gnn_att2", "L0_gnn_b2", "L0_ffn_sW1", "L0_ffn_sb1", "L0_ffn_sW2", "L0_ffn_sb2", "L0_ffn_sW3",
        "L0_ffn_sb3", "L0_ffn_eW1", "L0_ffn_eb1", "L0_ffn_eW2", "L0_ffn_eb2", "L0_ffn_eW3", "L0_ffn_eb3",
        "L0_ffn_gW", "L0_ffn_gb"]


def gat_ffn_program(nc, inputs, out):
    a = inputs
    nodes, edges = a["x"].shape[0], a["src"].shape[0]
    m = Shared(nodes, edges)
    h1 = nc.dram_tensor("hidden", (nodes, F), F32, kind="Internal").ap()
    normed = nc.dram_tensor("normed", (nodes, F), F32, kind="Internal").ap()
    x1 = nc.dram_tensor("attended", (nodes, F), F32, kind="Internal").ap()
    with ExitStack() as ctx:
        setup(nc, m, a, ctx)
        dense_layers(nc, m, a["x"], normed, h1, x1)
        attend_edges(nc, m, 0, normed, None, h1)
        attend_edges(nc, m, 1, h1, a["x"], x1)
        ffn(nc, m, x1, out)


def kernel(**inputs):
    import concourse.bacc as bacc
    import numpy as np
    from concourse.bass_utils import run_bass_kernel_spmd

    nc = bacc.Bacc("TRN2", target_bir_lowering=False, num_devices=1)
    arrays, aps = {}, {}
    for name in _INS:
        v = np.ascontiguousarray(inputs[name])
        arrays[f"in_{name}_dram"] = v
        aps[name] = nc.dram_tensor(f"in_{name}_dram", v.shape, mybir.dt.from_np(v.dtype), kind="ExternalInput").ap()
    out = nc.dram_tensor("out_0_dram", inputs["x"].shape, F32, kind="ExternalOutput").ap()
    gat_ffn_program(nc, aps, out)
    result = run_bass_kernel_spmd(nc, [arrays], core_ids=[0])
    return result.results[0]["out_0_dram"]
```
